# Optimizing a Trainium2 kernel written in Bass

```python
import numpy as np
import jax
import jax.numpy as jnp

def _softmax(x, axis=-1):
    return jax.nn.softmax(x, axis=axis)

def _gelu(x):
    return jax.nn.gelu(x, approximate=True)

def _silu(x):
    return jax.nn.silu(x)

def _sigmoid(x):
    return jax.nn.sigmoid(x)

def _layernorm(x, axis=-1, eps=1e-05):
    m = jnp.mean(x, axis=axis, keepdims=True)
    v = jnp.var(x, axis=axis, keepdims=True)
    return (x - m) / jnp.sqrt(v + eps)

def _scatter_add(tgt, idx, src, axis=0):
    return tgt.at[idx].add(src)

def _segment_sum(src, seg, n):
    return jax.ops.segment_sum(src, seg, n)
kernel_name = 'mk_flamingo_gated_d4_seqx_r8_47ca67'

def setup_inputs(seed: int=0):
    np.random.seed(seed)
    _w = jnp.asarray

    def _rec_inputs():
        import jax
        import jax.numpy as jnp
        _rk = jax.random.key(seed)
        x = 7.22e-05 + 1 * jax.random.normal(jax.random.fold_in(_rk, 1), (64, 64, 256), jnp.float32)
        _lenS = 64 - jax.random.randint(jax.random.fold_in(_rk, 7), (64,), 0, max(1, 64 // 4) + 1, jnp.int32)
        _lenS2 = 64 - jax.random.randint(jax.random.fold_in(_rk, 8), (64,), 0, max(1, 64 // 4) + 1, jnp.int32)
        _ctx_2048P = jax.random.normal(jax.random.fold_in(_rk, 11), (64, 16, 256), jnp.float32)
        _ctx_2048c = jax.random.dirichlet(jax.random.fold_in(_rk, 511), 0.3 * jnp.ones((16,), jnp.float32), (64, 64))
        _ctx_2048t = jnp.einsum('bsk,bkd->bsd', _ctx_2048c, _ctx_2048P)
        _ctx_2048t = _ctx_2048t * jax.lax.rsqrt(jnp.mean(jnp.square(_ctx_2048t)) + 1e-12) * 0.953939
        ctx_2048 = 4.13588e-05 + 0.999923 * (_ctx_2048t + 0.3 * jax.random.normal(jax.random.fold_in(_rk, 611), (64, 64, 256), jnp.float32))
        _g = jax.random.normal(jax.random.fold_in(_rk, 9001), (2, 4), jnp.float32)
        _g = jnp.sign(_g) * jnp.maximum(jnp.abs(_g), 1.0) + (_g == 0) * 1.0
        g_xattn = _g[0]
        g_ffn = _g[1]
        return (x, ctx_2048, _lenS2, g_xattn, g_ffn)
    x, ctx_2048, _lenS2, g_xattn, g_ffn = _rec_inputs()

    def _L0_xattn_setup():
        import jax, jax.numpy as jnp
        import numpy as np
        N_HEAD = 8
        key = jax.random.key(seed)
        k1, k2, k3 = jax.random.split(key, 3)
        b, d, m = (4, 128, 256)
        c, n = (128, 256)
        q = jax.random.normal(k1, (b, d, m), dtype=jnp.float32)
        k = jax.random.normal(k2, (d // d * b, d, n), dtype=jnp.float32).reshape(b, d, n)
        v = jax.random.normal(k3, (b, c, n), dtype=jnp.float32)
        return {'q': q, 'k': k, 'v': v}
    _L0_xattn_all = _L0_xattn_setup()
    _L0_xattn_in = {k: v for k, v in _L0_xattn_all.items() if k in ()}
    del _L0_xattn_all

    def _L0_ffn_setup():
        import jax, jax.numpy as jnp
        import numpy as np
        ALPHA = 1.702
        LIMIT = 7.0
        TOP_K = 4
        B, S, H = (1, 128, 256)
        E, D = (16, 256)
        key = jax.random.key(seed)
        ks = jax.random.split(key, 7)
        s = 0.02
        return {'hidden_states': jax.random.normal(ks[0], (B, S, H), dtype=jnp.float32), 'router_weight': jax.random.normal(ks[1], (E, H), dtype=jnp.float32) * s, 'router_bias': jax.random.normal(ks[2], (E,), dtype=jnp.float32) * s, 'gate_up_proj': jax.random.normal(ks[3], (E, H, 2 * D), dtype=jnp.float32) * s, 'gate_up_proj_bias': jax.random.normal(ks[4], (E, 2 * D), dtype=jnp.float32) * s, 'down_proj': jax.random.normal(ks[5], (E, D, H), dtype=jnp.float32) * s, 'down_proj_bias': jax.random.normal(ks[6], (E, H), dtype=jnp.float32) * s}
    _L0_ffn_all = _L0_ffn_setup()
    _L0_ffn_in = {k: v for k, v in _L0_ffn_all.items() if k in ('router_weight', 'router_bias', 'gate_up_proj', 'gate_up_proj_bias', 'down_proj', 'down_proj_bias')}
    del _L0_ffn_all

    def _L1_xattn_setup():
        import jax, jax.numpy as jnp
        import numpy as np
        N_HEAD = 8
        ALPHA = 5.0
        EPS = 1e-12

        def _l2norm(x, axis):
            n = jnp.sqrt(jnp.sum(x * x, axis=axis, keepdims=True))
            return x / jnp.maximum(n, EPS)
        key = jax.random.key(seed)
        kq, kk, kv = jax.random.split(key, 3)
        B, D, T = (4, 128, 256)
        q = jax.random.normal(kq, (B, D, T), dtype=jnp.float32)
        k = jax.random.normal(kk, (B, D, T), dtype=jnp.float32)
        v = jax.random.normal(kv, (B, D, T), dtype=jnp.float32)
        return {'q': q, 'k': k, 'v': v}
    _L1_xattn_all = _L1_xattn_setup()
    _L1_xattn_in = {k: v for k, v in _L1_xattn_all.items() if k in ()}
    del _L1_xattn_all

    def _L1_ffn_setup():
        import jax, jax.numpy as jnp
        import numpy as np
        EPS = 1e-05

        def rmsnorm(x, weight, eps=EPS):
            var = jnp.mean(x * x, axis=-1, keepdims=True)
            return x * jax.lax.rsqrt(var + eps) * weight

        def activation_quant(x):
            scale = 127.0 / jnp.clip(jnp.max(jnp.abs(x), axis=-1, keepdims=True), 1e-05, None)
            return jnp.clip(jnp.round(x * scale), -128, 127) / scale

        def weight_quant(w):
            scale = 1.0 / jnp.clip(jnp.mean(jnp.abs(w)), 1e-05, None)
            return jnp.clip(jnp.round(w * scale), -1, 1) / scale

        def bitlinear(x, w):
            xq = activation_quant(x)
            wq = weight_quant(w)
            return jnp.einsum('bsh,oh->bso', xq, wq)
        key = jax.random.key(seed)
        k1, k2, k3 = jax.random.split(key, 3)
        B, S, H, F = (4, 256, 256, 704)
        x = jax.random.normal(k1, (B, S, H), dtype=jnp.float32)
        w_gate_up = jax.random.normal(k2, (2 * F, H), dtype=jnp.float32) * 0.02
        w_down = jax.random.normal(k3, (H, F), dtype=jnp.float32) * 0.02
        norm_weight = jnp.ones((H,), dtype=jnp.float32)
        return {'x': x, 'w_gate_up': w_gate_up, 'w_down': w_down, 'norm_weight': norm_weight}
    _L1_ffn_all = _L1_ffn_setup()
    _L1_ffn_in = {k: v for k, v in _L1_ffn_all.items() if k in ('w_gate_up', 'w_down', 'norm_weight')}
    del _L1_ffn_all

    def _L2_xattn_setup():
        import jax, jax.numpy as jnp
        import numpy as np
        DIM = 256
        N_HEADS = 16
        HEAD_DIM = DIM // N_HEADS
        EPS = 1e-06
        IMG_LEN = 257

        def rms_norm(x, g, eps=EPS):
            var = jnp.mean(x * x, axis=-1, keepdims=True)
            return x * jax.lax.rsqrt(var + eps) * g

        def _attend(q, k, v, k_mask=None):
            scale = 1.0 / jnp.sqrt(jnp.asarray(HEAD_DIM, q.dtype))
            scores = jnp.einsum('bqnd,bknd->bnqk', q, k) * scale
            if k_mask is not None:
                neg = jnp.asarray(jnp.finfo(scores.dtype).min, scores.dtype)
                scores = jnp.where(k_mask[:, None, None, :], scores, neg)
            probs = jax.nn.softmax(scores, axis=-1)
            return jnp.einsum('bnqk,bknd->bqnd', probs, v)
        key = jax.random.key(seed)
        ks = jax.random.split(key, 16)
        B, L1, L2 = (1, 2048, 769)
        std = 0.02
        inp = {'x': jax.random.normal(ks[0], (B, L1, DIM), jnp.float32), 'context': jax.random.normal(ks[1], (B, L2, DIM), jnp.float32), 'context_lens': jax.random.randint(ks[2], (B,), 32, 513, jnp.int32), 'Wq': jax.random.normal(ks[3], (DIM, DIM), jnp.float32) * std, 'bq': jnp.zeros((DIM,), jnp.float32), 'gq': jnp.ones((DIM,), jnp.float32), 'Wk': jax.random.normal(ks[4], (DIM, DIM), jnp.float32) * std, 'bk': jnp.zeros((DIM,), jnp.float32), 'gk': jnp.ones((DIM,), jnp.float32), 'Wv': jax.random.normal(ks[5], (DIM, DIM), jnp.float32) * std, 'bv': jnp.zeros((DIM,), jnp.float32), 'Wk_img': jax.random.normal(ks[6], (DIM, DIM), jnp.float32) * std, 'bk_img': jnp.zeros((DIM,), jnp.float32), 'gk_img': jnp.ones((DIM,), jnp.float32), 'Wv_img': jax.random.normal(ks[7], (DIM, DIM), jnp.float32) * std, 'bv_img': jnp.zeros((DIM,), jnp.float32), 'Wo': jax.random.normal(ks[8], (DIM, DIM), jnp.float32) * std, 'bo': jnp.zeros((DIM,), jnp.float32)}
        return inp
    _L2_xattn_all = _L2_xattn_setup()
    _L2_xattn_in = {k: v for k, v in _L2_xattn_all.items() if k in ('context_lens', 'Wq', 'bq', 'gq', 'Wk', 'bk', 'gk', 'Wv', 'bv', 'Wk_img', 'bk_img', 'gk_img', 'Wv_img', 'bv_img', 'Wo', 'bo')}
    del _L2_xattn_all

    def _L2_ffn_setup():
        import jax, jax.numpy as jnp
        import numpy as np
        H = 256
        I = 128
        K = 8
        E = 128
        TOPK = 4
        EPS = 1e-08
        key = jax.random.key(seed)
        ks = jax.random.split(key, 10)
        s = 0.02
        return {'x': jax.random.normal(ks[0], (4, 256, H), jnp.float32), 'w_router': jax.random.normal(ks[1], (H, E), jnp.float32) * s, 'w_gate': jax.random.normal(ks[2], (H, K * I), jnp.float32) * s, 'w_up': jax.random.normal(ks[3], (H, K * I), jnp.float32) * s, 'w_down': jax.random.normal(ks[4], (I, H), jnp.float32) * s, 'amplitudes': jax.random.normal(ks[5], (E, K, 2), jnp.float32) * 0.1, 'expert_scale': jnp.ones((E,), jnp.float32), 'shared_w_gate': jax.random.normal(ks[6], (H, 2 * I), jnp.float32) * s, 'shared_w_up': jax.random.normal(ks[7], (H, 2 * I), jnp.float32) * s, 'shared_w_down': jax.random.normal(ks[8], (2 * I, H), jnp.float32) * s}
    _L2_ffn_all = _L2_ffn_setup()
    _L2_ffn_in = {k: v for k, v in _L2_ffn_all.items() if k in ('w_router', 'w_gate', 'w_up', 'w_down', 'amplitudes', 'expert_scale', 'shared_w_gate', 'shared_w_up', 'shared_w_down')}
    del _L2_ffn_all

    def _L3_xattn_setup():
        import jax, jax.numpy as jnp
        import numpy as np
        DIM = 256
        HEADS = 16
        HEAD_DIM = DIM // HEADS
        EPS = 1e-06
        IMG_TOKENS = 257
        B, L1, L2 = (2, 512, 769)
        SCALE = 1.0 / np.sqrt(HEAD_DIM).astype(np.float32)

        def rms_norm(x, g):
            return x * jax.lax.rsqrt(jnp.mean(x * x, axis=-1, keepdims=True) + EPS) * g

        def attention(q, k, v, kv_mask=None):
            s = jnp.einsum('bqhd,bkhd->bhqk', q, k) * SCALE
            if kv_mask is not None:
                s = jnp.where(kv_mask[:, None, None, :], s, jnp.float32(-1000000000.0))
            p = jax.nn.softmax(s, axis=-1)
            return jnp.einsum('bhqk,bkhd->bqhd', p, v)
        key = jax.random.key(seed)
        ks = jax.random.split(key, 20)
        std = 0.02

        def lin(i):
            return (jax.random.normal(ks[i], (DIM, DIM), jnp.float32) * std, jnp.zeros((DIM,), jnp.float32))
        w_q, b_q = lin(0)
        w_k, b_k = lin(1)
        w_v, b_v = lin(2)
        w_k_img, b_k_img = lin(3)
        w_v_img, b_v_img = lin(4)
        w_o, b_o = lin(5)
        return {'x': jax.random.normal(ks[6], (B, L1, DIM), jnp.float32), 'context': jax.random.normal(ks[7], (B, L2, DIM), jnp.float32), 'context_lens': jax.random.randint(ks[8], (B,), 32, 513, jnp.int64 if jax.config.jax_enable_x64 else jnp.int32), 'w_q': w_q, 'b_q': b_q, 'w_k': w_k, 'b_k': b_k, 'w_v': w_v, 'b_v': b_v, 'w_k_img': w_k_img, 'b_k_img': b_k_img, 'w_v_img': w_v_img, 'b_v_img': b_v_img, 'w_o': w_o, 'b_o': b_o, 'g_q': jnp.ones((DIM,), jnp.float32), 'g_k': jnp.ones((DIM,), jnp.float32), 'g_k_img': jnp.ones((DIM,), jnp.float32)}
    _L3_xattn_all = _L3_xattn_setup()
    _L3_xattn_in = {k: v for k, v in _L3_xattn_all.items() if k in ('w_q', 'b_q', 'w_k', 'b_k', 'w_v', 'b_v', 'w_k_img', 'b_k_img', 'w_v_img', 'b_v_img', 'w_o', 'b_o', 'g_q', 'g_k', 'g_k_img')}
    del _L3_xattn_all

    def _L3_ffn_setup():
        import jax, jax.numpy as jnp
        import numpy as np
        import math
        D_MODEL = 256
        D_FF = 1024
        NUM_EXPERTS = 8
        TOP_K = 2
        CAPACITY_FACTOR = 1.25
        BATCH, SEQ = (4, 256)

        def _moe_forward(x, Wg, w1, w2):
            B, T, d = x.shape
            S = B * T
            E, K = (NUM_EXPERTS, TOP_K)
            C = math.ceil(CAPACITY_FACTOR * S * K / E)
            xr = x.reshape(S, d)
            probs = jax.nn.softmax(xr @ Wg, axis=-1)
            gate_vals, expert_idx = jax.lax.top_k(probs, K)
            flat_e = expert_idx.reshape(-1)
            oh = jax.nn.one_hot(flat_e, E, dtype=jnp.int32)
            pos = jnp.sum((jnp.cumsum(oh, axis=0) - 1) * oh, axis=1)
            kept = pos < C
            i = jnp.arange(S * K)
            slot = i % K * S + i // K
            sentinel = S * K
            pos_w = jnp.where(kept, pos, C)
            dispatch_mask = jnp.full((E, C), sentinel, dtype=jnp.int32)
            dispatch_mask = dispatch_mask.at[flat_e, pos_w].set(slot.astype(jnp.int32), mode='drop')
            combine_weights = (gate_vals * kept.reshape(S, K)).T
            dispatched = xr[dispatch_mask.reshape(-1) % S].reshape(E, C, d)
            h = jax.nn.relu(jnp.einsum('ecd,edf->ecf', dispatched, w1))
            expert_out = jnp.einsum('ecf,efd->ecd', h, w2)
            rerouted = jnp.zeros((S * K + 1, d), dtype=expert_out.dtype)
            rerouted = rerouted.at[dispatch_mask.reshape(-1)].set(expert_out.reshape(-1, d))
            rerouted = rerouted[:-1].reshape(K, S, d)
            out = jnp.einsum('ks,ksm->sm', combine_weights, rerouted)
            return out.reshape(B, T, d)
        key = jax.random.key(seed)
        k1, k2, k3, k4 = jax.random.split(key, 4)
        x = jax.random.normal(k1, (BATCH, SEQ, D_MODEL), dtype=jnp.float32)
        Wg = jax.random.normal(k2, (D_MODEL, NUM_EXPERTS), dtype=jnp.float32) * 0.02
        w1 = jax.random.normal(k3, (NUM_EXPERTS, D_MODEL, D_FF), dtype=jnp.float32) * 0.02
        w2 = jax.random.normal(k4, (NUM_EXPERTS, D_FF, D_MODEL), dtype=jnp.float32) * 0.02
        return {'x': x, 'Wg': Wg, 'w1': w1, 'w2': w2}
    _L3_ffn_all = _L3_ffn_setup()
    _L3_ffn_in = {k: v for k, v in _L3_ffn_all.items() if k in ('Wg', 'w1', 'w2')}
    del _L3_ffn_all
    return {'x': x, 'ctx_2048': ctx_2048, '_lenS2': _lenS2, 'g_xattn': g_xattn, 'g_ffn': g_ffn, 'L0_ffn_router_weight': _L0_ffn_in['router_weight'], 'L0_ffn_router_bias': _L0_ffn_in['router_bias'], 'L0_ffn_gate_up_proj': _L0_ffn_in['gate_up_proj'], 'L0_ffn_gate_up_proj_bias': _L0_ffn_in['gate_up_proj_bias'], 'L0_ffn_down_proj': _L0_ffn_in['down_proj'], 'L0_ffn_down_proj_bias': _L0_ffn_in['down_proj_bias'], 'L1_ffn_w_gate_up': _L1_ffn_in['w_gate_up'], 'L1_ffn_w_down': _L1_ffn_in['w_down'], 'L1_ffn_norm_weight': _L1_ffn_in['norm_weight'], 'L2_xattn_context_lens': _L2_xattn_in['context_lens'], 'L2_xattn_Wq': _L2_xattn_in['Wq'], 'L2_xattn_bq': _L2_xattn_in['bq'], 'L2_xattn_gq': _L2_xattn_in['gq'], 'L2_xattn_Wk': _L2_xattn_in['Wk'], 'L2_xattn_bk': _L2_xattn_in['bk'], 'L2_xattn_gk': _L2_xattn_in['gk'], 'L2_xattn_Wv': _L2_xattn_in['Wv'], 'L2_xattn_bv': _L2_xattn_in['bv'], 'L2_xattn_Wk_img': _L2_xattn_in['Wk_img'], 'L2_xattn_bk_img': _L2_xattn_in['bk_img'], 'L2_xattn_gk_img': _L2_xattn_in['gk_img'], 'L2_xattn_Wv_img': _L2_xattn_in['Wv_img'], 'L2_xattn_bv_img': _L2_xattn_in['bv_img'], 'L2_xattn_Wo': _L2_xattn_in['Wo'], 'L2_xattn_bo': _L2_xattn_in['bo'], 'L2_ffn_w_router': _L2_ffn_in['w_router'], 'L2_ffn_w_gate': _L2_ffn_in['w_gate'], 'L2_ffn_w_up': _L2_ffn_in['w_up'], 'L2_ffn_w_down': _L2_ffn_in['w_down'], 'L2_ffn_amplitudes': _L2_ffn_in['amplitudes'], 'L2_ffn_expert_scale': _L2_ffn_in['expert_scale'], 'L2_ffn_shared_w_gate': _L2_ffn_in['shared_w_gate'], 'L2_ffn_shared_w_up': _L2_ffn_in['shared_w_up'], 'L2_ffn_shared_w_down': _L2_ffn_in['shared_w_down'], 'L3_xattn_w_q': _L3_xattn_in['w_q'], 'L3_xattn_b_q': _L3_xattn_in['b_q'], 'L3_xattn_w_k': _L3_xattn_in['w_k'], 'L3_xattn_b_k': _L3_xattn_in['b_k'], 'L3_xattn_w_v': _L3_xattn_in['w_v'], 'L3_xattn_b_v': _L3_xattn_in['b_v'], 'L3_xattn_w_k_img': _L3_xattn_in['w_k_img'], 'L3_xattn_b_k_img': _L3_xattn_in['b_k_img'], 'L3_xattn_w_v_img': _L3_xattn_in['w_v_img'], 'L3_xattn_b_v_img': _L3_xattn_in['b_v_img'], 'L3_xattn_w_o': _L3_xattn_in['w_o'], 'L3_xattn_b_o': _L3_xattn_in['b_o'], 'L3_xattn_g_q': _L3_xattn_in['g_q'], 'L3_xattn_g_k': _L3_xattn_in['g_k'], 'L3_xattn_g_k_img': _L3_xattn_in['g_k_img'], 'L3_ffn_Wg': _L3_ffn_in['Wg'], 'L3_ffn_w1': _L3_ffn_in['w1'], 'L3_ffn_w2': _L3_ffn_in['w2']}

def reference(x, ctx_2048, _lenS2, g_xattn, g_ffn, L0_ffn_router_weight, L0_ffn_router_bias, L0_ffn_gate_up_proj, L0_ffn_gate_up_proj_bias, L0_ffn_down_proj, L0_ffn_down_proj_bias, L1_ffn_w_gate_up, L1_ffn_w_down, L1_ffn_norm_weight, L2_xattn_context_lens, L2_xattn_Wq, L2_xattn_bq, L2_xattn_gq, L2_xattn_Wk, L2_xattn_bk, L2_xattn_gk, L2_xattn_Wv, L2_xattn_bv, L2_xattn_Wk_img, L2_xattn_bk_img, L2_xattn_gk_img, L2_xattn_Wv_img, L2_xattn_bv_img, L2_xattn_Wo, L2_xattn_bo, L2_ffn_w_router, L2_ffn_w_gate, L2_ffn_w_up, L2_ffn_w_down, L2_ffn_amplitudes, L2_ffn_expert_scale, L2_ffn_shared_w_gate, L2_ffn_shared_w_up, L2_ffn_shared_w_down, L3_xattn_w_q, L3_xattn_b_q, L3_xattn_w_k, L3_xattn_b_k, L3_xattn_w_v, L3_xattn_b_v, L3_xattn_w_k_img, L3_xattn_b_k_img, L3_xattn_w_v_img, L3_xattn_b_v_img, L3_xattn_w_o, L3_xattn_b_o, L3_xattn_g_q, L3_xattn_g_k, L3_xattn_g_k_img, L3_ffn_Wg, L3_ffn_w1, L3_ffn_w2):
    import jax
    import jax.numpy as jnp

    def _L0_xattn_ref(q, k, v):
        import jax, jax.numpy as jnp
        import numpy as np
        N_HEAD = 8
        b, d, m = q.shape
        c = v.shape[1]
        h = N_HEAD
        qh = q.reshape(b * h, d // h, m)
        kh = k.reshape(b * h, d // h, -1)
        vh = v.reshape(b * h, c // h, -1)
        scale = 1.0 / jnp.sqrt(jnp.asarray(d // h, dtype=q.dtype))
        qk = jnp.einsum('bdm,bdn->bmn', qh, kh) * scale
        sm = jax.nn.softmax(qk, axis=-1)
        ret = jnp.einsum('bmn,bcn->bcm', sm, vh)
        return ret.reshape(b, c, m)

    def _L0_ffn_ref(hidden_states, router_weight, router_bias, gate_up_proj, gate_up_proj_bias, down_proj, down_proj_bias):
        import jax, jax.numpy as jnp
        import numpy as np
        ALPHA = 1.702
        LIMIT = 7.0
        TOP_K = 4
        B, S, H = (1, 128, 256)
        E, D = (16, 256)
        batch, seq, hdim = hidden_states.shape
        x = hidden_states.reshape(-1, hdim)
        T = x.shape[0]
        logits = x @ router_weight.T + router_bias
        top_val, top_idx = jax.lax.top_k(logits, TOP_K)
        top_val = jax.nn.softmax(top_val, axis=-1)
        router_scores = jnp.zeros_like(logits).at[jnp.arange(T)[:, None], top_idx].set(top_val)
        gate_up = jnp.einsum('th,ehd->etd', x, gate_up_proj) + gate_up_proj_bias[:, None, :]
        gate = gate_up[..., ::2]
        up = gate_up[..., 1::2]
        gate = jnp.minimum(gate, LIMIT)
        up = jnp.clip(up, -LIMIT, LIMIT)
        glu = gate * jax.nn.sigmoid(gate * ALPHA)
        out = jnp.einsum('etd,edh->eth', (up + 1.0) * glu, down_proj) + down_proj_bias[:, None, :]
        out = out * router_scores.T[:, :, None]
        out = out.sum(axis=0)
        return out.reshape(batch, seq, hdim)

    def _L1_xattn_ref(q, k, v):
        import jax, jax.numpy as jnp
        import numpy as np
        N_HEAD = 8
        ALPHA = 5.0
        EPS = 1e-12

        def _l2norm(x, axis):
            n = jnp.sqrt(jnp.sum(x * x, axis=axis, keepdims=True))
            return x / jnp.maximum(n, EPS)
        B, D, Tq = q.shape
        Tk = k.shape[-1]
        Dv = v.shape[-2]
        h = N_HEAD
        d = D // h
        dv = Dv // h
        qh = q.reshape(B, h, d, Tq)
        kh = k.reshape(B, h, d, Tk)
        vh = v.reshape(B, h, dv, Tk)
        qn = _l2norm(qh, axis=-2)
        kn = _l2norm(kh, axis=-2)
        qk = ALPHA * jnp.einsum('bhdq,bhdk->bhqk', qn, kn)
        sm = jax.nn.softmax(qk, axis=-1)
        out = jnp.einsum('bhqk,bhdk->bhdq', sm, vh)
        return out.reshape(B, Dv, Tq)

    def _L1_ffn_ref(x, w_gate_up, w_down, norm_weight):
        import jax, jax.numpy as jnp
        import numpy as np
        EPS = 1e-05

        def rmsnorm(x, weight, eps=EPS):
            var = jnp.mean(x * x, axis=-1, keepdims=True)
            return x * jax.lax.rsqrt(var + eps) * weight

        def activation_quant(x):
            scale = 127.0 / jnp.clip(jnp.max(jnp.abs(x), axis=-1, keepdims=True), 1e-05, None)
            return jnp.clip(jnp.round(x * scale), -128, 127) / scale

        def weight_quant(w):
            scale = 1.0 / jnp.clip(jnp.mean(jnp.abs(w)), 1e-05, None)
            return jnp.clip(jnp.round(w * scale), -1, 1) / scale

        def bitlinear(x, w):
            xq = activation_quant(x)
            wq = weight_quant(w)
            return jnp.einsum('bsh,oh->bso', xq, wq)
        x_norm = rmsnorm(x, norm_weight)
        gate_up = bitlinear(x_norm, w_gate_up)
        gate, up = jnp.split(gate_up, 2, axis=-1)
        hidden = jnp.square(jax.nn.relu(gate)) * up
        return bitlinear(hidden, w_down)

    def _L2_xattn_ref(x, context, context_lens, Wq, bq, gq, Wk, bk, gk, Wv, bv, Wk_img, bk_img, gk_img, Wv_img, bv_img, Wo, bo):
        import jax, jax.numpy as jnp
        import numpy as np
        DIM = 256
        N_HEADS = 16
        HEAD_DIM = DIM // N_HEADS
        EPS = 1e-06
        IMG_LEN = 257

        def rms_norm(x, g, eps=EPS):
            var = jnp.mean(x * x, axis=-1, keepdims=True)
            return x * jax.lax.rsqrt(var + eps) * g

        def _attend(q, k, v, k_mask=None):
            scale = 1.0 / jnp.sqrt(jnp.asarray(HEAD_DIM, q.dtype))
            scores = jnp.einsum('bqnd,bknd->bnqk', q, k) * scale
            if k_mask is not None:
                neg = jnp.asarray(jnp.finfo(scores.dtype).min, scores.dtype)
                scores = jnp.where(k_mask[:, None, None, :], scores, neg)
            probs = jax.nn.softmax(scores, axis=-1)
            return jnp.einsum('bnqk,bknd->bqnd', probs, v)
        b = x.shape[0]
        n, d = (N_HEADS, HEAD_DIM)
        ctx_img = context[:, :IMG_LEN]
        ctx_txt = context[:, IMG_LEN:]
        q = rms_norm(x @ Wq + bq, gq).reshape(b, -1, n, d)
        k = rms_norm(ctx_txt @ Wk + bk, gk).reshape(b, -1, n, d)
        v = (ctx_txt @ Wv + bv).reshape(b, -1, n, d)
        k_img = rms_norm(ctx_img @ Wk_img + bk_img, gk_img).reshape(b, -1, n, d)
        v_img = (ctx_img @ Wv_img + bv_img).reshape(b, -1, n, d)
        img_x = _attend(q, k_img, v_img)
        k_mask = jnp.arange(k.shape[1])[None, :] < context_lens[:, None]
        txt_x = _attend(q, k, v, k_mask)
        out = (txt_x + img_x).reshape(b, -1, n * d)
        return out @ Wo + bo

    def _L2_ffn_ref(x, w_router, w_gate, w_up, w_down, amplitudes, expert_scale, shared_w_gate, shared_w_up, shared_w_down):
        import jax, jax.numpy as jnp
        import numpy as np
        H = 256
        I = 128
        K = 8
        E = 128
        TOPK = 4
        EPS = 1e-08
        B, S, _ = x.shape
        T = B * S
        xt = x.reshape(T, H)
        probs = jax.nn.softmax(xt @ w_router, axis=-1)
        topk_p, topk_idx = jax.lax.top_k(probs, TOPK)
        topk_w = topk_p / (jnp.sum(topk_p, axis=-1, keepdims=True) + EPS)
        gate = (xt @ w_gate).reshape(T, K, I)
        up = (xt @ w_up).reshape(T, K, I)
        basis = jax.nn.silu(gate) * up
        p = amplitudes[..., 0] ** 2 + amplitudes[..., 1] ** 2
        mix = p / (jnp.sum(p, axis=-1, keepdims=True) + EPS)
        mix_sel = mix[topk_idx]
        mixed = jnp.einsum('tek,tki->tei', mix_sel, basis)
        down = jnp.einsum('tei,ih->teh', mixed, w_down)
        coeff = topk_w * expert_scale[topk_idx]
        out = jnp.einsum('teh,te->th', down, coeff)
        shared = jax.nn.silu(xt @ shared_w_gate) * (xt @ shared_w_up) @ shared_w_down
        out = out + shared
        return out.reshape(B, S, H)

    def _L3_xattn_ref(x, context, context_lens, w_q, b_q, w_k, b_k, w_v, b_v, w_k_img, b_k_img, w_v_img, b_v_img, w_o, b_o, g_q, g_k, g_k_img):
        import jax, jax.numpy as jnp
        import numpy as np
        DIM = 256
        HEADS = 16
        HEAD_DIM = DIM // HEADS
        EPS = 1e-06
        IMG_TOKENS = 257
        B, L1, L2 = (2, 512, 769)
        SCALE = 1.0 / np.sqrt(HEAD_DIM).astype(np.float32)

        def rms_norm(x, g):
            return x * jax.lax.rsqrt(jnp.mean(x * x, axis=-1, keepdims=True) + EPS) * g

        def attention(q, k, v, kv_mask=None):
            s = jnp.einsum('bqhd,bkhd->bhqk', q, k) * SCALE
            if kv_mask is not None:
                s = jnp.where(kv_mask[:, None, None, :], s, jnp.float32(-1000000000.0))
            p = jax.nn.softmax(s, axis=-1)
            return jnp.einsum('bhqk,bkhd->bqhd', p, v)
        b = x.shape[0]
        ctx_img = context[:, :IMG_TOKENS]
        ctx_txt = context[:, IMG_TOKENS:]
        q = rms_norm(x @ w_q.T + b_q, g_q).reshape(b, -1, HEADS, HEAD_DIM)
        k = rms_norm(ctx_txt @ w_k.T + b_k, g_k).reshape(b, -1, HEADS, HEAD_DIM)
        v = (ctx_txt @ w_v.T + b_v).reshape(b, -1, HEADS, HEAD_DIM)
        k_img = rms_norm(ctx_img @ w_k_img.T + b_k_img, g_k_img).reshape(b, -1, HEADS, HEAD_DIM)
        v_img = (ctx_img @ w_v_img.T + b_v_img).reshape(b, -1, HEADS, HEAD_DIM)
        txt_len = ctx_txt.shape[1]
        kv_mask = jnp.arange(txt_len)[None, :] < context_lens[:, None]
        img_x = attention(q, k_img, v_img)
        txt_x = attention(q, k, v, kv_mask)
        out = (txt_x + img_x).reshape(b, -1, DIM)
        return out @ w_o.T + b_o

    def _L3_ffn_ref(x, Wg, w1, w2):
        import jax, jax.numpy as jnp
        import numpy as np
        import math
        D_MODEL = 256
        D_FF = 1024
        NUM_EXPERTS = 8
        TOP_K = 2
        CAPACITY_FACTOR = 1.25
        BATCH, SEQ = (4, 256)

        def _moe_forward(x, Wg, w1, w2):
            B, T, d = x.shape
            S = B * T
            E, K = (NUM_EXPERTS, TOP_K)
            C = math.ceil(CAPACITY_FACTOR * S * K / E)
            xr = x.reshape(S, d)
            probs = jax.nn.softmax(xr @ Wg, axis=-1)
            gate_vals, expert_idx = jax.lax.top_k(probs, K)
            flat_e = expert_idx.reshape(-1)
            oh = jax.nn.one_hot(flat_e, E, dtype=jnp.int32)
            pos = jnp.sum((jnp.cumsum(oh, axis=0) - 1) * oh, axis=1)
            kept = pos < C
            i = jnp.arange(S * K)
            slot = i % K * S + i // K
            sentinel = S * K
            pos_w = jnp.where(kept, pos, C)
            dispatch_mask = jnp.full((E, C), sentinel, dtype=jnp.int32)
            dispatch_mask = dispatch_mask.at[flat_e, pos_w].set(slot.astype(jnp.int32), mode='drop')
            combine_weights = (gate_vals * kept.reshape(S, K)).T
            dispatched = xr[dispatch_mask.reshape(-1) % S].reshape(E, C, d)
            h = jax.nn.relu(jnp.einsum('ecd,edf->ecf', dispatched, w1))
            expert_out = jnp.einsum('ecf,efd->ecd', h, w2)
            rerouted = jnp.zeros((S * K + 1, d), dtype=expert_out.dtype)
            rerouted = rerouted.at[dispatch_mask.reshape(-1)].set(expert_out.reshape(-1, d))
            rerouted = rerouted[:-1].reshape(K, S, d)
            out = jnp.einsum('ks,ksm->sm', combine_weights, rerouted)
            return out.reshape(B, T, d)
        return _moe_forward(x, Wg, w1, w2)
    x = x + jnp.tanh(g_xattn[0]) * _L0_xattn_ref(_layernorm(x, axis=-1), ctx_2048, ctx_2048)
    x = x + jnp.tanh(g_ffn[0]) * _L0_ffn_ref(_layernorm(x, axis=-1), L0_ffn_router_weight, L0_ffn_router_bias, L0_ffn_gate_up_proj, L0_ffn_gate_up_proj_bias, L0_ffn_down_proj, L0_ffn_down_proj_bias)
    x = x + jnp.tanh(g_xattn[1]) * _L1_xattn_ref(_layernorm(x, axis=-1), ctx_2048, ctx_2048)
    x = x + jnp.tanh(g_ffn[1]) * _L1_ffn_ref(_layernorm(x, axis=-1), L1_ffn_w_gate_up, L1_ffn_w_down, L1_ffn_norm_weight)
    x = x + jnp.tanh(g_xattn[2]) * _L2_xattn_ref(_layernorm(x, axis=-1), ctx_2048, L2_xattn_context_lens, L2_xattn_Wq, L2_xattn_bq, L2_xattn_gq, L2_xattn_Wk, L2_xattn_bk, L2_xattn_gk, L2_xattn_Wv, L2_xattn_bv, L2_xattn_Wk_img, L2_xattn_bk_img, L2_xattn_gk_img, L2_xattn_Wv_img, L2_xattn_bv_img, L2_xattn_Wo, L2_xattn_bo)
    x = x + jnp.tanh(g_ffn[2]) * _L2_ffn_ref(_layernorm(x, axis=-1), L2_ffn_w_router, L2_ffn_w_gate, L2_ffn_w_up, L2_ffn_w_down, L2_ffn_amplitudes, L2_ffn_expert_scale, L2_ffn_shared_w_gate, L2_ffn_shared_w_up, L2_ffn_shared_w_down)
    x = x + jnp.tanh(g_xattn[3]) * _L3_xattn_ref(_layernorm(x, axis=-1), ctx_2048, _lenS2, L3_xattn_w_q, L3_xattn_b_q, L3_xattn_w_k, L3_xattn_b_k, L3_xattn_w_v, L3_xattn_b_v, L3_xattn_w_k_img, L3_xattn_b_k_img, L3_xattn_w_v_img, L3_xattn_b_v_img, L3_xattn_w_o, L3_xattn_b_o, L3_xattn_g_q, L3_xattn_g_k, L3_xattn_g_k_img)
    x = x + jnp.tanh(g_ffn[3]) * _L3_ffn_ref(_layernorm(x, axis=-1), L3_ffn_Wg, L3_ffn_w1, L3_ffn_w2)
    return x

_drawn_inputs = setup_inputs


def setup_inputs(seed=0):
    import zlib

    import numpy as np

    out = dict(_drawn_inputs(seed))
    spreads = {'L1_ffn_norm_weight': (1.0, 0.6),
     'L2_xattn_bq': (0.0, 2.0),
     'L2_xattn_gq': (1.0, 0.6),
     'L2_xattn_bk': (0.0, 0.1),
     'L2_xattn_gk': (1.0, 0.2),
     'L2_xattn_bv': (0.0, 0.1),
     'L2_xattn_bk_img': (0.0, 2.0),
     'L2_xattn_gk_img': (1.0, 0.6),
     'L2_xattn_bv_img': (0.0, 2.0),
     'L2_xattn_bo': (0.0, 0.8),
     'L2_ffn_expert_scale': (1.0, 0.6),
     'L3_xattn_b_q': (0.0, 2.0),
     'L3_xattn_b_k': (0.0, 0.1),
     'L3_xattn_b_v': (0.0, 0.1),
     'L3_xattn_b_k_img': (0.0, 2.0),
     'L3_xattn_b_v_img': (0.0, 2.0),
     'L3_xattn_b_o': (0.0, 0.8),
     'L3_xattn_g_q': (1.0, 0.6),
     'L3_xattn_g_k': (1.0, 0.2),
     'L3_xattn_g_k_img': (1.0, 0.6)}
    factors = {'g_ffn': 8.0,
     'L0_ffn_router_weight': 3.16,
     'L0_ffn_router_bias': 8.0,
     'L0_ffn_gate_up_proj': 2.963,
     'L0_ffn_gate_up_proj_bias': 8.0,
     'L0_ffn_down_proj': 2.888,
     'L0_ffn_down_proj_bias': 8.0,
     'L1_ffn_w_gate_up': 5.64,
     'L1_ffn_w_down': 4.341,
     'L2_xattn_Wq': 26.968,
     'L2_xattn_Wk_img': 25.736,
     'L2_ffn_w_router': 8.0,
     'L2_ffn_w_gate': 8.0,
     'L2_ffn_w_up': 8.0,
     'L2_ffn_w_down': 8.0,
     'L2_ffn_amplitudes': 8.0,
     'L2_ffn_shared_w_gate': 3.83,
     'L2_ffn_shared_w_up': 3.82,
     'L2_ffn_shared_w_down': 3.795,
     'L3_xattn_w_q': 26.2,
     'L3_xattn_w_k_img': 25.264,
     'L2_xattn_Wv_img': 8.0,
     'L2_xattn_Wo': 8.0,
     'L3_xattn_w_v_img': 8.0,
     'L3_xattn_w_o': 8.0,
     'L3_ffn_Wg': 8.0,
     'L3_ffn_w1': 8.0,
     'L3_ffn_w2': 8.0}
    for name, (base, spread) in spreads.items():
        noise = np.random.default_rng([zlib.crc32(name.encode()), seed]).standard_normal(out[name].shape)
        drawn = base * np.exp(spread * noise) if base else spread * noise
        out[name] = jnp.asarray(drawn.astype(out[name].dtype))
    for name, factor in factors.items():
        out[name] = (out[name] * factor).astype(out[name].dtype)
    return out
```

```python
from contextlib import ExitStack

import concourse.bass as bass
from concourse import mybir

F32 = mybir.dt.float32
BF16 = mybir.dt.bfloat16
U32 = mybir.dt.uint32
ALU = mybir.AluOpType
ACT = mybir.ActivationFunctionType
AX_X = mybir.AxisListType.X

P = 128
BATCH, SEQ, DIM = 64, 64, 256
TILES = BATCH * SEQ // P
KC = DIM // P
LN_EPS = 1e-5
PIECES = 3
ROUND_MAGIC = 1.5 * 2.0 ** 23
CAPACITY = 1280


def wait_count(eng, sem, value):
    if not isinstance(value, int) or value > 0:
        eng.wait_ge(sem, value)


def looped(eng, n):
    def run(step):
        step(0)
        with eng.Fori(1, n) as i:
            step(i)
    return run


class Chain:

    def __init__(self, eng, sem, step=0, per=0, base=0):
        self.eng, self.sem, self.step, self.per, self.base, self.n = eng, sem, step, per, base, 0

    def link(self, ins):
        self.n += 1
        ins.then_inc(self.sem, 1)
        self.eng.wait_ge(self.sem, self.step * self.per + (self.base + self.n))

    def close(self):
        assert self.n == self.per, f"{self.n} links, not {self.per}"


class Core:

    def __init__(self, nc, ctx):
        self.nc, self.ctx, self.sems, self.used = nc, ctx, ExitStack(), []
        sb = self.sb
        self.xs = sb(ctx, "xs", [P, TILES, DIM], F32)
        self.ident = sb(ctx, "ident", [P, P], F32)
        self.gates = sb(ctx, "gates", [P, 8], F32)
        self.mv = sb(ctx, "mv", [P, TILES, 2], F32)
        self.rstd = sb(ctx, "rstd", [P, TILES], F32)
        self.half = sb(ctx, "half", [P, 64], F32)

    def sb(self, ctx, name, shape, dt):
        return ctx.enter_context(self.nc.sbuf_tensor(name, shape, dt))

    def ps(self, ctx, name, shape, dt=F32):
        return ctx.enter_context(self.nc.psum_tensor(name, shape, dt))

    def sem(self, name):
        handle = self.sems.enter_context(self.nc.semaphore(name))
        self.used.append(handle.num)
        return handle

    def clear_semaphores(self):
        nums = sorted(self.used)
        starts = [n for n in nums if n - 1 not in nums]
        ends = [n + 1 for n in nums if n + 1 not in nums]
        with self.nc.Block() as block:
            @block.gpsimd
            def _(pool):
                for lo, hi in zip(starts, ends):
                    pool.sem_clear(range(lo, hi))
        self.sems.close()
        self.used = []


def phase_setup(core, x, g_xattn, g_ffn):
    nc = core.nc
    loaded, made, made0, tanhed = (core.sem(n) for n in ("x_loaded", "const_made", "const_zeroed", "gates_tanhed"))
    xv = x.rearrange("b s d -> (b s) d").rearrange("(t p) d -> p t d", p=P)
    with nc.Block() as block:
        @block.sync
        def _(sp):
            sp.dma_start(core.xs[:, :, :], xv).then_inc(loaded, 16)
            sp.dma_start(core.gates[:, 0:4], g_xattn.rearrange("(a n) -> a n", a=1).broadcast_to([P, 4])).then_inc(loaded, 16)
            sp.dma_start(core.gates[:, 4:8], g_ffn.rearrange("(a n) -> a n", a=1).broadcast_to([P, 4])).then_inc(loaded, 16)

        @block.gpsimd
        def _(pool):
            pool.memset(core.ident[:, :], 0.0).then_inc(made0, 1)
            pool.memset(core.half[:, :], -0.5).then_inc(made, 1)
            pool.wait_ge(made0, 1)
            pool.affine_select(out=core.ident[:, :], in_=core.ident[:, :], compare_op=ALU.not_equal, fill=1.0,
                               base=0, pattern=[[-1, P]], channel_multiplier=1).then_inc(made, 1)
            pool.wait_ge(made, 2)

        @block.scalar
        def _(act):
            act.wait_ge(loaded, 48)
            act.activation(core.gates[:, :], core.gates[:, :], ACT.Tanh).then_inc(tanhed, 1)
            act.wait_ge(tanhed, 1)


def phase_norms(core, name):
    nc = core.nc
    stats_done, aggr_done, powed = core.sem(name + "_stats"), core.sem(name + "_aggr"), core.sem(name + "_pow")
    with ExitStack() as ctx:
        stats = core.sb(ctx, name + "_st", [P, TILES, 6], F32)
        vareps = core.sb(ctx, name + "_ve", [P, TILES], F32)
        with nc.Block() as block:
            @block.vector
            def _(dve):
                for t in range(TILES):
                    dve.bn_stats(stats[:, t, :], core.xs[:, t, :]).then_inc(stats_done, 1)
                for t in range(TILES):
                    dve.wait_ge(stats_done, t + 1)
                    dve.bn_aggr(core.mv[:, t, :], stats[:, t, :]).then_inc(aggr_done, 1)
                dve.wait_ge(aggr_done, TILES)
                dve.tensor_scalar(vareps[:, :], core.mv[:, :, 1], LN_EPS, None, ALU.add).then_inc(aggr_done, 1)

            @block.gpsimd
            def _(pool):
                pool.wait_ge(aggr_done, TILES + 1)
                pool.tensor_tensor(core.rstd[:, :], vareps[:, :], core.half[:, 0:TILES], ALU.pow).then_inc(powed, 1)
                pool.wait_ge(powed, 1)



def phase_logits(core, name, E, yT_all, lg_all, router_rows=None, router_cols=None, router_b=None):
    nc = core.nc
    w_loaded, bias_loaded, w_turned, w_ready = (core.sem(name + n) for n in ("_w", "_b", "_wt", "_wr"))
    y_ready, y_turned, staged, logits, taken = (core.sem(name + n) for n in ("_y", "_yt", "_sg", "_lg", "_tk"))
    stored = [core.sem(name + f"_st{u}") for u in range(2)]
    with ExitStack() as ctx:
        rwT = core.sb(ctx, name + "_rwT", [P, KC, E], F32)
        rw = core.sb(ctx, name + "_rw", [P, DIM], F32)
        rb = core.sb(ctx, name + "_rb", [P, E], F32)
        y = core.sb(ctx, name + "_y_sb", [P, 2, DIM], F32)
        stage = core.sb(ctx, name + "_stage", [P, 2, KC, P], F32)
        turned = core.ps(ctx, name + "_psT", [P, 2, 512])
        psL = core.ps(ctx, name + "_psL", [P, 2, 512])
        with nc.Block() as block:
            @block.sync
            def _(sp):
                if router_rows is not None:
                    sp.dma_start(rw[0:E, :], router_rows).then_inc(w_loaded, 16)
                else:
                    sp.dma_start(rwT[:, :, :], router_cols.rearrange("(k p) e -> p k e", p=P)).then_inc(w_ready, 16)
                if router_b is not None:
                    sp.dma_start(rb[:, :], router_b.rearrange("(a n) -> a n", a=1).broadcast_to([P, E])).then_inc(bias_loaded, 16)
                @looped(sp, TILES // 2)
                def _(i):
                    for u in range(2):
                        sp.wait_ge(staged, i * 2 + (u + 3))
                        sp.dma_start(yT_all[i * 2 + u], stage[:, u, :, :].rearrange("p k c -> p (k c)")).then_inc(stored[u], 16)
                for u in range(2):
                    sp.wait_ge(stored[u], 16 * (TILES // 2))

            @block.tensor
            def _(pe):
                if router_rows is not None:
                    pe.wait_ge(w_loaded, 16)
                    for k in range(KC):
                        ins = pe.transpose(psL[:, 0, k * E:(k + 1) * E], rw[0:E, k * P:(k + 1) * P], core.ident[0:E, 0:E])
                    ins.then_inc(w_turned, 1)
                pe.wait_ge(w_ready, 16)
                pe.sem_inc(logits, 2)
                @looped(pe, TILES // 2)
                def _(i):
                    for u in range(2):
                        pe.wait_ge(y_ready, i * 2 + (u + 1))
                        pe.wait_ge(staged, i * 2 + (u + 1))
                        for k in range(KC):
                            ins = pe.transpose(turned[:, u, k * P:(k + 1) * P], y[:, u, k * P:(k + 1) * P], core.ident[:, :])
                        ins.then_inc(y_turned, 1)
                        pe.wait_ge(staged, i * 2 + (u + 3))
                        pe.wait_ge(taken, i * 2 + (u + 1))
                        for k in range(KC):
                            ins = pe.matmul(psL[:, u, 0:E], stage[:, u, k, :], rwT[:, k, :], start=(k == 0), stop=(k == KC - 1))
                        ins.then_inc(logits, 1)

            @block.vector
            def _(dve):
                if router_rows is not None:
                    dve.wait_ge(w_turned, 1)
                    dve.tensor_copy(rwT[:, :, :], psL[:, 0, 0:KC * E].rearrange("p (k e) -> p k e", k=KC)).then_inc(w_ready, 16)
                    dve.wait_ge(w_ready, 16)
                if router_b is not None:
                    dve.wait_ge(bias_loaded, 16)
                dve.sem_inc(staged, 2)
                dve.sem_inc(taken, 2)
                @looped(dve, TILES // 2)
                def _(i):
                    for u in range(2):
                        dve.wait_ge(staged, i * 2 + (u + 1))
                        dve.tensor_scalar(y[:, u, :], core.xs[:, i * 2 + u, :], core.mv[:, i * 2 + u, 0:1],
                                          core.rstd[:, bass.ds(i * 2 + u, 1)], ALU.subtract, ALU.mult).then_inc(y_ready, 1)
                        dve.wait_ge(y_turned, i * 2 + (u + 1))
                        wait_count(dve, stored[u], i * 16)
                        dve.wait_ge(logits, i * 2 + (u + 1))
                        dve.tensor_copy(stage[:, u, :, :], turned[:, u, 0:KC * P].rearrange("p (k c) -> p k c", k=KC)).then_inc(staged, 1)
                        dve.wait_ge(logits, i * 2 + (u + 3))
                        if router_b is not None:
                            dve.tensor_tensor(lg_all[:, i * 2 + u, :], psL[:, u, 0:E], rb[:, :], ALU.add).then_inc(taken, 1)
                        else:
                            dve.tensor_copy(lg_all[:, i * 2 + u, :], psL[:, u, 0:E]).then_inc(taken, 1)
                dve.wait_ge(taken, TILES + 2)


def phase_topk(core, name, E, K, lg_all, score_all, gate, kind, capacity=None):
    nc = core.nc
    T = TILES
    chain, found, exped, posed, ioted = (core.sem(name + n) for n in ("_ch", "_fd", "_ex", "_ps", "_io"))
    with ExitStack() as ctx:
        top = core.sb(ctx, name + "_top", [P, T, 8], F32)
        idx = core.sb(ctx, name + "_idx", [P, T, 8], U32)
        idxf = core.sb(ctx, name + "_idxf", [P, T, 8], F32)
        ex = core.sb(ctx, name + "_exs", [P, T, K], F32)
        exall = core.sb(ctx, name + "_exall", [P, T, E], F32)
        den = core.sb(ctx, name + "_den", [P, 2, T], F32)
        hot = core.sb(ctx, name + "_hot", [P, 2, T, E], F32)
        iota = core.sb(ctx, name + "_iota", [P, E], F32)
        io_b = iota[:, :].rearrange("p (a e) -> p a e", a=1).broadcast_to([P, T, E])

        def per_tile(ap, n):
            return ap.rearrange("p (t a) -> p t a", a=1).broadcast_to([P, T, n])

        if capacity is not None:
            mask = core.sb(ctx, name + "_mask", [P, T, E], F32)
            before = core.sb(ctx, name + "_before", [P, P], F32)
            ones = core.sb(ctx, name + "_ones", [P, P], F32)
            cum = core.sb(ctx, name + "_cum", [P, T, E], F32)
            psR = core.ps(ctx, name + "_psR", [P, 512])
            psC = core.ps(ctx, name + "_psC", [P, 512])
        with nc.Block() as block:
            @block.gpsimd
            def _(pool):
                pool.iota(iota[:, :], pattern=[[1, E]], base=0, channel_multiplier=0,
                          allow_small_or_imprecise_dtypes=True).then_inc(ioted, 1)
                if capacity is not None:
                    pool.memset(before[:, :], 1.0).then_inc(ioted, 1)
                    pool.memset(ones[:, :], 1.0).then_inc(ioted, 1)
                    pool.wait_ge(ioted, 3)
                    pool.affine_select(out=before[:, :], in_=before[:, :], compare_op=ALU.is_gt, fill=0.0,
                                       base=0, pattern=[[1, P]], channel_multiplier=-1).then_inc(ioted, 1)

            @block.scalar
            def _(act):
                act.wait_ge(chain, 1)
                act.activation(ex[:, :, :], ex[:, :, :], ACT.Exp).then_inc(exped, 1)
                if kind != "top":
                    act.wait_ge(chain, 2)
                    act.activation(exall[:, :, :], exall[:, :, :], ACT.Exp).then_inc(exped, 1)

            @block.tensor
            def _(pe):
                if capacity is not None:
                    pe.wait_ge(posed, 1)
                    pe.wait_ge(ioted, 4)
                    pe.matmul(psR[:, 0:T * E], before[:, :], mask[:, :, :], start=True, stop=True).then_inc(found, 1)
                    pe.matmul(psC[:, 0:T * E], ones[:, :], mask[:, :, :], start=True, stop=True).then_inc(found, 1)

            @block.vector
            def _(dve):
                tops, indices = core.sem(name + '_tp'), core.sem(name + '_ix')
                for t in range(T):
                    dve.max(top[:, t, :], lg_all[:, t, :]).then_inc(tops, 1)
                for t in range(T):
                    dve.wait_ge(tops, t + 1)
                    dve.max_index(idx[:, t, :], top[:, t, :], lg_all[:, t, :]).then_inc(indices, 1)
                c = Chain(dve, chain)
                c.link(dve.tensor_tensor(ex[:, :, :], top[:, :, 0:K], per_tile(top[:, :, 0], K), ALU.subtract))
                if kind != "top":
                    c.link(dve.tensor_tensor(exall[:, :, :], lg_all[:, :, :], per_tile(top[:, :, 0], E), ALU.subtract))
                dve.wait_ge(indices, T)
                c.link(dve.tensor_copy(idxf[:, :, :], idx[:, :, :]))
                dve.wait_ge(exped, 1 if kind == "top" else 2)
                c.link(dve.tensor_reduce(den[:, 0, :], ex[:, :, :], AX_X, ALU.add))
                if kind != "top":
                    c.link(dve.tensor_reduce(den[:, 1, :], exall[:, :, :], AX_X, ALU.add))
                if kind == "all":
                    c.link(dve.tensor_copy(den[:, 0, :], den[:, 1, :]))
                if kind == "eps":
                    c.link(dve.scalar_tensor_tensor(out=den[:, 0, :], in0=den[:, 1, :], scalar=1e-8, in1=den[:, 0, :],
                                                    op0=ALU.mult, op1=ALU.add))
                c.link(dve.reciprocal(den[:, 1, :], den[:, 0, :]))
                c.link(dve.tensor_tensor(ex[:, :, :], ex[:, :, :], per_tile(den[:, 1, :], K), ALU.mult))
                c.link(dve.tensor_scalar(ex[:, :, :], ex[:, :, :], gate, None, ALU.mult))
                dve.wait_ge(ioted, 1)
                for k in range(K):
                    c.link(dve.tensor_tensor(hot[:, 0, :, :], io_b, per_tile(idxf[:, :, k], E), ALU.is_equal))
                    if capacity is not None:
                        if k == 0:
                            c.link(dve.tensor_copy(mask[:, :, :], hot[:, 0, :, :]))
                        else:
                            c.link(dve.tensor_tensor(mask[:, :, :], mask[:, :, :], hot[:, 0, :, :], ALU.add))
                    out = score_all[:, :, :] if k == 0 else hot[:, 1, :, :]
                    c.link(dve.tensor_tensor(out, hot[:, 0, :, :], per_tile(ex[:, :, k], E), ALU.mult))
                    if k:
                        c.link(dve.tensor_tensor(score_all[:, :, :], score_all[:, :, :], hot[:, 1, :, :], ALU.add))
                if capacity is not None:
                    dve.sem_inc(posed, 1)
                    dve.wait_ge(found, 2)
                    c.link(dve.tensor_copy(hot[:, 0, :, :], psC[:, 0:T * E].rearrange("p (t e) -> p t e", t=T)))
                    c.link(dve.memset(hot[:, 1, :, :], 1.0))
                    for e in range(E):
                        ins = dve.tensor_tensor_scan(cum[:, :, e], hot[:, 1, :, e], hot[:, 0, :, e], 0.0, ALU.mult, ALU.add)
                        c.link(ins)
                    c.link(dve.tensor_tensor(cum[:, :, :], cum[:, :, :], hot[:, 0, :, :], ALU.subtract))
                    c.link(dve.tensor_tensor(cum[:, :, :], psR[:, 0:T * E].rearrange("p (t e) -> p t e", t=T), cum[:, :, :], ALU.add))
                    c.link(dve.tensor_scalar(cum[:, :, :], cum[:, :, :], float(capacity), None, ALU.is_lt))
                    c.link(dve.tensor_tensor(score_all[:, :, :], score_all[:, :, :], cum[:, :, :], ALU.mult))


def phase_moe0(core, yT_all, score_all, gate_up, gate_up_b, down, down_b):
    nc = core.nc
    E, D2, D = 16, 2 * DIM, DIM
    n = "m0_"
    loaded, fetched = core.sem(n + "loaded"), core.sem(n + "fetched")
    staged, half_ready, sT_turned, sT_ready = (core.sem(n + k) for k in ("staged", "half", "sTt", "sTr"))
    up_done, biased, capped, clipped, tanhed, glu, acted = (core.sem(n + k) for k in ("up", "bias", "cap", "clip", "tanh", "glu", "act"))
    turned, evac, down_done, added = (core.sem(n + k) for k in ("turn", "evac", "down", "add"))
    with ExitStack() as ctx:
        wgu = core.sb(ctx, n + "wgu", [P, E, KC, D2], F32)
        wd = core.sb(ctx, n + "wd", [P, E, KC, D], F32)
        bgu = core.sb(ctx, n + "bgu", [P, E, D2], F32)
        bd = core.sb(ctx, n + "bd", [E, D], F32)
        yT = core.sb(ctx, n + "yT", [P, KC, P], F32)
        yT_in = core.sb(ctx, n + "yT_in", [P, KC, P], F32)
        sc = core.sb(ctx, n + "sc", [P, 2, E], F32)
        scT = core.sb(ctx, n + "scT", [E, P], F32)
        gub = core.sb(ctx, n + "gub", [P, D, 2], F32)
        gcap = core.sb(ctx, n + "gcap", [P, 2, D], F32)
        gsc = core.sb(ctx, n + "gsc", [P, 2, D], F32)
        ucl = core.sb(ctx, n + "ucl", [P, 2, D], F32)
        th = core.sb(ctx, n + "th", [P, 2, D], F32)
        h = core.sb(ctx, n + "h", [P, 2, D], F32)
        hT = core.sb(ctx, n + "hT", [P, 2, KC, P], F32)
        psG = core.ps(ctx, n + "psG", [P, 2, 512])
        psA = core.ps(ctx, n + "psA", [P, 2, 512])
        psO = core.ps(ctx, n + "psO", [P, 512])
        psB = core.ps(ctx, n + "psB", [P, 512])
        with nc.Block() as block:
            @block.sync
            def _(sp):
                for e in range(E):
                    sp.dma_start(wgu[:, e, :, :], gate_up[e].rearrange("(k p) f -> p k f", p=P)).then_inc(loaded, 16)
                    sp.dma_start(wd[:, e, :, :], down[e].rearrange("(k p) f -> p k f", p=P)).then_inc(loaded, 16)
                sp.dma_start(bgu[:, :, :], gate_up_b.rearrange("(a e) f -> a e f", a=1).broadcast_to([P, E, D2])).then_inc(loaded, 16)
                sp.dma_start(bd[:, :], down_b).then_inc(loaded, 16)
                @looped(sp, TILES)
                def _(i):
                    wait_count(sp, staged, i)
                    sp.dma_start(yT_in[:, :, :], yT_all[i].rearrange("p (k c) -> p k c", k=KC)).then_inc(fetched, 16)

            @block.tensor
            def _(pe):
                pe.wait_ge(loaded, 16 * (2 * E + 2))
                pe.sem_inc(turned, 2)
                pe.sem_inc(down_done, 2)
                @looped(pe, TILES)
                def _(i):
                    def up(e):
                        pe.wait_ge(biased, i * E + (e + 1))
                        for k in range(KC):
                            ins = pe.matmul(psG[:, e % 2, :], yT[:, k, :], wgu[:, e, k, :], start=(k == 0), stop=(k == KC - 1))
                        ins.then_inc(up_done, 1)

                    def turn(e):
                        pe.wait_ge(acted, i * E + (e + 3))
                        pe.wait_ge(evac, i * E + (e + 1))
                        for k in range(KC):
                            ins = pe.transpose(psA[:, e % 2, k * P:(k + 1) * P], h[:, e % 2, k * P:(k + 1) * P], core.ident[:, :])
                        ins.then_inc(turned, 1)

                    def project(e):
                        pe.wait_ge(evac, i * E + (e + 3))
                        for k in range(KC):
                            ins = pe.matmul(psO[:, 0:D], hT[:, e % 2, k, :], wd[:, e, k, :], start=False,
                                            stop=(e == E - 1 and k == KC - 1))
                        ins.then_inc(down_done, 1)

                    pe.wait_ge(staged, i + 1)
                    up(0)
                    up(1)
                    pe.wait_ge(half_ready, i + 1)
                    pe.transpose(psB[0:E, 0:P], sc[:, 0, :], core.ident[:, :]).then_inc(sT_turned, 1)
                    pe.wait_ge(sT_ready, i + 1)
                    wait_count(pe, added, i)
                    pe.matmul(psO[:, 0:D], scT[:, :], bd[:, :], start=True, stop=False)
                    for e in range(E):
                        turn(e)
                        if e + 2 < E:
                            up(e + 2)
                        project(e)

            @block.scalar
            def _(act):
                act.sem_inc(evac, 2)
                @looped(act, TILES)
                def _(i):
                    act.wait_ge(down_done, i * E + 2)
                    act.wait_ge(fetched, i * 16 + 16)
                    act.activation(yT[:, :, :], yT_in[:, :, :], ACT.Copy).then_inc(staged, 1)
                    act.wait_ge(sT_turned, i + 1)
                    act.activation(scT[:, :], psB[0:E, 0:P], ACT.Copy).then_inc(sT_ready, 1)

                    def tanh(e):
                        act.wait_ge(capped, i * E + (e + 1))
                        act.wait_ge(acted, i * E + (e + 1))
                        act.activation(th[:, e % 2, :], gcap[:, e % 2, :], ACT.Tanh, scale=0.5 * 1.702).then_inc(tanhed, 1)

                    tanh(0)
                    for e in range(E):
                        if e + 1 < E:
                            tanh(e + 1)
                        act.wait_ge(turned, i * E + (e + 3))
                        act.wait_ge(down_done, i * E + (e + 1))
                        act.activation(hT[:, e % 2, :, :], psA[:, e % 2, 0:KC * P].rearrange("p (k c) -> p k c", k=KC), ACT.Copy).then_inc(evac, 1)

            @block.vector
            def _(dve):
                dve.wait_ge(loaded, 16 * (2 * E + 2))
                dve.sem_inc(biased, 2)
                dve.sem_inc(acted, 2)
                @looped(dve, TILES)
                def _(i):
                    wait_count(dve, sT_turned, i)
                    dve.tensor_scalar(sc[:, 0, :], score_all[:, i, :], 1.0, None, ALU.mult)
                    dve.tensor_scalar(sc[:, 1, :], score_all[:, i, :], 0.5, None, ALU.mult).then_inc(half_ready, 1)
                    dve.wait_ge(half_ready, i + 1)

                    def gate_and_up(e):
                        dve.wait_ge(up_done, i * E + (e + 1))
                        wait_count(dve, clipped, i * E + e)
                        dve.tensor_tensor(gub[:, :, :], psG[:, e % 2, :].rearrange("p (d a) -> p d a", a=2),
                                          bgu[:, e, :].rearrange("p (d a) -> p d a", a=2), ALU.add).then_inc(biased, 1)
                        dve.wait_ge(biased, i * E + (e + 3))
                        dve.tensor_scalar(gcap[:, e % 2, :], gub[:, :, 0], 7.0, None, ALU.min).then_inc(capped, 1)
                        dve.tensor_scalar(gsc[:, e % 2, :], gub[:, :, 0], 7.0, sc[:, 1, e:e + 1], ALU.min, ALU.mult)
                        dve.tensor_scalar(ucl[:, e % 2, :], gub[:, :, 1], 7.0, -7.0, ALU.min, ALU.max).then_inc(clipped, 1)

                    def activate(e):
                        dve.wait_ge(tanhed, i * E + (e + 1))
                        dve.wait_ge(clipped, i * E + (e + 1))
                        dve.scalar_tensor_tensor(out=gsc[:, e % 2, :], in0=th[:, e % 2, :], scalar=1.0, in1=gsc[:, e % 2, :],
                                                 op0=ALU.add, op1=ALU.mult).then_inc(glu, 1)
                        dve.wait_ge(glu, i * E + (e + 1))
                        dve.wait_ge(turned, i * E + (e + 1))
                        dve.scalar_tensor_tensor(out=h[:, e % 2, :], in0=ucl[:, e % 2, :], scalar=1.0, in1=gsc[:, e % 2, :],
                                                 op0=ALU.add, op1=ALU.mult).then_inc(acted, 1)

                    gate_and_up(0)
                    for e in range(E):
                        if e + 1 < E:
                            gate_and_up(e + 1)
                        activate(e)
                    dve.wait_ge(down_done, i * E + (E + 2))
                    dve.tensor_tensor(core.xs[:, i, :], core.xs[:, i, :], psO[:, 0:D], ALU.add).then_inc(added, 1)
                dve.wait_ge(added, TILES)



def phase_moe3(core, yT_all, score_all, w1, w2):
    nc = core.nc
    E, F, D, N2 = 8, 1024, DIM, 2 * P
    FC = F // P
    n = "m3_"
    fetched = core.sem(n + "fetched")
    loaded, staged, up_done, relued, down_done, added = (core.sem(n + k) for k in ("loaded", "staged", "up", "relu", "down", "add"))
    with ExitStack() as ctx:
        w1s = core.sb(ctx, n + "w1", [P, E, KC, F], F32)
        w2s = core.sb(ctx, n + "w2", [P, E, FC, D], F32)
        yT = core.sb(ctx, n + "yT", [P, 2, KC, P], F32)
        yT_in = core.sb(ctx, n + "yT_in", [P, 2, KC * P], F32)
        hT = core.sb(ctx, n + "hT", [P, FC, N2], F32)
        psH = core.ps(ctx, n + "psH", [P, FC // 2, 512])
        psD = core.ps(ctx, n + "psD", [P, 2, 512])
        with nc.Block() as block:
            @block.sync
            def _(sp):
                for e in range(E):
                    sp.dma_start(w1s[:, e, :, :], w1[e].rearrange("(k p) f -> p k f", p=P)).then_inc(loaded, 16)
                    sp.dma_start(w2s[:, e, :, :], w2[e].rearrange("(k p) d -> p k d", p=P)).then_inc(loaded, 16)
                @looped(sp, TILES // 2)
                def _(i):
                    wait_count(sp, staged, i)
                    sp.dma_start(yT_in[:, :, :], yT_all[bass.ds(i * 2, 2)].rearrange("t p c -> p t c")).then_inc(fetched, 16)

            @block.tensor
            def _(pe):
                pe.wait_ge(loaded, 16 * 2 * E)
                @looped(pe, TILES // 2)
                def _(i):
                    def up(e):
                        for b in range(FC // 2):
                            pe.wait_ge(relued, i * (E * 4) + (e * 4 + b + 1))
                            for f in (2 * b, 2 * b + 1):
                                for k in range(KC):
                                    ins = pe.matmul(psH[:, b, (f % 2) * N2:(f % 2 + 1) * N2], w1s[:, e, k, f * P:(f + 1) * P],
                                                    yT[:, :, k, :], start=(k == 0), stop=(k == KC - 1))
                            ins.then_inc(up_done, 1)

                    def project(e):
                        pe.wait_ge(relued, i * (E * 4) + (e * 4 + 8))
                        pe.wait_ge(added, i * (E * 2) + (e * 2 + 2))
                        for tt in range(2):
                            for f in range(FC):
                                ins = pe.matmul(psD[:, e % 2, tt * D:(tt + 1) * D], hT[:, f, tt * P:(tt + 1) * P],
                                                w2s[:, e, f, :], start=(f == 0), stop=(f == FC - 1))
                        ins.then_inc(down_done, 1)

                    pe.wait_ge(staged, i + 1)
                    up(0)
                    for e in range(E):
                        if e + 1 < E:
                            up(e + 1)
                        project(e)

            @block.scalar
            def _(act):
                act.sem_inc(relued, 4)
                @looped(act, TILES // 2)
                def _(i):
                    wait_count(act, down_done, i * E)
                    act.wait_ge(fetched, i * 16 + 16)
                    act.activation(yT[:, :, :, :], yT_in[:, :, :].rearrange("p t (k c) -> p t k c", k=KC), ACT.Copy).then_inc(staged, 1)
                    for e in range(E):
                        for b in range(FC // 2):
                            act.wait_ge(up_done, i * (E * 4) + (e * 4 + b + 1))
                            wait_count(act, down_done, i * E + e)
                            act.activation(hT[:, 2 * b:2 * b + 2, :], psH[:, b, :].rearrange("p (f c) -> p f c", f=2), ACT.Relu).then_inc(relued, 1)

            @block.vector
            def _(dve):
                dve.sem_inc(added, 4)
                @looped(dve, TILES // 2)
                def _(i):
                    for e in range(E):
                        dve.wait_ge(down_done, i * E + (e + 1))
                        for tt in range(2):
                            dve.wait_ge(added, i * (E * 2) + (e * 2 + tt + 3))
                            dve.scalar_tensor_tensor(out=core.xs[:, i * 2 + tt, :], in0=psD[:, e % 2, tt * D:(tt + 1) * D],
                                                     scalar=score_all[:, i * 2 + tt, e:e + 1], in1=core.xs[:, i * 2 + tt, :],
                                                     op0=ALU.mult, op1=ALU.add).then_inc(added, 1)
                dve.wait_ge(added, 4 + TILES * E)


def phase_store(core, out):
    nc = core.nc
    stored = core.sem("stored")
    with nc.Block() as block:
        @block.sync
        def _(sp):
            sp.dma_start(out.rearrange("b s d -> (b s) d").rearrange("(t p) d -> p t d", p=P), core.xs[:, :, :]).then_inc(stored, 16)
            sp.wait_ge(stored, 16)


HEADS, HD = 8, 8
PAIRS = HEADS // 2
Q_SLOTS, K_SLOTS = (0, 0, 1, 0, 1, 2), (0, 1, 0, 2, 1, 0)
SLOTS = len(Q_SLOTS)
GROUP = 4
ROWS = 2 * SLOTS * HD


def phase_split(core, name, src, aug, slots, l2norm):
    nc = core.nc
    G = GROUP
    chain, loaded, zready, p_ready, r_ready, squared, summed, rooted, used = (
        core.sem(name + k) for k in ("_ch", "_ld", "_z", "_p", "_r", "_sq", "_sm", "_rt", "_us"))
    made, stored = core.sem(name + "_mk"), core.sem(name + "_st")
    with ExitStack() as ctx:
        z = core.sb(ctx, name + "_zz", [P, G, DIM], F32)
        nrm = core.sb(ctx, name + "_nrm", [P, G, DIM], F32)
        r = core.sb(ctx, name + "_rr", [P, 2, G, DIM], F32)
        parts = core.sb(ctx, name + "_parts", [P, PIECES, G, DIM], BF16)
        block_ones = core.sb(ctx, name + "_bo", [P, P], F32)
        psN = core.ps(ctx, name + "_psN", [P, G, DIM])
        n_store = len(slots) * 4
        with nc.Block() as block:
            @block.sync
            def _(sp):
                @looped(sp, TILES // G)
                def _(i):
                    if src is not None:
                        wait_count(sp, p_ready, i * PIECES)
                        sp.dma_start(z[:, :, :], src[bass.ds(i * G, G)].rearrange("t p c -> p t c")).then_inc(loaded, 16)
                    for s, piece in enumerate(slots):
                        sp.wait_ge(p_ready, i * PIECES + (piece + 1))
                        for b in range(2):
                            for hh in range(2):
                                r0 = (hh * SLOTS + s) * HD
                                lo = 64 * b + 32 * hh
                                sp.dma_start(aug[i, b, r0:r0 + HD].rearrange("r a c -> a r c"),
                                             parts[lo:lo + 32, piece, :, :].rearrange("p g c -> p (g c)")).then_inc(stored, 16)
                sp.wait_ge(stored, 16 * n_store * (TILES // G))

            @block.gpsimd
            def _(pool):
                if l2norm:
                    bo = block_ones[:, :].rearrange("p (a r) -> p a r", r=HD)
                    pool.memset(block_ones[:, :], 1.0).then_inc(made, 1)
                    pool.wait_ge(made, 1)
                    pool.affine_select(out=bo, in_=bo, compare_op=ALU.is_ge, fill=0.0, base=0,
                                       pattern=[[-HD, P // HD], [0, HD]], channel_multiplier=1).then_inc(made, 1)
                    pool.wait_ge(made, 2)
                    pool.affine_select(out=bo, in_=bo, compare_op=ALU.is_ge, fill=0.0, base=HD - 1,
                                       pattern=[[HD, P // HD], [0, HD]], channel_multiplier=-1).then_inc(made, 1)

            @block.tensor
            def _(pe):
                if l2norm:
                    pe.wait_ge(made, 3)
                    @looped(pe, TILES // G)
                    def _(i):
                        pe.wait_ge(squared, i + 1)
                        for g in range(0, G, 2):
                            ins = pe.matmul(psN[:, g:g + 2, :], block_ones[:, :], nrm[:, g:g + 2, :], start=True, stop=True)
                        ins.then_inc(summed, 1)

            @block.scalar
            def _(act):
                @looped(act, TILES // G)
                def _(i):
                    if l2norm:
                        act.wait_ge(zready, i + 1)
                        wait_count(act, used, i)
                        act.activation(nrm[:, :, :], z[:, :, :], ACT.Square).then_inc(squared, 1)
                        act.wait_ge(summed, i + 1)
                        act.activation(nrm[:, :, :], psN[:, :, :], ACT.Sqrt).then_inc(rooted, 1)
                        act.wait_ge(used, i + 1)
                    else:
                        act.wait_ge(zready, i + 1)
                    wait_count(act, stored, i * (16 * n_store))
                    act.activation(parts[:, 0, :, :], z[:, :, :], ACT.Copy).then_inc(p_ready, 1)
                    for k in range(1, PIECES):
                        act.wait_ge(r_ready, i * 2 + k)
                        act.activation(parts[:, k, :, :], r[:, k - 1, :, :], ACT.Copy).then_inc(p_ready, 1)

            @block.vector
            def _(dve):
                @looped(dve, TILES // G)
                def _(i):
                    if src is None:
                        wait_count(dve, p_ready, i * PIECES)
                        for g in range(G):
                            ins = dve.tensor_scalar(z[:, g, :], core.xs[:, i * G + g, :], core.mv[:, i * G + g, 0:1],
                                                    core.rstd[:, bass.ds(i * G + g, 1)], ALU.subtract, ALU.mult)
                        ins.then_inc(zready, 1)
                        dve.wait_ge(zready, i + 1)
                    else:
                        dve.wait_ge(loaded, i * 16 + 16)
                        dve.sem_inc(zready, 1)
                    if l2norm:
                        c = Chain(dve, chain, i, 2)
                        dve.wait_ge(rooted, i + 1)
                        c.link(dve.tensor_scalar(nrm[:, :, :], nrm[:, :, :], 1e-12, None, ALU.max))
                        c.link(dve.reciprocal(nrm[:, :, :], nrm[:, :, :]))
                        dve.tensor_tensor(z[:, :, :], z[:, :, :], nrm[:, :, :], ALU.mult).then_inc(used, 1)
                        dve.wait_ge(used, i + 1)
                        c.close()
                    dve.wait_ge(p_ready, i * PIECES + 1)
                    dve.tensor_tensor(r[:, 0, :, :], z[:, :, :], parts[:, 0, :, :], ALU.subtract).then_inc(r_ready, 1)
                    dve.wait_ge(p_ready, i * PIECES + 2)
                    dve.wait_ge(r_ready, i * 2 + 1)
                    dve.tensor_tensor(r[:, 1, :, :], r[:, 0, :, :], parts[:, 1, :, :], ALU.subtract).then_inc(r_ready, 1)


def phase_context(core, ctx_tiles, ctxT_dram, vt_dram):
    nc = core.nc
    loaded = [core.sem(f"cx_loaded{u}") for u in range(2)]
    stored = [core.sem(f"cx_stored{u}") for u in range(2)]
    turned, taken, made = (core.sem("cx_" + k) for k in ("turned", "taken", "made"))
    with ExitStack() as ctx:
        cx = core.sb(ctx, "cx_in", [P, 2, DIM], F32)
        ct = core.sb(ctx, "cx_ct", [P, 2, KC, P], F32)
        vt = core.sb(ctx, "cx_vt", [P, 2, KC, 2 * HEADS, HD + 1], F32)
        psT = core.ps(ctx, "cx_ps", [P, 2, 512])
        with nc.Block() as block:
            @block.sync
            def _(sp):
                @looped(sp, TILES // 2)
                def _(i):
                    for u in range(2):
                        sp.wait_ge(turned, i * 2 + (u + 1))
                        sp.dma_start(cx[:, u, :], ctx_tiles[i * 2 + u]).then_inc(loaded[u], 16)
                    for u in range(2):
                        sp.wait_ge(taken, i * 4 + (2 * u + 6))
                        sp.dma_start(ctxT_dram[i * 2 + u], ct[:, u, :, :].rearrange("p k c -> p (k c)")).then_inc(stored[u], 16)
                        sp.dma_start(vt_dram[i * 2 + u], vt[:, u, :, :, :].rearrange("p k h d -> p (k h d)")).then_inc(stored[u], 16)
                for u in range(2):
                    sp.wait_ge(stored[u], 32 * (TILES // 2))

            @block.gpsimd
            def _(pool):
                pool.memset(vt[:, :, :, :, :], 1.0).then_inc(made, 1)

            @block.tensor
            def _(pe):
                pe.sem_inc(turned, 2)
                @looped(pe, TILES // 2)
                def _(i):
                    for u in range(2):
                        pe.wait_ge(loaded[u], i * 16 + 16)
                        pe.wait_ge(taken, i * 4 + (2 * u + 2))
                        for k in range(KC):
                            ins = pe.transpose(psT[:, u, k * P:(k + 1) * P], cx[:, u, k * P:(k + 1) * P], core.ident[:, :])
                        ins.then_inc(turned, 1)

            @block.vector
            def _(dve):
                dve.sem_inc(taken, 4)
                dve.wait_ge(made, 1)
                @looped(dve, TILES // 2)
                def _(i):
                    for u in range(2):
                        dve.wait_ge(turned, i * 2 + (u + 3))
                        wait_count(dve, stored[u], i * 32)
                        dve.tensor_copy(ct[:, u, :, :], psT[:, u, 0:KC * P].rearrange("p (k c) -> p k c", k=KC)).then_inc(taken, 1)
                        for k in range(KC):
                            ins = dve.tensor_copy(vt[:, u, k, :, 0:HD], psT[:, u, k * P:(k + 1) * P].rearrange("p (h d) -> p h d", d=HD))
                        ins.then_inc(taken, 1)


def phase_attend(core, name, q_aug, k_aug, vt_dram, gate, scale, with_max):
    nc = core.nc
    n = name
    NB = 4
    STEPS = 2 * TILES // NB
    KR = ROWS + 4 if with_max else ROWS
    q_loaded = [core.sem(f"{n}_ql{m}") for m in range(NB)]
    v_loaded = [core.sem(f"{n}_vl{m}") for m in range(2)]
    shift_loaded = [core.sem(f"{n}_sl{m}") for m in range(NB)]
    s_done, max_done, max_turned, shift_read, shift_ready = (core.sem(n + k) for k in ("_s", "_mx", "_mt", "_sr", "_sh"))
    st_done, exp_done, pv_done, out_done, nd_done, added, chain, made, cleared, rec_done = (
        core.sem(n + k) for k in ("_st", "_ex", "_pv", "_ov", "_nd", "_ad", "_ch", "_mk", "_cl", "_rd"))
    with ExitStack() as ctx:
        qa = core.sb(ctx, n + "_qa", [P, NB, 2, PAIRS, DIM], BF16)
        ka = core.sb(ctx, n + "_ka", [P, NB, PAIRS, DIM], BF16)
        vt = core.sb(ctx, n + "_vt", [P, 2, KC, 2 * HEADS, HD + 1], F32)
        pt = core.sb(ctx, n + "_pt", [P, PAIRS, KC, 2 * DIM], F32)
        mx = core.sb(ctx, n + "_mx_sb", [P, 2, 2 * HEADS], F32)
        sh = core.sb(ctx, n + "_sh_sb", [2 * HEADS, 2, 2, P], BF16)
        ov = core.sb(ctx, n + "_ov_sb", [P, 2, 2, DIM], F32)
        rec = core.sb(ctx, n + "_rec", [P, DIM], F32)
        pick = core.sb(ctx, n + "_pick", [P, 2, 2, 64], F32)
        psM = core.ps(ctx, n + "_psM", [P, 2, 512])
        psS = core.ps(ctx, n + "_psS", [P, 2, KC, 512])
        psV = core.ps(ctx, n + "_psV", [P, 2, DIM])
        psN = core.ps(ctx, n + "_psN", [P, 2, DIM])

        def aug_tile(aug, b, t):
            return aug[t // GROUP, b].rearrange("r a (g c) -> g r a c", g=GROUP)[t % GROUP]

        def count(j, m, per, more):
            return j * (NB * per) + (m * per + more)

        with nc.Block() as block:
            @block.gpsimd
            def _(pool):
                pool.memset(qa[:, :, :, :, :], 0.0).then_inc(made, 1)
                pool.memset(ka[:, :, :, :], 1.0).then_inc(made, 1)
                pool.memset(pick[:, :, :, :], 0.0).then_inc(made, 1)
                pool.wait_ge(made, 3)
                for d in range(2):
                    for g in range(2):
                        v = pick[:, d, g, :].rearrange("p (hh g a i) -> p g hh a i", hh=2, g=2, a=2)[:, g]
                        pool.affine_select(out=v, in_=v, compare_op=ALU.not_equal, fill=1.0, base=-HD * d,
                                           pattern=[[-32, 2], [-64, 2], [d - 1, HD]], channel_multiplier=1).then_inc(made, 1)

            @block.sync
            def _(sp):
                def load(j, m):
                    b = m % 2
                    t = j * 2 + m // 2
                    for hh in range(2):
                        r = slice(hh * SLOTS * HD, (hh + 1) * SLOTS * HD)
                        sp.dma_start(qa[r, m, hh, :, :], aug_tile(q_aug, b, t)[r]).then_inc(q_loaded[m], 16)
                    sp.dma_start(ka[0:ROWS, m, :, :], aug_tile(k_aug, b, t)).then_inc(q_loaded[m], 16)

                def load_values(j, u):
                    sp.dma_start(vt[:, u, :, :, :].rearrange("p k h d -> p (k h d)"), vt_dram[j * 2 + u]).then_inc(v_loaded[u], 16)

                def shift(j, m):
                    sp.wait_ge(shift_ready, count(j, m, 1, 1))
                    for hh in range(2):
                        for s in range(2):
                            row = ROWS + 2 * hh + s
                            sp.dma_start(qa[row:row + 1, m, hh, :, :].rearrange("p a (f c) -> p (a f) c", f=2),
                                         sh[8 * hh:8 * hh + 8, m % 2, s, :]).then_inc(shift_loaded[m], 16)

                sp.wait_ge(made, 3)
                for m in range(NB):
                    load(0, m)
                for u in range(2):
                    load_values(0, u)
                if with_max:
                    shift(0, 0)
                    shift(0, 1)

                def step(j, last):
                    for m in range(NB):
                        if with_max and not (last and m >= 2):
                            shift(j + (m + 2) // NB, (m + 2) % NB)
                        if not last:
                            sp.wait_ge(st_done, count(j, m, PAIRS, PAIRS))
                            load(j + 1, m)
                            if m % 2:
                                sp.wait_ge(pv_done, count(j, m, 2, 4))
                                load_values(j + 1, m // 2)

                @looped(sp, STEPS - 1)
                def _(j):
                    step(j, False)
                step(STEPS - 1, True)

            @block.tensor
            def _(pe):
                def scores(j, m, heads):
                    for h in heads:
                        if h == 0:
                            pe.wait_ge(q_loaded[m], j * 48 + 48)
                            wait_count(pe, shift_read, count(j, m, 1, 0))
                        pe.wait_ge(max_done, count(j, m, HEADS, h + 1))
                        a, hh = h // 2, h % 2
                        for f in range(2):
                            ins = pe.matmul(psM[:, h % 2, f * DIM:(f + 1) * DIM], qa[0:ROWS, m, hh, a, f * P:(f + 1) * P],
                                            ka[0:ROWS, m, a, :], start=True, stop=True)
                        ins.then_inc(s_done, 1)

                def turn_max(j, m):
                    pe.wait_ge(max_done, count(j, m, HEADS, HEADS + 2))
                    pe.transpose(psM[0:2 * HEADS, 0, 0:P], mx[:, m % 2, :], core.ident[:, :]).then_inc(max_turned, 1)

                def scores_t(j, m, a):
                    if a == 0:
                        pe.wait_ge(q_loaded[m], j * 48 + 48)
                        if with_max:
                            pe.wait_ge(shift_loaded[m], j * 64 + 64)
                    pe.wait_ge(exp_done, count(j, m, PAIRS, a + 1))
                    for k in range(KC):
                        ins = pe.matmul(psS[:, a % 2, k, :], ka[0:KR, m, a, k * P:(k + 1) * P], qa[0:KR, m, :, a, :], start=True, stop=True)
                    ins.then_inc(st_done, 1)

                def values(j, m, g):
                    if g == 0:
                        wait_count(pe, out_done, count(j, m, 1, 0))
                        pe.wait_ge(v_loaded[m // 2], j * 16 + 16)
                    pe.wait_ge(exp_done, count(j, m, PAIRS, 2 * g + 4))
                    for k in range(KC):
                        for q in range(4):
                            a, hh = 2 * g + q // 2, q % 2
                            ins = pe.matmul(psV[32 * q:32 * q + HD + 1, g, :], vt[:, m // 2, k, HEADS * (m % 2) + 4 * hh + a, :],
                                            pt[:, a, k, hh * DIM:(hh + 1) * DIM], start=(k == 0), stop=(k == KC - 1),
                                            tile_position=(0, 32 * q))
                    ins.then_inc(pv_done, 1)

                def gather_heads(j, m):
                    pe.wait_ge(out_done, count(j, m, 1, 1))
                    b = m % 2
                    if b == 0:
                        wait_count(pe, added, j * 2 + m // 2)
                    for d in range(2):
                        for g in range(2):
                            ins = pe.matmul(psN[64 * b:64 * b + 64, d, :], pick[:, d, g, :], ov[:, b, g, :],
                                            start=(g == 0), stop=(g == 1), tile_position=(0, 64 * b))
                    ins.then_inc(nd_done, 1)

                pe.sem_inc(pv_done, 2)
                pe.sem_inc(nd_done, 2)
                pe.wait_ge(made, 7)
                pe.wait_ge(cleared, 1)
                if with_max:
                    for m in range(2):
                        scores(0, m, range(HEADS))
                        turn_max(0, m)

                def step(j, first, last):
                    for m in range(NB):
                        ahead = with_max and not (last and m >= 2)
                        nj, nm = j + (m + 2) // NB, (m + 2) % NB
                        scores_t(j, m, 0)
                        scores_t(j, m, 1)
                        if not (first and m == 0):
                            if m:
                                gather_heads(j, m - 1)
                            else:
                                gather_heads(j - 1, NB - 1)
                        if ahead:
                            scores(nj, nm, (0, 1))
                        scores_t(j, m, 2)
                        if ahead:
                            scores(nj, nm, (2, 3))
                        scores_t(j, m, 3)
                        if ahead:
                            scores(nj, nm, (4, 5))
                        values(j, m, 0)
                        if ahead:
                            scores(nj, nm, (6, 7))
                        values(j, m, 1)
                        if ahead:
                            turn_max(nj, nm)

                step(0, True, False)
                with pe.Fori(1, STEPS - 1) as j:
                    step(j, False, False)
                step(STEPS - 1, False, True)
                gather_heads(STEPS - 1, NB - 1)

            @block.scalar
            def _(act):
                act.sem_inc(exp_done, 2)
                act.wait_ge(made, 7)

                def step(j):
                    for m in range(NB):
                        for a in range(PAIRS):
                            act.wait_ge(st_done, count(j, m, PAIRS, a + 1))
                            act.wait_ge(pv_done, count(j, m, 2, a // 2 + 1))
                            act.activation(pt[:, a, :, :], psS[:, a % 2, :, :], ACT.Exp, scale=scale).then_inc(exp_done, 1)
                        act.wait_ge(pv_done, count(j, m, 2, 4))
                        act.wait_ge(nd_done, count(j, m, 1, 1))
                        act.activation(ov[:, m % 2, :, :], psV[:, :, :], ACT.Copy).then_inc(out_done, 1)

                @looped(act, STEPS)
                def _(j):
                    step(j)

            @block.vector
            def _(dve):
                def maxima(j, m, heads):
                    for h in heads:
                        dve.wait_ge(s_done, count(j, m, HEADS, h + 1))
                        if h == 0:
                            wait_count(dve, max_turned, count(j, m, 1, 0))
                        dve.tensor_reduce(mx[:, m % 2, h % 2 * 8 + h // 2 * 2:h % 2 * 8 + h // 2 * 2 + 2], psM[:, h % 2, :].rearrange("p (f c) -> p f c", f=2),
                                          AX_X, ALU.max).then_inc(max_done, 1)

                def shifts(j, m):
                    dve.wait_ge(max_turned, count(j, m, 1, 1))
                    if m >= 2:
                        dve.wait_ge(shift_loaded[m - 2], j * 64 + 64)
                    else:
                        wait_count(dve, shift_loaded[m + 2], j * 64)
                    dve.tensor_scalar(sh[:, m % 2, 0, :], psM[0:2 * HEADS, 0, 0:P], -1.0, None, ALU.mult).then_inc(chain, 1)
                    dve.wait_ge(chain, count(j, m, 1, 1))
                    dve.scalar_tensor_tensor(out=sh[:, m % 2, 1, :], in0=psM[0:2 * HEADS, 0, 0:P], scalar=-1.0,
                                             in1=sh[:, m % 2, 0, :], op0=ALU.mult, op1=ALU.subtract).then_inc(shift_ready, 1)
                    dve.wait_ge(shift_ready, count(j, m, 1, 1))
                    dve.sem_inc(shift_read, 1)

                def add_tile(j, u):
                    t = j * 2 + u
                    dve.wait_ge(nd_done, j * NB + (2 * u + 4))
                    dve.reciprocal(rec[:, :], psN[:, 1, :]).then_inc(rec_done, 1)
                    dve.wait_ge(rec_done, j * 4 + (2 * u + 1))
                    dve.tensor_tensor(rec[:, :], psN[:, 0, :], rec[:, :], ALU.mult).then_inc(rec_done, 1)
                    dve.wait_ge(rec_done, j * 4 + (2 * u + 2))
                    dve.scalar_tensor_tensor(out=core.xs[:, t, :], in0=rec[:, :], scalar=gate, in1=core.xs[:, t, :],
                                             op0=ALU.mult, op1=ALU.add).then_inc(added, 1)
                    dve.wait_ge(added, t + 1)

                dve.memset(psV[:, :, :], 0.0).then_inc(cleared, 1)
                dve.sem_inc(max_done, 2)
                if with_max:
                    for m in range(2):
                        maxima(0, m, range(HEADS))
                        shifts(0, m)

                def step(j, first, last):
                    for m in range(NB):
                        ahead = with_max and not (last and m >= 2)
                        nj, nm = j + (m + 2) // NB, (m + 2) % NB
                        if ahead:
                            maxima(nj, nm, range(0, 2))
                        if m == 2:
                            add_tile(j, 0)
                        if m == 0 and not first:
                            add_tile(j - 1, 1)
                        if ahead:
                            maxima(nj, nm, range(2, HEADS))
                            shifts(nj, nm)

                step(0, True, False)
                with dve.Fori(1, STEPS - 1) as j:
                    step(j, False, False)
                step(STEPS - 1, False, True)
                add_tile(STEPS - 1, 1)


def pipelined(eng, step, first, last, head, tail):
    lo, hi = first + head, last - tail
    assert lo % 2 == 0 and (hi - lo) % 2 == 0
    for s in range(first, lo):
        step(s, s % 2)
    with eng.Fori(lo // 2, hi // 2) as j:
        for v in range(2):
            step(j * 2 + v, v)
    for s in range(hi, last):
        step(s, s % 2)


def valid(t):
    return not isinstance(t, int) or 0 <= t < TILES


def phase_turn_weights(core, name, pairs):
    nc = core.nc
    n = len(pairs)
    loaded, turned, copied, stored = (core.sem(name + k) for k in ("_l", "_t", "_c", "_s"))
    with ExitStack() as ctx:
        w = core.sb(ctx, name + "_w", [P, n, KC, DIM], F32)
        wt = core.sb(ctx, name + "_wt", [P, n, KC, DIM], F32)
        ps = core.ps(ctx, name + "_ps", [P, n, 512])
        with nc.Block() as block:
            @block.sync
            def _(sp):
                for m, (src, _) in enumerate(pairs):
                    sp.dma_start(w[:, m, :, :], src.rearrange("(o p) i -> p o i", p=P)).then_inc(loaded, 16)
                for m, (_, dst) in enumerate(pairs):
                    sp.wait_ge(copied, m + 1)
                    sp.dma_start(dst.rearrange("(k p) o -> p k o", p=P), wt[:, m, :, :]).then_inc(stored, 16)
                sp.wait_ge(stored, 16 * n)

            @block.tensor
            def _(pe):
                pe.wait_ge(loaded, 16 * n)
                for m in range(n):
                    for k in range(KC):
                        for o in range(KC):
                            ins = pe.transpose(ps[:, m, k * DIM + o * P:k * DIM + (o + 1) * P], w[:, m, o, k * P:(k + 1) * P], core.ident[:, :])
                    ins.then_inc(turned, 1)

            @block.scalar
            def _(act):
                for m in range(n):
                    act.wait_ge(turned, m + 1)
                    act.activation(wt[:, m, :, :], ps[:, m, :].rearrange("p (k o) -> p k o", k=KC), ACT.Copy).then_inc(copied, 1)


def phase_keys_values(core, name, ctxT_dram, kv_all, wk, wv, bk, bv):
    nc = core.nc
    w_loaded, done, added = (core.sem(name + k) for k in ("_w", "_d", "_a"))
    loaded = [core.sem(f"{name}_l{u}") for u in range(2)]
    with ExitStack() as ctx:
        w = core.sb(ctx, name + "_ws", [P, KC, 2, DIM], F32)
        b = core.sb(ctx, name + "_bs", [P, 2, DIM], F32)
        ct = core.sb(ctx, name + "_ct", [P, 2, KC, P], F32)
        ps = core.ps(ctx, name + "_ps", [P, 2, 512])
        with nc.Block() as block:
            @block.sync
            def _(sp):
                for m, (ww, bb) in enumerate(((wk, bk), (wv, bv))):
                    sp.dma_start(w[:, :, m, :], ww.rearrange("(k p) o -> p k o", p=P)).then_inc(w_loaded, 16)
                    sp.dma_start(b[:, m, :], bb.rearrange("(a n) -> a n", a=1).broadcast_to([P, DIM])).then_inc(w_loaded, 16)
                @looped(sp, TILES // 2)
                def _(i):
                    for u in range(2):
                        sp.wait_ge(done, i * 2 + (u + 1))
                        sp.dma_start(ct[:, u, :, :].rearrange("p k c -> p (k c)"), ctxT_dram[i * 2 + u]).then_inc(loaded[u], 16)

            @block.tensor
            def _(pe):
                pe.sem_inc(done, 2)
                pe.wait_ge(w_loaded, 64)
                @looped(pe, TILES // 2)
                def _(i):
                    for u in range(2):
                        pe.wait_ge(loaded[u], i * 16 + 16)
                        pe.wait_ge(added, i * 2 + (u + 1))
                        for k in range(KC):
                            ins = pe.matmul(ps[:, u, :], ct[:, u, k, :], w[:, k, :, :], start=(k == 0), stop=(k == KC - 1))
                        ins.then_inc(done, 1)

            @block.vector
            def _(dve):
                dve.sem_inc(added, 2)
                dve.wait_ge(w_loaded, 64)
                @looped(dve, TILES // 2)
                def _(i):
                    for u in range(2):
                        dve.wait_ge(done, i * 2 + (u + 3))
                        dve.tensor_tensor(kv_all[:, i * 2 + u, :], ps[:, u, :], b[:, :, :].rearrange("p m o -> p (m o)"), ALU.add).then_inc(added, 1)
                dve.wait_ge(added, TILES + 2)


def phase_rms(core, name, q_all, kv_all, rq, rk, eps):
    nc = core.nc
    summed, based, powed = (core.sem(name + k) for k in ("_s", "_b", "_p"))
    with ExitStack() as ctx:
        junk = core.sb(ctx, name + "_junk", [P, 2, DIM], F32)
        ss = core.sb(ctx, name + "_ss", [P, 2, TILES], F32)
        base = core.sb(ctx, name + "_base", [P, 2, TILES], F32)
        with nc.Block() as block:
            @block.vector
            def _(dve):
                for t in range(TILES):
                    for m, src in ((0, q_all[:, t, :]), (1, kv_all[:, t, 0:DIM])):
                        if t:
                            dve.wait_ge(summed, 2 * t + m - 1)
                        dve.tensor_tensor_reduce(out=junk[:, m, :], in0=src, in1=src, scale=1.0, scalar=0.0, op0=ALU.mult,
                                                 op1=ALU.add, accum_out=ss[:, m, t:t + 1]).then_inc(summed, 1)
                dve.wait_ge(summed, 2 * TILES)
                dve.tensor_scalar(base[:, :, :], ss[:, :, :], 1.0 / DIM, eps, ALU.mult, ALU.add).then_inc(based, 1)

            @block.gpsimd
            def _(pool):
                pool.wait_ge(based, 1)
                pool.tensor_tensor(rq, base[:, 0, :], core.half[:, 0:TILES], ALU.pow).then_inc(powed, 1)
                pool.tensor_tensor(rk, base[:, 1, :], core.half[:, 0:TILES], ALU.pow).then_inc(powed, 1)
                pool.wait_ge(powed, 2)


def phase_cross(core, name, q_all, kv_all, rq, rk, gq, gk, wo, bo, gate):
    nc = core.nc
    H, W = 16, DIM // 16
    HP, HK = H // 2, H // KC
    n = name + "_"
    w_loaded, made, scaled_bias = (core.sem(n + k) for k in ("wl", "mk", "gb"))
    laid = core.sem(n + "la")
    normed, qk_turned, qk_copied, keys_ready, values_ready = (core.sem(n + k) for k in ("nm", "qt", "qc", "kr", "vr"))
    s_done, maxed, shifted, exped, summed, p_turned, p_copied, pv_done = (
        core.sem(n + k) for k in ("sd", "mx", "sf", "ex", "sm", "pt", "pc", "pv"))
    o_ready, o_turned, o_copied, out_done, added, part_added, den_ready = (
        core.sem(n + k) for k in ("or", "ot", "oc", "od", "ad", "pa", "dn"))
    with ExitStack() as ctx:
        sb, ps = core.sb, core.ps
        wos = sb(ctx, n + "wo", [P, KC, DIM], F32)
        gains = sb(ctx, n + "gains", [P, 3, DIM], F32)
        mask = sb(ctx, n + "mask", [P, HK], F32)
        qkn = sb(ctx, n + "qkn", [P, 2, 2, DIM], F32)
        qkT = sb(ctx, n + "qkT", [P, 2, 2, KC, P], F32)
        kbd = sb(ctx, n + "kbd", [P, 2, KC, 2, HK, SEQ], F32)
        vbd = sb(ctx, n + "vbd", [P, 2, 2, HP, 2, W], F32)
        prob = sb(ctx, n + "prob", [P, 2, H, SEQ], F32)
        pT = sb(ctx, n + "pT", [P, 2, HP, P], F32)
        mx = sb(ctx, n + "mx_sb", [P, H], F32)
        den = sb(ctx, n + "den", [P, H], F32)
        rden = sb(ctx, n + "rden", [P, 2, H], F32)
        o = sb(ctx, n + "o", [P, 2, DIM], F32)
        oT = sb(ctx, n + "oT", [P, 2, KC, P], F32)
        psT = ps(ctx, n + "psT", [P, 512])
        psS = ps(ctx, n + "psS", [P, 2, 512])
        psP = ps(ctx, n + "psP", [P, 2, 512])
        psO = ps(ctx, n + "psO", [P, 512])
        psQ = ps(ctx, n + "psQ", [P, 512])
        psX = ps(ctx, n + "psX", [P, 512])

        with nc.Block() as block:
            @block.sync
            def _(sp):
                sp.dma_start(wos[:, :, :], wo.rearrange("(k p) o -> p k o", p=P)).then_inc(w_loaded, 16)
                for m, v in enumerate((gq, gk, bo)):
                    sp.dma_start(gains[:, m, :], v.rearrange("(a n) -> a n", a=1).broadcast_to([P, DIM])).then_inc(w_loaded, 16)

            @block.gpsimd
            def _(pool):
                pool.memset(mask[:, :], 1.0).then_inc(made, 1)
                pool.memset(vbd[:, :, :, :, :, :], 0.0).then_inc(made, 1)
                pool.wait_ge(made, 2)
                pool.affine_select(out=mask[:, :], in_=mask[:, :], compare_op=ALU.is_ge, fill=0.0, base=0,
                                   pattern=[[-W, HK]], channel_multiplier=1).then_inc(made, 1)
                pool.wait_ge(made, 3)
                pool.affine_select(out=mask[:, :], in_=mask[:, :], compare_op=ALU.is_ge, fill=0.0, base=W - 1,
                                   pattern=[[W, HK]], channel_multiplier=-1).then_inc(made, 1)
                pool.wait_ge(made, 4)

                def step(s, v):
                    t, u = s + 2, v
                    if valid(t):
                        pool.wait_ge(qk_copied, t + 1)
                        wait_count(pool, s_done, t - 1)
                        for k in range(KC):
                            for b in range(2):
                                src = qkT[:, u, 1, k, SEQ * b:SEQ * b + SEQ].rearrange("p (a c) -> p a c", a=1).broadcast_to([P, HK, SEQ])
                                ins = pool.tensor_tensor(kbd[:, u, k, b, :, :], src,
                                                         mask[:, :].rearrange("p (h a) -> p h a", a=1).broadcast_to([P, HK, SEQ]), ALU.mult)
                        ins.then_inc(keys_ready, 1)
                    t, u = s + 1, (v + 1) % 2
                    if valid(t):
                        wait_count(pool, pv_done, t - 1)
                        for c, (b, hh) in enumerate(((0, 0), (1, 1), (0, 1), (1, 0))):
                            if c == 0 and valid(s + 2):
                                pool.wait_ge(keys_ready, s + 3)
                            if c:
                                pool.wait_ge(laid, t * 3 + c)
                            src = kv_all[SEQ * b:SEQ * b + SEQ, t, DIM:2 * DIM].rearrange("p (a h w) -> p a h w", h=2, w=W)[:, :, hh, :]
                            pool.tensor_copy(vbd[SEQ * hh:SEQ * hh + SEQ, u, b, :, hh, :], src).then_inc(laid if c < 3 else values_ready, 1)
                        pool.wait_ge(values_ready, t + 1)

                pipelined(pool, step, -2, TILES, 4, 2)

            @block.tensor
            def _(pe):
                pe.wait_ge(w_loaded, 64)

                def step(s, v):
                    t, u = s, v
                    if valid(t):
                        pe.wait_ge(exped, t + 1)
                        wait_count(pe, p_copied, t)
                        for a in range(HP):
                            ins = pe.transpose(psP[:, a // 4, a % 4 * P:(a % 4 + 1) * P],
                                               prob[:, u, 2 * a:2 * a + 2, :].rearrange("p h c -> p (h c)"), core.ident[:, :])
                        ins.then_inc(p_turned, 1)
                    t, u = s + 1, (v + 1) % 2
                    if valid(t):
                        pe.wait_ge(keys_ready, t + 1)
                        wait_count(pe, shifted, t)
                        for k in range(KC):
                            for b in range(2):
                                ins = pe.matmul(psS[SEQ * b:SEQ * b + SEQ, k, :], qkT[:, u, 0, k, SEQ * b:SEQ * b + SEQ],
                                                kbd[:, u, k, b, :, :], start=True, stop=True, tile_position=(0, SEQ * b))
                        ins.then_inc(s_done, 1)
                    t, u = s - 1, (v + 1) % 2
                    if valid(t):
                        pe.wait_ge(o_ready, t + 1)
                        wait_count(pe, o_copied, t)
                        for k in range(KC):
                            ins = pe.transpose(psQ[:, k * P:(k + 1) * P], o[:, u, k * P:(k + 1) * P], core.ident[:, :])
                        ins.then_inc(o_turned, 1)
                    t, u = s + 2, v
                    if valid(t):
                        pe.wait_ge(normed, t + 1)
                        wait_count(pe, qk_copied, t)
                        for m in range(2):
                            for k in range(KC):
                                at = (m * KC + k) * P
                                ins = pe.transpose(psT[:, at:at + P], qkn[:, u, m, k * P:(k + 1) * P], core.ident[:, :])
                        ins.then_inc(qk_turned, 1)
                    t, u = s, v
                    if valid(t):
                        pe.wait_ge(p_copied, t + 1)
                        pe.wait_ge(values_ready, t + 1)
                        wait_count(pe, o_ready, t)
                        for a in range(HP):
                            for b in range(2):
                                ins = pe.matmul(psO[SEQ * b:SEQ * b + SEQ, 2 * W * a:2 * W * (a + 1)], pT[:, u, a, SEQ * b:SEQ * b + SEQ],
                                                vbd[:, u, b, a, :, :], start=True, stop=True, tile_position=(0, SEQ * b))
                        ins.then_inc(pv_done, 1)
                    t, u = s - 1, (v + 1) % 2
                    if valid(t):
                        pe.wait_ge(o_copied, t + 1)
                        wait_count(pe, part_added, t)
                        for k in range(KC):
                            ins = pe.matmul(psX[:, 0:DIM], oT[:, u, k, :], wos[:, k, :], start=(k == 0), stop=(k == KC - 1))
                        ins.then_inc(out_done, 1)

                pipelined(pe, step, -2, TILES + 1, 4, 3)

            @block.scalar
            def _(act):
                def step(s, v):
                    t, u = s, v
                    if valid(t):
                        act.wait_ge(p_turned, t + 1)
                        wait_count(act, pv_done, t - 1)
                        act.activation(pT[:, u, :, :], psP[:, :, :].rearrange("p b (a c) -> p (b a) c", c=P), ACT.Copy).then_inc(p_copied, 1)
                    t, u = s + 1, (v + 1) % 2
                    if valid(t):
                        act.wait_ge(shifted, t + 1)
                        act.activation(prob[:, u, :, :], prob[:, u, :, :], ACT.Exp, scale=W ** -0.5).then_inc(exped, 1)
                    t, u = s - 1, (v + 1) % 2
                    if valid(t):
                        act.wait_ge(o_turned, t + 1)
                        wait_count(act, out_done, t - 1)
                        act.activation(oT[:, u, :, :], psQ[:, 0:KC * P].rearrange("p (k c) -> p k c", k=KC), ACT.Copy).then_inc(o_copied, 1)
                    t, u = s + 2, v
                    if valid(t):
                        act.wait_ge(qk_turned, t + 1)
                        wait_count(act, s_done, t - 1)
                        wait_count(act, keys_ready, t - 1)
                        act.activation(qkT[:, u, :, :, :], psT[:, :].rearrange("p (m k c) -> p m k c", m=2, k=KC), ACT.Copy).then_inc(qk_copied, 1)

                pipelined(act, step, -2, TILES + 1, 4, 3)

            @block.vector
            def _(dve):
                dve.wait_ge(w_loaded, 64)
                dve.tensor_scalar(gains[:, 2, :], gains[:, 2, :], gate, None, ALU.mult).then_inc(scaled_bias, 1)
                dve.wait_ge(scaled_bias, 1)

                def normalise(t, u):
                    if valid(t):
                        wait_count(dve, qk_turned, t - 1)
                        dve.scalar_tensor_tensor(out=qkn[:, u, 0, :], in0=q_all[:, t, :], scalar=rq[:, bass.ds(t, 1)], in1=gains[:, 0, :],
                                                 op0=ALU.mult, op1=ALU.mult)
                        dve.scalar_tensor_tensor(out=qkn[:, u, 1, :], in0=kv_all[:, t, 0:DIM], scalar=rk[:, bass.ds(t, 1)], in1=gains[:, 1, :],
                                                 op0=ALU.mult, op1=ALU.mult).then_inc(normed, 1)

                def step(s, v):
                    t, u = s + 1, (v + 1) % 2
                    if valid(t):
                        dve.wait_ge(s_done, t + 1)
                        wait_count(dve, shifted, t)
                        scores = psS[:, :, :].rearrange("p k (h c) -> p (k h) c", c=SEQ)
                        dve.tensor_reduce(mx[:, :], scores, AX_X, ALU.max).then_inc(maxed, 1)
                        dve.wait_ge(maxed, t + 1)
                        wait_count(dve, p_turned, t - 1)
                        dve.tensor_tensor(prob[:, u, :, :], scores, mx[:, :].rearrange("p (h a) -> p h a", a=1).broadcast_to([P, H, SEQ]),
                                          ALU.subtract).then_inc(shifted, 1)
                    normalise(s + 3, (v + 1) % 2)
                    t, u = s + 1, (v + 1) % 2
                    if valid(t):
                        dve.wait_ge(exped, t + 1)
                        dve.tensor_reduce(den[:, :], prob[:, u, :, :], AX_X, ALU.add).then_inc(summed, 1)
                        dve.wait_ge(summed, t + 1)
                        dve.reciprocal(rden[:, u, :], den[:, :]).then_inc(den_ready, 1)
                        dve.wait_ge(den_ready, t + 1)
                    t, u = s, v
                    if valid(t):
                        dve.wait_ge(pv_done, t + 1)
                        wait_count(dve, o_turned, t - 1)
                        dve.tensor_tensor(o[:, u, :].rearrange("p (h w) -> p h w", w=W), psO[:, 0:DIM].rearrange("p (h w) -> p h w", w=W),
                                          rden[:, u, :].rearrange("p (h a) -> p h a", a=1).broadcast_to([P, H, W]), ALU.mult).then_inc(o_ready, 1)
                        dve.tensor_tensor(core.xs[:, t, :], core.xs[:, t, :], gains[:, 2, :], ALU.add).then_inc(added, 1)
                    t, u = s - 1, (v + 1) % 2
                    if valid(t):
                        dve.wait_ge(out_done, t + 1)
                        dve.wait_ge(added, t + 1)
                        dve.scalar_tensor_tensor(out=core.xs[:, t, :], in0=psX[:, 0:DIM], scalar=gate, in1=core.xs[:, t, :],
                                                 op0=ALU.mult, op1=ALU.add).then_inc(part_added, 1)

                normalise(0, 0)
                normalise(1, 1)
                pipelined(dve, step, -1, TILES + 1, 3, 5)
                dve.wait_ge(part_added, TILES)


F1 = 704
F1C = (F1 + P - 1) // P


def phase_bit_weights(core, gu_dram, down_dram, guT, downT, mu):
    nc = core.nc
    loaded, summed, total, chain, cut, turned, copied, made = (core.sem("bw_" + k) for k in ("l", "s", "t", "c", "q", "tr", "cp", "mk"))
    RG = 2 * F1 // P
    with ExitStack() as ctx:
        wg = core.sb(ctx, "bw_wg", [P, RG, DIM], F32)
        wd = core.sb(ctx, "bw_wd", [P, KC, F1], F32)
        junk = core.sb(ctx, "bw_junk", [P, RG, DIM], F32)
        tg = core.sb(ctx, "bw_tg", [P, RG, DIM], BF16)
        td = core.sb(ctx, "bw_td", [P, KC, F1], BF16)
        part = core.sb(ctx, "bw_part", [P, 2], F32)
        inv = core.sb(ctx, "bw_inv", [P, 2], F32)
        ones = core.sb(ctx, "bw_ones", [P, P], F32)
        ident16 = core.sb(ctx, "bw_id", [P, P], BF16)
        psA = core.ps(ctx, "bw_psA", [P, 512])
        psB = [core.ps(ctx, f"bw_psB{i}", [P, KC * P], BF16) for i in range(2)]
        with nc.Block() as block:
            @block.sync
            def _(sp):
                sp.dma_start(wg[:, :, :], gu_dram.rearrange("(o p) i -> p o i", p=P)).then_inc(loaded, 16)
                sp.dma_start(wd[:, :, :], down_dram.rearrange("(o p) i -> p o i", p=P)).then_inc(loaded, 16)

            @block.gpsimd
            def _(pool):
                pool.memset(ones[:, :], 1.0).then_inc(made, 1)
                pool.tensor_copy(ident16[:, :], core.ident[:, :]).then_inc(made, 1)

            @block.scalar
            def _(act):
                act.wait_ge(loaded, 32)
                act.activation(junk[:, :, :], wg[:, :, :], ACT.Abs, accum_out=part[:, 0:1]).then_inc(summed, 1)
                act.wait_ge(summed, 1)
                act.activation(junk[:, 0:KC * F1 // DIM + 1, :].rearrange("p o i -> p (o i)")[:, 0:KC * F1],
                               wd[:, :, :].rearrange("p o i -> p (o i)"), ACT.Abs, accum_out=part[:, 1:2]).then_inc(summed, 1)

            def turns():
                for o in range(RG):
                    yield [(guT[:, k, o * P:(o + 1) * P], tg[:, o, k * P:(k + 1) * P], P) for k in range(KC)]
                for c in range(F1C):
                    rows = min(P, F1 - c * P)
                    yield [(downT[0:rows, c, k * P:(k + 1) * P], td[:, k, c * P:c * P + rows], rows) for k in range(KC)]

            @block.tensor
            def _(pe):
                pe.wait_ge(summed, 2)
                pe.wait_ge(made, 2)
                pe.matmul(psA[:, 0:2], ones[:, :], part[:, :], start=True, stop=True).then_inc(total, 1)
                pe.wait_ge(cut, 2)
                for n, group in enumerate(turns()):
                    if n >= 2:
                        pe.wait_ge(copied, n - 1)
                    for k, (_, src, rows) in enumerate(group):
                        ins = pe.transpose(psB[n % 2][0:rows, k * P:(k + 1) * P], src, ident16[:, :])
                    ins.then_inc(turned, 1)

            @block.vector
            def _(dve):
                dve.wait_ge(total, 1)
                c = Chain(dve, chain)
                c.link(dve.tensor_scalar(mu[:, 0:1], psA[:, 0:1], 1.0 / (2 * F1 * DIM), 1e-5, ALU.mult, ALU.max))
                c.link(dve.tensor_scalar(mu[:, 1:2], psA[:, 1:2], 1.0 / (F1 * DIM), 1e-5, ALU.mult, ALU.max))
                c.link(dve.reciprocal(inv[:, :], mu[:, 0:2]))
                for m, (w, t) in enumerate(((wg, tg), (wd, td))):
                    c.link(dve.tensor_scalar(w[:, :, :], w[:, :, :], inv[:, m:m + 1], ROUND_MAGIC, ALU.mult, ALU.add))
                    c.link(dve.tensor_scalar(w[:, :, :], w[:, :, :], ROUND_MAGIC, 1.0, ALU.subtract, ALU.min))
                    dve.tensor_scalar(t[:, :, :], w[:, :, :], -1.0, None, ALU.max).then_inc(cut, 1)
                for n, group in enumerate(turns()):
                    dve.wait_ge(turned, n + 1)
                    for k, (dst, _, rows) in enumerate(group):
                        ins = dve.tensor_copy(dst, psB[n % 2][0:rows, k * P:(k + 1) * P])
                    ins.then_inc(copied, 1)
                dve.wait_ge(copied, RG + F1C)


def phase_bit_inputs(core, norm_w, qT_all, sg_all, mu):
    nc = core.nc
    G = 4
    loaded, based, powed, chain, quantised, turned, copied, made, maxed = (
        core.sem("bi_" + k) for k in ("l", "b", "p", "c", "q", "t", "cp", "mk", "mx"))
    with ExitStack() as ctx:
        wb = core.sb(ctx, "bi_w", [P, DIM], F32)
        rr = core.sb(ctx, "bi_rr", [P, TILES], F32)
        tmp = core.sb(ctx, "bi_tmp", [P, 2, TILES], F32)
        z = core.sb(ctx, "bi_z", [P, G, DIM], F32)
        za = core.sb(ctx, "bi_za", [P, G, DIM], F32)
        am = core.sb(ctx, "bi_am", [P, G], F32)
        s1 = core.sb(ctx, "bi_s1", [P, G], F32)
        q = core.sb(ctx, "bi_q", [P, G, DIM], BF16)
        ident16 = core.sb(ctx, "bi_id", [P, P], BF16)
        psT = core.ps(ctx, "bi_psT", [P, G * KC * P], BF16)
        with nc.Block() as block:
            @block.sync
            def _(sp):
                sp.dma_start(wb[:, :], norm_w.rearrange("(a n) -> a n", a=1).broadcast_to([P, DIM])).then_inc(loaded, 16)

            @block.gpsimd
            def _(pool):
                pool.tensor_copy(ident16[:, :], core.ident[:, :]).then_inc(made, 1)
                pool.wait_ge(based, 1)
                pool.tensor_tensor(tmp[:, 1, :], tmp[:, 0, :], core.half[:, 0:TILES], ALU.pow).then_inc(powed, 1)

            @block.tensor
            def _(pe):
                pe.wait_ge(made, 1)
                @looped(pe, TILES // G)
                def _(i):
                    pe.wait_ge(quantised, i + 1)
                    wait_count(pe, copied, i)
                    for g in range(G):
                        for k in range(KC):
                            at = (g * KC + k) * P
                            ins = pe.transpose(psT[:, at:at + P], q[:, g, k * P:(k + 1) * P], ident16[:, :])
                    ins.then_inc(turned, 1)

            @block.scalar
            def _(act):
                @looped(act, TILES // G)
                def _(i):
                    act.wait_ge(turned, i + 1)
                    act.activation(qT_all[:, bass.ds(i * G, G), :, :], psT[:, :].rearrange("p (g k c) -> p g k c", g=G, k=KC), ACT.Copy).then_inc(copied, 1)
                act.wait_ge(copied, TILES // G)

            @block.vector
            def _(dve):
                c = Chain(dve, chain)
                c.link(dve.tensor_tensor(tmp[:, 0, :], core.rstd[:, :], core.rstd[:, :], ALU.mult))
                c.link(dve.tensor_tensor(tmp[:, 0, :], tmp[:, 0, :], core.mv[:, :, 1], ALU.mult))
                dve.tensor_scalar(tmp[:, 0, :], tmp[:, 0, :], 1e-5, None, ALU.add).then_inc(based, 1)
                dve.wait_ge(powed, 1)
                c.link(dve.tensor_tensor(rr[:, :], tmp[:, 1, :], core.rstd[:, :], ALU.mult))
                dve.wait_ge(loaded, 16)
                @looped(dve, TILES // G)
                def _(i):
                    c2 = Chain(dve, chain, i, 7, base=3)
                    for g in range(G):
                        ins = dve.tensor_scalar(z[:, g, :], core.xs[:, i * G + g, :], core.mv[:, i * G + g, 0:1],
                                                rr[:, bass.ds(i * G + g, 1)], ALU.subtract, ALU.mult)
                    c2.link(ins)
                    c2.link(dve.tensor_tensor(z[:, :, :], z[:, :, :], wb[:, :].rearrange("p (a c) -> p a c", a=1).broadcast_to([P, G, DIM]), ALU.mult))
                    c2.link(dve.tensor_reduce(am[:, :], z[:, :, :], AX_X, ALU.max, apply_absolute_value=True))
                    c2.link(dve.tensor_scalar(am[:, :], am[:, :], 1e-5, 1.0 / 127.0, ALU.max, ALU.mult))
                    c2.link(dve.reciprocal(s1[:, :], am[:, :]))
                    for g in range(G):
                        ins = dve.tensor_scalar(z[:, g, :], z[:, g, :], s1[:, g:g + 1], ROUND_MAGIC, ALU.mult, ALU.add)
                    c2.link(ins)
                    wait_count(dve, turned, i)
                    dve.tensor_scalar(q[:, :, :], z[:, :, :], ROUND_MAGIC, None, ALU.subtract).then_inc(quantised, 1)
                    dve.wait_ge(quantised, i + 1)
                    c2.link(dve.tensor_scalar(sg_all[:, bass.ds(i * G, G)], am[:, :], mu[:, 0:1], None, ALU.mult))
                    c2.close()


def phase_bit_ffn(core, qT_all, sg_all, guT, downT, mu, gate):
    nc = core.nc
    n = "bf_"
    HALF = F1 // 2
    gu_done, relued, squared, u_read, maxed, quantised, turned, copied, down_done, added, chain, cubed, made = (
        core.sem(n + k) for k in ("gu", "re", "sq", "ur", "mx", "q", "t", "c", "d", "a", "ch", "cu", "mk"))
    with ExitStack() as ctx:
        rg = core.sb(ctx, n + "rg", [P, 2, HALF], F32)
        h = core.sb(ctx, n + "h", [P, 2, 2, HALF], F32)
        q = core.sb(ctx, n + "q", [P, 2, F1], BF16)
        hT = core.sb(ctx, n + "hT", [P, 2, F1C, P], BF16)
        sg3 = core.sb(ctx, n + "sg3", [P, TILES], F32)
        isg3 = core.sb(ctx, n + "isg3", [P, TILES], F32)
        sm = core.sb(ctx, n + "sm", [P, 2, 4], F32)
        ident16 = core.sb(ctx, n + "id", [P, P], BF16)
        psG = core.ps(ctx, n + "psG", [P, 4, 512])
        psT = core.ps(ctx, n + "psT", [P, 1024], BF16)
        psD = core.ps(ctx, n + "psD", [P, 512])
        with nc.Block() as block:
            @block.gpsimd
            def _(pool):
                pool.tensor_copy(ident16[:, :], core.ident[:, :]).then_inc(made, 1)

            @block.tensor
            def _(pe):
                pe.wait_ge(made, 1)

                def step(s, v):
                    t, u = s + 1, (v + 1) % 2
                    if valid(t):
                        wait_count(pe, relued, t)
                        for b in range(4):
                            if b == 2:
                                wait_count(pe, u_read, t)
                            for k in range(KC):
                                ins = pe.matmul(psG[:, b, 0:HALF], qT_all[:, t, k, :], guT[:, k, b * HALF:(b + 1) * HALF],
                                                start=(k == 0), stop=(k == KC - 1))
                            if b % 2:
                                ins.then_inc(gu_done, 1)
                    t, u = s, v
                    if valid(t):
                        pe.wait_ge(quantised, t + 1)
                        wait_count(pe, copied, t * 2)
                        for c in range(F1C):
                            rows = min(P, F1 - c * P)
                            ins = pe.transpose(psT[0:rows, c * P:(c + 1) * P], q[:, u, c * P:c * P + rows], ident16[:, :])
                        ins.then_inc(turned, 1)
                        pe.wait_ge(copied, t * 2 + 2)
                        wait_count(pe, added, t)
                        for c in range(F1C):
                            rows = min(P, F1 - c * P)
                            ins = pe.matmul(psD[:, 0:DIM], hT[0:rows, u, c, :], downT[0:rows, c, :], start=(c == 0), stop=(c == F1C - 1))
                        ins.then_inc(down_done, 1)

                pipelined(pe, step, -1, TILES, 3, 2)

            @block.scalar
            def _(act):
                def step(s, v):
                    t, u = s + 1, (v + 1) % 2
                    if valid(t):
                        act.wait_ge(gu_done, t * 2 + 1)
                        wait_count(act, squared, t)
                        act.activation(rg[:, :, :], psG[:, 0:2, 0:HALF], ACT.Relu).then_inc(relued, 1)
                        act.wait_ge(relued, t + 1)
                        wait_count(act, quantised, t - 1)
                        act.activation(h[:, u, :, :], rg[:, :, :], ACT.Square).then_inc(squared, 1)
                    t, u = s, v
                    if valid(t):
                        act.wait_ge(turned, t + 1)
                        wait_count(act, down_done, t - 1)
                        act.activation(hT[:, u, 0:F1C - 1, :], psT[:, 0:(F1C - 1) * P].rearrange("p (c d) -> p c d", d=P), ACT.Copy).then_inc(copied, 1)
                        act.activation(hT[0:64, u, F1C - 1, :], psT[0:64, (F1C - 1) * P:F1C * P], ACT.Copy).then_inc(copied, 1)

                pipelined(act, step, -1, TILES, 3, 2)

            @block.vector
            def _(dve):
                c = Chain(dve, cubed)
                c.link(dve.tensor_tensor(sg3[:, :], sg_all[:, :], sg_all[:, :], ALU.mult))
                c.link(dve.tensor_tensor(sg3[:, :], sg3[:, :], sg_all[:, :], ALU.mult))

                def step(s, v):
                    t, u = s, v
                    if valid(t):
                        PER = 6
                        k0 = t * PER

                        def link(ins, k):
                            ins.then_inc(chain, 1)
                            dve.wait_ge(chain, k0 + k)

                        dve.wait_ge(gu_done, t * 2 + 2)
                        dve.wait_ge(squared, t + 1)
                        dve.tensor_tensor(h[:, u, :, :], psG[:, 2:4, 0:HALF], h[:, u, :, :], ALU.mult).then_inc(u_read, 1)
                        dve.wait_ge(u_read, t + 1)
                        link(dve.tensor_reduce(sm[:, u, 0:1], h[:, u, :, :].rearrange("p a c -> p (a c)"), AX_X, ALU.max, apply_absolute_value=True), 1)
                        link(dve.tensor_scalar(sm[:, u, 1:2], sm[:, u, 0:1], sg3[:, bass.ds(t, 1)], 1e-5, ALU.mult, ALU.max), 2)
                        link(dve.tensor_scalar(sm[:, u, 1:2], sm[:, u, 1:2], 1.0 / 127.0, None, ALU.mult), 3)
                        link(dve.reciprocal(sm[:, u, 2:3], sm[:, u, 1:2]), 4)
                        link(dve.tensor_scalar(sm[:, u, 2:3], sm[:, u, 2:3], sg3[:, bass.ds(t, 1)], None, ALU.mult), 5)
                        link(dve.tensor_scalar(h[:, u, :, :], h[:, u, :, :], sm[:, u, 2:3], ROUND_MAGIC, ALU.mult, ALU.add), 6)
                        wait_count(dve, turned, t - 1)
                        dve.tensor_scalar(q[:, u, :], h[:, u, :, :].rearrange("p a c -> p (a c)"), ROUND_MAGIC, None, ALU.subtract).then_inc(quantised, 1)
                        dve.tensor_scalar(sm[:, u, 3:4], sm[:, u, 1:2], mu[:, 1:2], gate, ALU.mult, ALU.mult).then_inc(maxed, 1)
                    t, u = s - 1, (v + 1) % 2
                    if valid(t):
                        dve.wait_ge(down_done, t + 1)
                        dve.wait_ge(maxed, t + 1)
                        dve.scalar_tensor_tensor(out=core.xs[:, t, :], in0=psD[:, 0:DIM], scalar=sm[:, u, 3:4], in1=core.xs[:, t, :],
                                                 op0=ALU.mult, op1=ALU.add).then_inc(added, 1)

                pipelined(dve, step, 0, TILES + 1, 2, 1)
                dve.wait_ge(added, TILES)


def phase_mix(core, name, amplitudes, expert_scale, mix):
    nc = core.nc
    E, K = 128, 8
    loaded, chain = core.sem(name + "_l"), core.sem(name + "_c")
    with ExitStack() as ctx:
        a = core.sb(ctx, name + "_a", [E, K, 2], F32)
        es = core.sb(ctx, name + "_es", [E, 1], F32)
        p = core.sb(ctx, name + "_p", [E, K], F32)
        s = core.sb(ctx, name + "_s", [E, 1], F32)
        with nc.Block() as block:
            @block.sync
            def _(sp):
                sp.dma_start(a[:, :, :], amplitudes).then_inc(loaded, 16)
                sp.dma_start(es[:, :], expert_scale.rearrange("(e a) -> e a", a=1)).then_inc(loaded, 16)

            @block.vector
            def _(dve):
                dve.wait_ge(loaded, 32)
                c = Chain(dve, chain)
                c.link(dve.tensor_tensor(a[:, :, :], a[:, :, :], a[:, :, :], ALU.mult))
                c.link(dve.tensor_tensor(p[:, :], a[:, :, 0], a[:, :, 1], ALU.add))
                c.link(dve.tensor_reduce(s[:, :], p[:, :], AX_X, ALU.add))
                c.link(dve.tensor_scalar(s[:, :], s[:, :], 1e-8, None, ALU.add))
                c.link(dve.reciprocal(s[:, :], s[:, :]))
                c.link(dve.tensor_scalar(mix[:, :], p[:, :], s[:, 0:1], es[:, 0:1], ALU.mult, ALU.mult))


def phase_basis_ffn(core, yT_all, score_all, mix, w_gate, w_up, w_down, s_gate, s_up, s_down, gate):
    nc = core.nc
    K, I, E = 8, 128, 128
    n = "bs_"
    loaded = core.sem(n + "l")
    fetched = [core.sem(f"{n}f{u}") for u in range(2)]
    sc_ready, small_done, small_copied, c_done, c_ready = (core.sem(n + k) for k in ("scr", "sm", "smc", "cd", "cr"))
    g_done, u_done, s_done, tanhed, glued, mixed, m_turned, m_copied, down_done, added, chain, basised = (
        core.sem(n + k) for k in ("g", "u", "s", "th", "gl", "mx", "mt", "mc", "d", "a", "ch", "bb"))
    with ExitStack() as ctx:
        sb, ps = core.sb, core.ps
        wg = sb(ctx, n + "wg", [P, KC, K * I], F32)
        wu = sb(ctx, n + "wu", [P, KC, K * I], F32)
        ws = sb(ctx, n + "ws", [P, KC, 2, DIM], F32)
        wd = sb(ctx, n + "wd", [P, 1 + KC, DIM], F32)
        yT = sb(ctx, n + "yT", [P, 2, KC, P], F32)
        sc = sb(ctx, n + "sc", [P, 2, E], F32)
        scT = sb(ctx, n + "scT", [P, 2, E], F32)
        cf = sb(ctx, n + "cf", [P, 2, K], F32)
        th = sb(ctx, n + "th", [P, K * I], F32)
        ths = sb(ctx, n + "ths", [P, DIM], F32)
        b = sb(ctx, n + "b", [P, K, I], F32)
        m = sb(ctx, n + "m", [P, 2, 3, P], F32)
        mT = sb(ctx, n + "mT", [P, 2, 3, P], F32)
        psG = ps(ctx, n + "psG", [P, 2, 512])
        psU = ps(ctx, n + "psU", [P, 2, 512])
        psS = ps(ctx, n + "psS", [P, 512])
        psT = ps(ctx, n + "psT", [P, 512])
        psO = ps(ctx, n + "psO", [P, 512])
        psC = ps(ctx, n + "psC", [P, 512])
        with nc.Block() as block:
            @block.sync
            def _(sp):
                for dst, src in ((wg[:, :, :], w_gate), (wu[:, :, :], w_up), (ws[:, :, 0, :], s_gate), (ws[:, :, 1, :], s_up),
                                 (wd[:, 1:3, :], s_down)):
                    sp.dma_start(dst, src.rearrange("(k p) o -> p k o", p=P)).then_inc(loaded, 16)
                sp.dma_start(wd[:, 0, :], w_down).then_inc(loaded, 16)

                def step(s, v):
                    wait_count(sp, u_done, s - 1)
                    sp.dma_start(yT[:, v, :, :].rearrange("p k c -> p (k c)"), yT_all[s]).then_inc(fetched[v], 16)

                pipelined(sp, step, 0, TILES, 2, 0)

            @block.gpsimd
            def _(pool):
                def step(s, v):
                    wait_count(pool, small_done, s - 1)
                    pool.tensor_copy(sc[:, v, :], score_all[:, s, :]).then_inc(sc_ready, 1)

                pipelined(pool, step, 0, TILES, 2, 0)

            @block.tensor
            def _(pe):
                pe.wait_ge(loaded, 96)

                def step(s, v, half):
                    t, u = s, v
                    if valid(t):
                        pe.wait_ge(fetched[u], half * 16 + 16)
                        wait_count(pe, glued, t)
                        for c in range(2):
                            for k in range(KC):
                                ins = pe.matmul(psG[:, c, :], yT[:, u, k, :], wg[:, k, c * 512:(c + 1) * 512], start=(k == 0), stop=(k == KC - 1))
                        ins.then_inc(g_done, 1)
                        pe.wait_ge(sc_ready, t + 1)
                        wait_count(pe, c_ready, t)
                        pe.transpose(psC[:, 0:E], sc[:, u, :], core.ident[:, :]).then_inc(small_done, 1)
                    t, u = s - 1, (v + 1) % 2
                    if valid(t):
                        pe.wait_ge(mixed, t * 2 + 2)
                        wait_count(pe, m_copied, t)
                        for k in range(3):
                            ins = pe.transpose(psT[:, k * P:(k + 1) * P], m[:, u, k, :], core.ident[:, :])
                        ins.then_inc(m_turned, 1)
                    t, u = s, v
                    if valid(t):
                        wait_count(pe, mixed, t * 2)
                        for k in range(KC):
                            ins = pe.matmul(psS[:, :], yT[:, u, k, :], ws[:, k, :, :], start=(k == 0), stop=(k == KC - 1))
                        ins.then_inc(s_done, 1)
                        wait_count(pe, basised, t)
                        for c in range(2):
                            for k in range(KC):
                                ins = pe.matmul(psU[:, c, :], yT[:, u, k, :], wu[:, k, c * 512:(c + 1) * 512], start=(k == 0), stop=(k == KC - 1))
                        ins.then_inc(u_done, 1)
                        pe.wait_ge(small_copied, t + 1)
                        pe.matmul(psC[:, 256:256 + K], scT[:, u, :], mix[:, :], start=True, stop=True).then_inc(c_done, 1)
                    t, u = s - 1, (v + 1) % 2
                    if valid(t):
                        pe.wait_ge(m_copied, t + 1)
                        wait_count(pe, added, t)
                        for k in range(3):
                            ins = pe.matmul(psO[:, 0:DIM], mT[:, u, k, :], wd[:, k, :], start=(k == 0), stop=(k == 2))
                        ins.then_inc(down_done, 1)

                for s in range(2):
                    step(s, s, 0)
                with pe.Fori(1, TILES // 2) as j:
                    for v in range(2):
                        step(j * 2 + v, v, j)
                step(TILES, 0, 0)

            @block.scalar
            def _(act):
                def step(s, v):
                    t, u = s, v
                    if valid(t):
                        act.wait_ge(g_done, t + 1)
                        wait_count(act, glued, t)
                        act.activation(th[:, :], psG[:, :, :].rearrange("p b c -> p (b c)"), ACT.Tanh, scale=0.5).then_inc(tanhed, 1)
                        act.wait_ge(small_done, t + 1)
                        wait_count(act, c_done, t - 1)
                        act.activation(scT[:, u, :], psC[:, 0:E], ACT.Copy).then_inc(small_copied, 1)
                    t, u = s - 1, (v + 1) % 2
                    if valid(t):
                        act.wait_ge(m_turned, t + 1)
                        wait_count(act, down_done, t - 1)
                        act.activation(mT[:, u, :, :], psT[:, 0:3 * P].rearrange("p (k c) -> p k c", c=P), ACT.Copy).then_inc(m_copied, 1)
                    t, u = s, v
                    if valid(t):
                        act.wait_ge(s_done, t + 1)
                        act.activation(ths[:, :], psS[:, 0:DIM], ACT.Tanh, scale=0.5).then_inc(tanhed, 1)

                pipelined(act, step, 0, TILES + 1, 2, 1)

            @block.vector
            def _(dve):
                dve.wait_ge(loaded, 96)

                def step(s, v):
                    t, u = s, v
                    if valid(t):
                        def link(ins, k):
                            ins.then_inc(chain, 1)
                            dve.wait_ge(chain, t * 2 + k)

                        dve.wait_ge(tanhed, t * 2 + 1)
                        dve.wait_ge(g_done, t + 1)
                        wait_count(dve, mixed, t * 2)
                        dve.scalar_tensor_tensor(out=b[:, :, :].rearrange("p k i -> p (k i)"), in0=th[:, :], scalar=1.0,
                                                 in1=psG[:, :, :].rearrange("p b c -> p (b c)"), op0=ALU.add, op1=ALU.mult).then_inc(glued, 1)
                        dve.wait_ge(tanhed, t * 2 + 2)
                        link(dve.scalar_tensor_tensor(out=ths[:, :], in0=ths[:, :], scalar=1.0, in1=psS[:, 0:DIM], op0=ALU.add, op1=ALU.mult), 1)
                        wait_count(dve, m_turned, t - 1)
                        dve.scalar_tensor_tensor(out=m[:, u, 1:3, :].rearrange("p k c -> p (k c)"), in0=psS[:, DIM:2 * DIM], scalar=0.5, in1=ths[:, :],
                                                 op0=ALU.mult, op1=ALU.mult).then_inc(mixed, 1)
                    t, u = s - 1, (v + 1) % 2
                    if valid(t):
                        dve.wait_ge(down_done, t + 1)
                        dve.scalar_tensor_tensor(out=core.xs[:, t, :], in0=psO[:, 0:DIM], scalar=gate, in1=core.xs[:, t, :],
                                                 op0=ALU.mult, op1=ALU.add).then_inc(added, 1)
                    t, u = s, v
                    if valid(t):
                        dve.wait_ge(u_done, t + 1)
                        dve.wait_ge(glued, t + 1)
                        dve.scalar_tensor_tensor(out=b[:, :, :].rearrange("p k i -> p (k i)"), in0=psU[:, :, :].rearrange("p b c -> p (b c)"), scalar=0.5,
                                                 in1=b[:, :, :].rearrange("p k i -> p (k i)"), op0=ALU.mult, op1=ALU.mult).then_inc(basised, 1)
                        dve.wait_ge(c_done, t + 1)
                        dve.tensor_copy(cf[:, u, :], psC[:, 256:256 + K]).then_inc(c_ready, 1)
                        dve.wait_ge(c_ready, t + 1)
                        dve.wait_ge(basised, t + 1)
                        link(dve.tensor_tensor(b[:, :, :], b[:, :, :], cf[:, u, :].rearrange("p (k a) -> p k a", a=1).broadcast_to([P, K, I]), ALU.mult), 2)
                        dve.tensor_reduce(m[:, u, 0, :], b[:, :, :].rearrange("p k i -> p i k"), AX_X, ALU.add).then_inc(mixed, 1)

                pipelined(dve, step, 0, TILES + 1, 2, 1)
                dve.wait_ge(added, TILES)


def flamingo_decoder(nc, a, out):
    def dram(name, shape, dt=F32):
        return nc.dram_tensor(name, shape, dt, kind="Internal").ap()

    ctx_tiles = a["ctx_2048"].rearrange("b s d -> (b s) d").rearrange("(t p) d -> t p d", p=P)
    ctxT = dram("ctxT", [TILES, P, DIM])
    vt = dram("vt", [TILES, P, KC * 2 * HEADS * (HD + 1)])
    yT = dram("yT", [TILES, P, DIM])
    q_aug = dram("q_aug", [TILES // GROUP, 2, ROWS, PAIRS, GROUP * DIM], BF16)
    k_aug = dram("k_aug", [TILES // GROUP, 2, ROWS, PAIRS, GROUP * DIM], BF16)
    with ExitStack() as ctx:
        core = Core(nc, ctx)

        def x_gate(layer):
            return core.gates[:, layer:layer + 1]

        def f_gate(layer):
            return core.gates[:, 4 + layer:5 + layer]

        phase_setup(core, a["x"], a["g_xattn"], a["g_ffn"])
        phase_context(core, ctx_tiles, ctxT, vt)

        phase_norms(core, "n0")
        phase_split(core, "k0", ctx_tiles, k_aug, K_SLOTS, False)
        phase_split(core, "q0", None, q_aug, Q_SLOTS, False)
        phase_attend(core, "a0", q_aug, k_aug, vt, x_gate(0), float(HD) ** -0.5, True)
        core.clear_semaphores()
        phase_norms(core, "n1")
        with ExitStack() as c:
            score = core.sb(c, "score0", [P, TILES, 16], F32)
            with ExitStack() as c2:
                logits = core.sb(c2, "logits0", [P, TILES, 16], F32)
                phase_logits(core, "l0", 16, yT, logits, router_rows=a["L0_ffn_router_weight"], router_b=a["L0_ffn_router_bias"])
                phase_topk(core, "t0", 16, 4, logits, score, f_gate(0), "top")
            phase_moe0(core, yT, score, a["L0_ffn_gate_up_proj"], a["L0_ffn_gate_up_proj_bias"],
                       a["L0_ffn_down_proj"], a["L0_ffn_down_proj_bias"])

        core.clear_semaphores()
        phase_norms(core, "n2")
        phase_split(core, "k1", ctx_tiles, k_aug, K_SLOTS, True)
        phase_split(core, "q1", None, q_aug, Q_SLOTS, True)
        phase_attend(core, "a1", q_aug, k_aug, vt, x_gate(1), 5.0, False)
        core.clear_semaphores()
        phase_norms(core, "n3")
        with ExitStack() as c:
            guT = core.sb(c, "guT", [P, KC, 2 * F1], BF16)
            downT = core.sb(c, "downT", [P, F1C, DIM], BF16)
            mu = core.sb(c, "mu", [P, 2], F32)
            qT = core.sb(c, "qT", [P, TILES, KC, P], BF16)
            sg = core.sb(c, "sg", [P, TILES], F32)
            phase_bit_weights(core, a["L1_ffn_w_gate_up"], a["L1_ffn_w_down"], guT, downT, mu)
            phase_bit_inputs(core, a["L1_ffn_norm_weight"], qT, sg, mu)
            phase_bit_ffn(core, qT, sg, guT, downT, mu, f_gate(1))

        def cross(layer, wq, wk, wv, wo, bq, bk, bv, bo, gq, gk):
            n = str(layer)
            with ExitStack() as c:
                q_all = core.sb(c, "q_all" + n, [P, TILES, DIM], F32)
                kv_all = core.sb(c, "kv_all" + n, [P, TILES, 2 * DIM], F32)
                rq = core.sb(c, "rq" + n, [P, TILES], F32)
                rk = core.sb(c, "rk" + n, [P, TILES], F32)
                phase_logits(core, "cq" + n, DIM, yT, q_all, router_cols=wq, router_b=bq)
                phase_keys_values(core, "kv" + n, ctxT, kv_all, wk, wv, bk, bv)
                phase_rms(core, "rm" + n, q_all, kv_all, rq[:, :], rk[:, :], 1e-6)
                phase_cross(core, "cr" + n, q_all, kv_all, rq, rk, gq, gk, wo, bo, x_gate(layer))

        core.clear_semaphores()
        phase_norms(core, "n4")
        cross(2, *(a["L2_xattn_" + k] for k in ("Wq", "Wk_img", "Wv_img", "Wo", "bq", "bk_img", "bv_img", "bo", "gq", "gk_img")))
        core.clear_semaphores()
        phase_norms(core, "n5")
        with ExitStack() as c:
            score = core.sb(c, "score2", [P, TILES, 128], F32)
            mix = core.sb(c, "mix", [P, 8], F32)
            with ExitStack() as c2:
                logits = core.sb(c2, "logits2", [P, TILES, 128], F32)
                phase_logits(core, "l2", 128, yT, logits, router_cols=a["L2_ffn_w_router"])
                phase_topk(core, "t2", 128, 4, logits, score, 1.0, "eps")
            phase_mix(core, "mx", a["L2_ffn_amplitudes"], a["L2_ffn_expert_scale"], mix)
            phase_basis_ffn(core, yT, score, mix, *(a["L2_ffn_" + k] for k in (
                "w_gate", "w_up", "w_down", "shared_w_gate", "shared_w_up", "shared_w_down")), f_gate(2))

        turned = [dram(f"turned{k}", [DIM, DIM]) for k in range(4)]
        core.clear_semaphores()
        phase_norms(core, "n6")
        phase_turn_weights(core, "tw", list(zip((a["L3_xattn_" + k] for k in ("w_q", "w_k_img", "w_v_img", "w_o")), turned)))
        cross(3, *turned, *(a["L3_xattn_" + k] for k in ("b_q", "b_k_img", "b_v_img", "b_o", "g_q", "g_k_img")))
        core.clear_semaphores()
        phase_norms(core, "n7")
        with ExitStack() as c:
            score = core.sb(c, "score3", [P, TILES, 8], F32)
            with ExitStack() as c2:
                logits = core.sb(c2, "logits3", [P, TILES, 8], F32)
                phase_logits(core, "l3", 8, yT, logits, router_cols=a["L3_ffn_Wg"])
                phase_topk(core, "t3", 8, 2, logits, score, f_gate(3), "all", capacity=CAPACITY)
            phase_moe3(core, yT, score, a["L3_ffn_w1"], a["L3_ffn_w2"])

        core.clear_semaphores()
        phase_store(core, out)


_INS = ['x', 'ctx_2048', 'g_xattn', 'g_ffn', 'L0_ffn_router_weight', 'L0_ffn_router_bias',
        'L0_ffn_gate_up_proj', 'L0_ffn_gate_up_proj_bias', 'L0_ffn_down_proj', 'L0_ffn_down_proj_bias',
        'L1_ffn_w_gate_up', 'L1_ffn_w_down', 'L1_ffn_norm_weight',
        'L2_xattn_Wq', 'L2_xattn_bq', 'L2_xattn_gq', 'L2_xattn_Wk_img', 'L2_xattn_bk_img', 'L2_xattn_gk_img',
        'L2_xattn_Wv_img', 'L2_xattn_bv_img', 'L2_xattn_Wo', 'L2_xattn_bo',
        'L2_ffn_w_router', 'L2_ffn_w_gate', 'L2_ffn_w_up', 'L2_ffn_w_down', 'L2_ffn_amplitudes',
        'L2_ffn_expert_scale', 'L2_ffn_shared_w_gate', 'L2_ffn_shared_w_up', 'L2_ffn_shared_w_down',
        'L3_xattn_w_q', 'L3_xattn_b_q', 'L3_xattn_w_k_img', 'L3_xattn_b_k_img', 'L3_xattn_w_v_img',
        'L3_xattn_b_v_img', 'L3_xattn_w_o', 'L3_xattn_b_o', 'L3_xattn_g_q', 'L3_xattn_g_k_img',
        'L3_ffn_Wg', 'L3_ffn_w1', 'L3_ffn_w2']


def kernel(**inputs):
    import numpy as _np
    import concourse.bacc as _bacc
    from concourse import mybir as _mybir
    from concourse.bass_utils import run_bass_kernel_spmd as _run

    nc = _bacc.Bacc("TRN2", target_bir_lowering=False, num_devices=1)
    arrays, aps = {}, {}
    for name in _INS:
        v = _np.ascontiguousarray(inputs[name])
        arrays[f"in_{name}_dram"] = v
        aps[name] = nc.dram_tensor(f"in_{name}_dram", v.shape, _mybir.dt.from_np(v.dtype), kind="ExternalInput").ap()
    out = nc.dram_tensor("out_0_dram", (BATCH, SEQ, DIM), _mybir.dt.float32, kind="ExternalOutput").ap()
    flamingo_decoder(nc, aps, out)
    r = _run(nc, [arrays], core_ids=[0])
    return r.results[0]["out_0_dram"]
```

```python
from contextlib import ExitStack

import concourse.bass as bass
from concourse import mybir

F32 = mybir.dt.float32
BF16 = mybir.dt.bfloat16
U32 = mybir.dt.uint32
I32 = mybir.dt.int32
ALU = mybir.AluOpType
ACT = mybir.ActivationFunctionType
AX_X = mybir.AxisListType.X

P = 128
BATCH, SEQ, DIM = 64, 64, 256
TILES = BATCH * SEQ // P
KC = DIM // P
LN_EPS = 1e-5
PIECES = 3
ROUND_MAGIC = 1.5 * 2.0 ** 23
CAPACITY = 1280

T0 = TILES * 4 + 16
D0 = T0 * P
ZERO_DMAS = 6


def wait_count(eng, sem, value):
    if not isinstance(value, int) or value > 0:
        eng.wait_ge(sem, value)


def looped(eng, n):
    def run(step):
        step(0)
        with eng.Fori(1, n) as i:
            step(i)
    return run


class Chain:

    def __init__(self, eng, sem, step=0, per=0, base=0):
        self.eng, self.sem, self.step, self.per, self.base, self.n = eng, sem, step, per, base, 0

    def link(self, ins):
        self.n += 1
        ins.then_inc(self.sem, 1)
        self.eng.wait_ge(self.sem, self.step * self.per + (self.base + self.n))

    def close(self):
        assert self.n == self.per, f"{self.n} links, not {self.per}"


class Core:

    def __init__(self, nc, ctx):
        self.nc, self.ctx, self.sems, self.used = nc, ctx, ExitStack(), []
        sb = self.sb
        self.xs = sb(ctx, "xs", [P, TILES, DIM], F32)
        self.ident = sb(ctx, "ident", [P, P], F32)
        self.gates = sb(ctx, "gates", [P, 8], F32)
        self.mv = sb(ctx, "mv", [P, TILES, 2], F32)
        self.rstd = sb(ctx, "rstd", [P, TILES], F32)
        self.zeros = sb(ctx, "zeros", [P, DIM], F32)
        self.rows_zeroed = self.lasting_sem("rows_zeroed")
        self.half = sb(ctx, "half", [P, 64], F32)

    def sb(self, ctx, name, shape, dt):
        return ctx.enter_context(self.nc.sbuf_tensor(name, shape, dt))

    def ps(self, ctx, name, shape, dt=F32):
        return ctx.enter_context(self.nc.psum_tensor(name, shape, dt))

    def sem(self, name):
        handle = self.sems.enter_context(self.nc.semaphore(name))
        self.used.append(handle.num)
        return handle

    def lasting_sem(self, name):
        return self.ctx.enter_context(self.nc.semaphore(name))

    def clear_semaphores(self):
        nums = sorted(self.used)
        starts = [n for n in nums if n - 1 not in nums]
        ends = [n + 1 for n in nums if n + 1 not in nums]
        with self.nc.Block() as block:
            @block.gpsimd
            def _(pool):
                for lo, hi in zip(starts, ends):
                    pool.sem_clear(range(lo, hi))
        self.sems.close()
        self.used = []


def phase_setup(core, x, g_xattn, g_ffn, rows):
    nc = core.nc
    loaded, made, made0, tanhed = (core.sem(n) for n in ("x_loaded", "const_made", "const_zeroed", "gates_tanhed"))
    xv = x.rearrange("b s d -> (b s) d").rearrange("(t p) d -> p t d", p=P)
    with nc.Block() as block:
        @block.sync
        def _(sp):
            sp.dma_start(core.xs[:, :, :], xv).then_inc(loaded, 16)
            sp.dma_start(core.gates[:, 0:4], g_xattn.rearrange("(a n) -> a n", a=1).broadcast_to([P, 4])).then_inc(loaded, 16)
            sp.dma_start(core.gates[:, 4:8], g_ffn.rearrange("(a n) -> a n", a=1).broadcast_to([P, 4])).then_inc(loaded, 16)

        @block.gpsimd
        def _(pool):
            pool.memset(core.ident[:, :], 0.0).then_inc(made0, 1)
            pool.memset(core.half[:, :], -0.5).then_inc(made, 1)
            pool.memset(core.zeros[:, :], 0.0).then_inc(made, 1)
            pool.wait_ge(made0, 1)
            pool.affine_select(out=core.ident[:, :], in_=core.ident[:, :], compare_op=ALU.not_equal, fill=1.0,
                               base=0, pattern=[[-1, P]], channel_multiplier=1).then_inc(made, 1)
            pool.wait_ge(made, 3)

        @block.scalar
        def _(act):
            act.wait_ge(made, 2)
            tiles = rows.rearrange("(t p) d -> p t d", p=P)
            n = T0 // ZERO_DMAS
            for k in range(ZERO_DMAS):
                act.dma_start(tiles[:, k * n:(k + 1) * n, :],
                              core.zeros[:, :].rearrange("p (a d) -> p a d", a=1).broadcast_to([P, n, DIM])).then_inc(core.rows_zeroed, 16)
            act.wait_ge(loaded, 48)
            act.activation(core.gates[:, :], core.gates[:, :], ACT.Tanh).then_inc(tanhed, 1)
            act.wait_ge(tanhed, 1)


def phase_norms(core, name):
    nc = core.nc
    stats_done, aggr_done, powed = core.sem(name + "_stats"), core.sem(name + "_aggr"), core.sem(name + "_pow")
    with ExitStack() as ctx:
        stats = core.sb(ctx, name + "_st", [P, TILES, 6], F32)
        vareps = core.sb(ctx, name + "_ve", [P, TILES], F32)
        with nc.Block() as block:
            @block.vector
            def _(dve):
                for t in range(TILES):
                    dve.bn_stats(stats[:, t, :], core.xs[:, t, :]).then_inc(stats_done, 1)
                for t in range(TILES):
                    dve.wait_ge(stats_done, t + 1)
                    dve.bn_aggr(core.mv[:, t, :], stats[:, t, :]).then_inc(aggr_done, 1)
                dve.wait_ge(aggr_done, TILES)
                dve.tensor_scalar(vareps[:, :], core.mv[:, :, 1], LN_EPS, None, ALU.add).then_inc(aggr_done, 1)

            @block.gpsimd
            def _(pool):
                pool.wait_ge(aggr_done, TILES + 1)
                pool.tensor_tensor(core.rstd[:, :], vareps[:, :], core.half[:, 0:TILES], ALU.pow).then_inc(powed, 1)
                pool.wait_ge(powed, 1)



def phase_logits(core, name, E, yT_all, lg_all, router_rows=None, router_cols=None, router_b=None):
    nc = core.nc
    w_loaded, bias_loaded, w_turned, w_ready = (core.sem(name + n) for n in ("_w", "_b", "_wt", "_wr"))
    y_ready, y_turned, staged, logits, taken = (core.sem(name + n) for n in ("_y", "_yt", "_sg", "_lg", "_tk"))
    stored = [core.sem(name + f"_st{u}") for u in range(2)]
    with ExitStack() as ctx:
        rwT = core.sb(ctx, name + "_rwT", [P, KC, E], F32)
        rw = core.sb(ctx, name + "_rw", [P, DIM], F32)
        rb = core.sb(ctx, name + "_rb", [P, E], F32)
        y = core.sb(ctx, name + "_y_sb", [P, 2, DIM], F32)
        stage = core.sb(ctx, name + "_stage", [P, 2, KC, P], F32)
        turned = core.ps(ctx, name + "_psT", [P, 2, 512])
        psL = core.ps(ctx, name + "_psL", [P, 2, 512])
        with nc.Block() as block:
            @block.sync
            def _(sp):
                if router_rows is not None:
                    sp.dma_start(rw[0:E, :], router_rows).then_inc(w_loaded, 16)
                else:
                    sp.dma_start(rwT[:, :, :], router_cols.rearrange("(k p) e -> p k e", p=P)).then_inc(w_ready, 16)
                if router_b is not None:
                    sp.dma_start(rb[:, :], router_b.rearrange("(a n) -> a n", a=1).broadcast_to([P, E])).then_inc(bias_loaded, 16)
                @looped(sp, TILES // 2)
                def _(i):
                    for u in range(2):
                        sp.wait_ge(staged, i * 2 + (u + 3))
                        sp.dma_start(yT_all[i * 2 + u], stage[:, u, :, :].rearrange("p k c -> p (k c)")).then_inc(stored[u], 16)
                for u in range(2):
                    sp.wait_ge(stored[u], 16 * (TILES // 2))

            @block.tensor
            def _(pe):
                if router_rows is not None:
                    pe.wait_ge(w_loaded, 16)
                    for k in range(KC):
                        ins = pe.transpose(psL[:, 0, k * E:(k + 1) * E], rw[0:E, k * P:(k + 1) * P], core.ident[0:E, 0:E])
                    ins.then_inc(w_turned, 1)
                pe.wait_ge(w_ready, 16)
                pe.sem_inc(logits, 2)
                @looped(pe, TILES // 2)
                def _(i):
                    for u in range(2):
                        pe.wait_ge(y_ready, i * 2 + (u + 1))
                        pe.wait_ge(staged, i * 2 + (u + 1))
                        for k in range(KC):
                            ins = pe.transpose(turned[:, u, k * P:(k + 1) * P], y[:, u, k * P:(k + 1) * P], core.ident[:, :])
                        ins.then_inc(y_turned, 1)
                        pe.wait_ge(staged, i * 2 + (u + 3))
                        pe.wait_ge(taken, i * 2 + (u + 1))
                        for k in range(KC):
                            ins = pe.matmul(psL[:, u, 0:E], stage[:, u, k, :], rwT[:, k, :], start=(k == 0), stop=(k == KC - 1))
                        ins.then_inc(logits, 1)

            @block.vector
            def _(dve):
                if router_rows is not None:
                    dve.wait_ge(w_turned, 1)
                    dve.tensor_copy(rwT[:, :, :], psL[:, 0, 0:KC * E].rearrange("p (k e) -> p k e", k=KC)).then_inc(w_ready, 16)
                    dve.wait_ge(w_ready, 16)
                if router_b is not None:
                    dve.wait_ge(bias_loaded, 16)
                dve.sem_inc(staged, 2)
                dve.sem_inc(taken, 2)
                @looped(dve, TILES // 2)
                def _(i):
                    for u in range(2):
                        dve.wait_ge(staged, i * 2 + (u + 1))
                        dve.tensor_scalar(y[:, u, :], core.xs[:, i * 2 + u, :], core.mv[:, i * 2 + u, 0:1],
                                          core.rstd[:, bass.ds(i * 2 + u, 1)], ALU.subtract, ALU.mult).then_inc(y_ready, 1)
                        dve.wait_ge(y_turned, i * 2 + (u + 1))
                        wait_count(dve, stored[u], i * 16)
                        dve.wait_ge(logits, i * 2 + (u + 1))
                        dve.tensor_copy(stage[:, u, :, :], turned[:, u, 0:KC * P].rearrange("p (k c) -> p k c", k=KC)).then_inc(staged, 1)
                        dve.wait_ge(logits, i * 2 + (u + 3))
                        if router_b is not None:
                            dve.tensor_tensor(lg_all[:, i * 2 + u, :], psL[:, u, 0:E], rb[:, :], ALU.add).then_inc(taken, 1)
                        else:
                            dve.tensor_copy(lg_all[:, i * 2 + u, :], psL[:, u, 0:E]).then_inc(taken, 1)
                dve.wait_ge(taken, TILES + 2)


def phase_topk(core, name, E, K, lg_all, score_all, gate, kind, capacity=None):
    nc = core.nc
    T = TILES
    chain, found, exped, posed, ioted = (core.sem(name + n) for n in ("_ch", "_fd", "_ex", "_ps", "_io"))
    with ExitStack() as ctx:
        top = core.sb(ctx, name + "_top", [P, T, 8], F32)
        idx = core.sb(ctx, name + "_idx", [P, T, 8], U32)
        idxf = core.sb(ctx, name + "_idxf", [P, T, 8], F32)
        ex = core.sb(ctx, name + "_exs", [P, T, K], F32)
        exall = core.sb(ctx, name + "_exall", [P, T, E], F32)
        den = core.sb(ctx, name + "_den", [P, 2, T], F32)
        hot = core.sb(ctx, name + "_hot", [P, 2, T, E], F32)
        iota = core.sb(ctx, name + "_iota", [P, E], F32)
        io_b = iota[:, :].rearrange("p (a e) -> p a e", a=1).broadcast_to([P, T, E])

        def per_tile(ap, n):
            return ap.rearrange("p (t a) -> p t a", a=1).broadcast_to([P, T, n])

        if capacity is not None:
            mask = core.sb(ctx, name + "_mask", [P, T, E], F32)
            before = core.sb(ctx, name + "_before", [P, P], F32)
            ones = core.sb(ctx, name + "_ones", [P, P], F32)
            cum = core.sb(ctx, name + "_cum", [P, T, E], F32)
            psR = core.ps(ctx, name + "_psR", [P, 512])
            psC = core.ps(ctx, name + "_psC", [P, 512])
        with nc.Block() as block:
            @block.gpsimd
            def _(pool):
                pool.iota(iota[:, :], pattern=[[1, E]], base=0, channel_multiplier=0,
                          allow_small_or_imprecise_dtypes=True).then_inc(ioted, 1)
                if capacity is not None:
                    pool.memset(before[:, :], 1.0).then_inc(ioted, 1)
                    pool.memset(ones[:, :], 1.0).then_inc(ioted, 1)
                    pool.wait_ge(ioted, 3)
                    pool.affine_select(out=before[:, :], in_=before[:, :], compare_op=ALU.is_gt, fill=0.0,
                                       base=0, pattern=[[1, P]], channel_multiplier=-1).then_inc(ioted, 1)

            @block.scalar
            def _(act):
                act.wait_ge(chain, 1)
                act.activation(ex[:, :, :], ex[:, :, :], ACT.Exp).then_inc(exped, 1)
                if kind != "top":
                    act.wait_ge(chain, 2)
                    act.activation(exall[:, :, :], exall[:, :, :], ACT.Exp).then_inc(exped, 1)

            @block.tensor
            def _(pe):
                if capacity is not None:
                    pe.wait_ge(posed, 1)
                    pe.wait_ge(ioted, 4)
                    pe.matmul(psR[:, 0:T * E], before[:, :], mask[:, :, :], start=True, stop=True).then_inc(found, 1)
                    pe.matmul(psC[:, 0:T * E], ones[:, :], mask[:, :, :], start=True, stop=True).then_inc(found, 1)

            @block.vector
            def _(dve):
                tops, indices = core.sem(name + '_tp'), core.sem(name + '_ix')
                for t in range(T):
                    dve.max(top[:, t, :], lg_all[:, t, :]).then_inc(tops, 1)
                for t in range(T):
                    dve.wait_ge(tops, t + 1)
                    dve.max_index(idx[:, t, :], top[:, t, :], lg_all[:, t, :]).then_inc(indices, 1)
                c = Chain(dve, chain)
                c.link(dve.tensor_tensor(ex[:, :, :], top[:, :, 0:K], per_tile(top[:, :, 0], K), ALU.subtract))
                if kind != "top":
                    c.link(dve.tensor_tensor(exall[:, :, :], lg_all[:, :, :], per_tile(top[:, :, 0], E), ALU.subtract))
                dve.wait_ge(indices, T)
                c.link(dve.tensor_copy(idxf[:, :, :], idx[:, :, :]))
                dve.wait_ge(exped, 1 if kind == "top" else 2)
                c.link(dve.tensor_reduce(den[:, 0, :], ex[:, :, :], AX_X, ALU.add))
                if kind != "top":
                    c.link(dve.tensor_reduce(den[:, 1, :], exall[:, :, :], AX_X, ALU.add))
                if kind == "all":
                    c.link(dve.tensor_copy(den[:, 0, :], den[:, 1, :]))
                if kind == "eps":
                    c.link(dve.scalar_tensor_tensor(out=den[:, 0, :], in0=den[:, 1, :], scalar=1e-8, in1=den[:, 0, :],
                                                    op0=ALU.mult, op1=ALU.add))
                c.link(dve.reciprocal(den[:, 1, :], den[:, 0, :]))
                c.link(dve.tensor_tensor(ex[:, :, :], ex[:, :, :], per_tile(den[:, 1, :], K), ALU.mult))
                c.link(dve.tensor_scalar(ex[:, :, :], ex[:, :, :], gate, None, ALU.mult))
                dve.wait_ge(ioted, 1)
                for k in range(K):
                    c.link(dve.tensor_tensor(hot[:, 0, :, :], io_b, per_tile(idxf[:, :, k], E), ALU.is_equal))
                    if capacity is not None:
                        if k == 0:
                            c.link(dve.tensor_copy(mask[:, :, :], hot[:, 0, :, :]))
                        else:
                            c.link(dve.tensor_tensor(mask[:, :, :], mask[:, :, :], hot[:, 0, :, :], ALU.add))
                    out = score_all[:, :, :] if k == 0 else hot[:, 1, :, :]
                    c.link(dve.tensor_tensor(out, hot[:, 0, :, :], per_tile(ex[:, :, k], E), ALU.mult))
                    if k:
                        c.link(dve.tensor_tensor(score_all[:, :, :], score_all[:, :, :], hot[:, 1, :, :], ALU.add))
                if capacity is not None:
                    dve.sem_inc(posed, 1)
                    dve.wait_ge(found, 2)
                    c.link(dve.tensor_copy(hot[:, 0, :, :], psC[:, 0:T * E].rearrange("p (t e) -> p t e", t=T)))
                    c.link(dve.memset(hot[:, 1, :, :], 1.0))
                    for e in range(E):
                        ins = dve.tensor_tensor_scan(cum[:, :, e], hot[:, 1, :, e], hot[:, 0, :, e], 0.0, ALU.mult, ALU.add)
                        c.link(ins)
                    c.link(dve.tensor_tensor(cum[:, :, :], cum[:, :, :], hot[:, 0, :, :], ALU.subtract))
                    c.link(dve.tensor_tensor(cum[:, :, :], psR[:, 0:T * E].rearrange("p (t e) -> p t e", t=T), cum[:, :, :], ALU.add))
                    c.link(dve.tensor_scalar(cum[:, :, :], cum[:, :, :], float(capacity), None, ALU.is_lt))
                    c.link(dve.tensor_tensor(score_all[:, :, :], score_all[:, :, :], cum[:, :, :], ALU.mult))


def phase_store(core, out):
    nc = core.nc
    stored = core.sem("stored")
    with nc.Block() as block:
        @block.sync
        def _(sp):
            sp.dma_start(out.rearrange("b s d -> (b s) d").rearrange("(t p) d -> p t d", p=P), core.xs[:, :, :]).then_inc(stored, 16)
            sp.wait_ge(stored, 16)


HEADS, HD = 8, 8
PAIRS = HEADS // 2
Q_SLOTS, K_SLOTS = (0, 0, 1, 0, 1, 2), (0, 1, 0, 2, 1, 0)
SLOTS = len(Q_SLOTS)
GROUP = 4
ROWS = 2 * SLOTS * HD


def phase_split(core, name, src, aug, slots, l2norm):
    nc = core.nc
    G = GROUP
    chain, loaded, zready, p_ready, r_ready, squared, summed, rooted, used = (
        core.sem(name + k) for k in ("_ch", "_ld", "_z", "_p", "_r", "_sq", "_sm", "_rt", "_us"))
    made, stored = core.sem(name + "_mk"), core.sem(name + "_st")
    with ExitStack() as ctx:
        z = core.sb(ctx, name + "_zz", [P, G, DIM], F32)
        nrm = core.sb(ctx, name + "_nrm", [P, G, DIM], F32)
        r = core.sb(ctx, name + "_rr", [P, 2, G, DIM], F32)
        parts = core.sb(ctx, name + "_parts", [P, PIECES, G, DIM], BF16)
        block_ones = core.sb(ctx, name + "_bo", [P, P], F32)
        psN = core.ps(ctx, name + "_psN", [P, G, DIM])
        n_store = len(slots) * 4
        with nc.Block() as block:
            @block.sync
            def _(sp):
                @looped(sp, TILES // G)
                def _(i):
                    if src is not None:
                        wait_count(sp, p_ready, i * PIECES)
                        sp.dma_start(z[:, :, :], src[bass.ds(i * G, G)].rearrange("t p c -> p t c")).then_inc(loaded, 16)
                    for s, piece in enumerate(slots):
                        sp.wait_ge(p_ready, i * PIECES + (piece + 1))
                        for b in range(2):
                            for hh in range(2):
                                r0 = (hh * SLOTS + s) * HD
                                lo = 64 * b + 32 * hh
                                sp.dma_start(aug[i, b, r0:r0 + HD].rearrange("r a c -> a r c"),
                                             parts[lo:lo + 32, piece, :, :].rearrange("p g c -> p (g c)")).then_inc(stored, 16)
                sp.wait_ge(stored, 16 * n_store * (TILES // G))

            @block.gpsimd
            def _(pool):
                if l2norm:
                    bo = block_ones[:, :].rearrange("p (a r) -> p a r", r=HD)
                    pool.memset(block_ones[:, :], 1.0).then_inc(made, 1)
                    pool.wait_ge(made, 1)
                    pool.affine_select(out=bo, in_=bo, compare_op=ALU.is_ge, fill=0.0, base=0,
                                       pattern=[[-HD, P // HD], [0, HD]], channel_multiplier=1).then_inc(made, 1)
                    pool.wait_ge(made, 2)
                    pool.affine_select(out=bo, in_=bo, compare_op=ALU.is_ge, fill=0.0, base=HD - 1,
                                       pattern=[[HD, P // HD], [0, HD]], channel_multiplier=-1).then_inc(made, 1)

            @block.tensor
            def _(pe):
                if l2norm:
                    pe.wait_ge(made, 3)
                    @looped(pe, TILES // G)
                    def _(i):
                        pe.wait_ge(squared, i + 1)
                        for g in range(0, G, 2):
                            ins = pe.matmul(psN[:, g:g + 2, :], block_ones[:, :], nrm[:, g:g + 2, :], start=True, stop=True)
                        ins.then_inc(summed, 1)

            @block.scalar
            def _(act):
                @looped(act, TILES // G)
                def _(i):
                    if l2norm:
                        act.wait_ge(zready, i + 1)
                        wait_count(act, used, i)
                        act.activation(nrm[:, :, :], z[:, :, :], ACT.Square).then_inc(squared, 1)
                        act.wait_ge(summed, i + 1)
                        act.activation(nrm[:, :, :], psN[:, :, :], ACT.Sqrt).then_inc(rooted, 1)
                        act.wait_ge(used, i + 1)
                    else:
                        act.wait_ge(zready, i + 1)
                    wait_count(act, stored, i * (16 * n_store))
                    act.activation(parts[:, 0, :, :], z[:, :, :], ACT.Copy).then_inc(p_ready, 1)
                    for k in range(1, PIECES):
                        act.wait_ge(r_ready, i * 2 + k)
                        act.activation(parts[:, k, :, :], r[:, k - 1, :, :], ACT.Copy).then_inc(p_ready, 1)

            @block.vector
            def _(dve):
                @looped(dve, TILES // G)
                def _(i):
                    if src is None:
                        wait_count(dve, p_ready, i * PIECES)
                        for g in range(G):
                            ins = dve.tensor_scalar(z[:, g, :], core.xs[:, i * G + g, :], core.mv[:, i * G + g, 0:1],
                                                    core.rstd[:, bass.ds(i * G + g, 1)], ALU.subtract, ALU.mult)
                        ins.then_inc(zready, 1)
                        dve.wait_ge(zready, i + 1)
                    else:
                        dve.wait_ge(loaded, i * 16 + 16)
                        dve.sem_inc(zready, 1)
                    if l2norm:
                        c = Chain(dve, chain, i, 2)
                        dve.wait_ge(rooted, i + 1)
                        c.link(dve.tensor_scalar(nrm[:, :, :], nrm[:, :, :], 1e-12, None, ALU.max))
                        c.link(dve.reciprocal(nrm[:, :, :], nrm[:, :, :]))
                        dve.tensor_tensor(z[:, :, :], z[:, :, :], nrm[:, :, :], ALU.mult).then_inc(used, 1)
                        dve.wait_ge(used, i + 1)
                        c.close()
                    dve.wait_ge(p_ready, i * PIECES + 1)
                    dve.tensor_tensor(r[:, 0, :, :], z[:, :, :], parts[:, 0, :, :], ALU.subtract).then_inc(r_ready, 1)
                    dve.wait_ge(p_ready, i * PIECES + 2)
                    dve.wait_ge(r_ready, i * 2 + 1)
                    dve.tensor_tensor(r[:, 1, :, :], r[:, 0, :, :], parts[:, 1, :, :], ALU.subtract).then_inc(r_ready, 1)


def phase_context(core, ctx_tiles, ctxT_dram, vt_dram):
    nc = core.nc
    loaded = [core.sem(f"cx_loaded{u}") for u in range(2)]
    stored = [core.sem(f"cx_stored{u}") for u in range(2)]
    turned, taken, made = (core.sem("cx_" + k) for k in ("turned", "taken", "made"))
    with ExitStack() as ctx:
        cx = core.sb(ctx, "cx_in", [P, 2, DIM], F32)
        ct = core.sb(ctx, "cx_ct", [P, 2, KC, P], F32)
        vt = core.sb(ctx, "cx_vt", [P, 2, KC, 2 * HEADS, HD + 1], F32)
        psT = core.ps(ctx, "cx_ps", [P, 2, 512])
        with nc.Block() as block:
            @block.sync
            def _(sp):
                @looped(sp, TILES // 2)
                def _(i):
                    for u in range(2):
                        sp.wait_ge(turned, i * 2 + (u + 1))
                        sp.dma_start(cx[:, u, :], ctx_tiles[i * 2 + u]).then_inc(loaded[u], 16)
                    for u in range(2):
                        sp.wait_ge(taken, i * 4 + (2 * u + 6))
                        sp.dma_start(ctxT_dram[i * 2 + u], ct[:, u, :, :].rearrange("p k c -> p (k c)")).then_inc(stored[u], 16)
                        sp.dma_start(vt_dram[i * 2 + u], vt[:, u, :, :, :].rearrange("p k h d -> p (k h d)")).then_inc(stored[u], 16)
                for u in range(2):
                    sp.wait_ge(stored[u], 32 * (TILES // 2))

            @block.gpsimd
            def _(pool):
                pool.memset(vt[:, :, :, :, :], 1.0).then_inc(made, 1)

            @block.tensor
            def _(pe):
                pe.sem_inc(turned, 2)
                @looped(pe, TILES // 2)
                def _(i):
                    for u in range(2):
                        pe.wait_ge(loaded[u], i * 16 + 16)
                        pe.wait_ge(taken, i * 4 + (2 * u + 2))
                        for k in range(KC):
                            ins = pe.transpose(psT[:, u, k * P:(k + 1) * P], cx[:, u, k * P:(k + 1) * P], core.ident[:, :])
                        ins.then_inc(turned, 1)

            @block.vector
            def _(dve):
                dve.sem_inc(taken, 4)
                dve.wait_ge(made, 1)
                @looped(dve, TILES // 2)
                def _(i):
                    for u in range(2):
                        dve.wait_ge(turned, i * 2 + (u + 3))
                        wait_count(dve, stored[u], i * 32)
                        dve.tensor_copy(ct[:, u, :, :], psT[:, u, 0:KC * P].rearrange("p (k c) -> p k c", k=KC)).then_inc(taken, 1)
                        for k in range(KC):
                            ins = dve.tensor_copy(vt[:, u, k, :, 0:HD], psT[:, u, k * P:(k + 1) * P].rearrange("p (h d) -> p h d", d=HD))
                        ins.then_inc(taken, 1)


def phase_attend(core, name, q_aug, k_aug, vt_dram, gate, scale, with_max):
    nc = core.nc
    n = name
    NB = 4
    STEPS = 2 * TILES // NB
    KR = ROWS + 4 if with_max else ROWS
    q_loaded = [core.sem(f"{n}_ql{m}") for m in range(NB)]
    v_loaded = [core.sem(f"{n}_vl{m}") for m in range(2)]
    shift_loaded = [core.sem(f"{n}_sl{m}") for m in range(NB)]
    s_done, max_done, max_turned, shift_read, shift_ready = (core.sem(n + k) for k in ("_s", "_mx", "_mt", "_sr", "_sh"))
    st_done, exp_done, pv_done, out_done, nd_done, added, chain, made, cleared, rec_done = (
        core.sem(n + k) for k in ("_st", "_ex", "_pv", "_ov", "_nd", "_ad", "_ch", "_mk", "_cl", "_rd"))
    with ExitStack() as ctx:
        qa = core.sb(ctx, n + "_qa", [P, NB, 2, PAIRS, DIM], BF16)
        ka = core.sb(ctx, n + "_ka", [P, NB, PAIRS, DIM], BF16)
        vt = core.sb(ctx, n + "_vt", [P, 2, KC, 2 * HEADS, HD + 1], F32)
        pt = core.sb(ctx, n + "_pt", [P, PAIRS, KC, 2 * DIM], F32)
        mx = core.sb(ctx, n + "_mx_sb", [P, 2, 2 * HEADS], F32)
        sh = core.sb(ctx, n + "_sh_sb", [2 * HEADS, 2, 2, P], BF16)
        ov = core.sb(ctx, n + "_ov_sb", [P, 2, 2, DIM], F32)
        rec = core.sb(ctx, n + "_rec", [P, DIM], F32)
        pick = core.sb(ctx, n + "_pick", [P, 2, 2, 64], F32)
        psM = core.ps(ctx, n + "_psM", [P, 2, 512])
        psS = core.ps(ctx, n + "_psS", [P, 2, KC, 512])
        psV = core.ps(ctx, n + "_psV", [P, 2, DIM])
        psN = core.ps(ctx, n + "_psN", [P, 2, DIM])

        def aug_tile(aug, b, t):
            return aug[t // GROUP, b].rearrange("r a (g c) -> g r a c", g=GROUP)[t % GROUP]

        def count(j, m, per, more):
            return j * (NB * per) + (m * per + more)

        with nc.Block() as block:
            @block.gpsimd
            def _(pool):
                pool.memset(qa[:, :, :, :, :], 0.0).then_inc(made, 1)
                pool.memset(ka[:, :, :, :], 1.0).then_inc(made, 1)
                pool.memset(pick[:, :, :, :], 0.0).then_inc(made, 1)
                pool.wait_ge(made, 3)
                for d in range(2):
                    for g in range(2):
                        v = pick[:, d, g, :].rearrange("p (hh g a i) -> p g hh a i", hh=2, g=2, a=2)[:, g]
                        pool.affine_select(out=v, in_=v, compare_op=ALU.not_equal, fill=1.0, base=-HD * d,
                                           pattern=[[-32, 2], [-64, 2], [d - 1, HD]], channel_multiplier=1).then_inc(made, 1)

            @block.sync
            def _(sp):
                def load(j, m):
                    b = m % 2
                    t = j * 2 + m // 2
                    for hh in range(2):
                        r = slice(hh * SLOTS * HD, (hh + 1) * SLOTS * HD)
                        sp.dma_start(qa[r, m, hh, :, :], aug_tile(q_aug, b, t)[r]).then_inc(q_loaded[m], 16)
                    sp.dma_start(ka[0:ROWS, m, :, :], aug_tile(k_aug, b, t)).then_inc(q_loaded[m], 16)

                def load_values(j, u):
                    sp.dma_start(vt[:, u, :, :, :].rearrange("p k h d -> p (k h d)"), vt_dram[j * 2 + u]).then_inc(v_loaded[u], 16)

                def shift(j, m):
                    sp.wait_ge(shift_ready, count(j, m, 1, 1))
                    for hh in range(2):
                        for s in range(2):
                            row = ROWS + 2 * hh + s
                            sp.dma_start(qa[row:row + 1, m, hh, :, :].rearrange("p a (f c) -> p (a f) c", f=2),
                                         sh[8 * hh:8 * hh + 8, m % 2, s, :]).then_inc(shift_loaded[m], 16)

                sp.wait_ge(made, 3)
                for m in range(NB):
                    load(0, m)
                for u in range(2):
                    load_values(0, u)
                if with_max:
                    shift(0, 0)
                    shift(0, 1)

                def step(j, last):
                    for m in range(NB):
                        if with_max and not (last and m >= 2):
                            shift(j + (m + 2) // NB, (m + 2) % NB)
                        if not last:
                            sp.wait_ge(st_done, count(j, m, PAIRS, PAIRS))
                            load(j + 1, m)
                            if m % 2:
                                sp.wait_ge(pv_done, count(j, m, 2, 4))
                                load_values(j + 1, m // 2)

                @looped(sp, STEPS - 1)
                def _(j):
                    step(j, False)
                step(STEPS - 1, True)

            @block.tensor
            def _(pe):
                def scores(j, m, heads):
                    for h in heads:
                        if h == 0:
                            pe.wait_ge(q_loaded[m], j * 48 + 48)
                            wait_count(pe, shift_read, count(j, m, 1, 0))
                        pe.wait_ge(max_done, count(j, m, HEADS, h + 1))
                        a, hh = h // 2, h % 2
                        for f in range(2):
                            ins = pe.matmul(psM[:, h % 2, f * DIM:(f + 1) * DIM], qa[0:ROWS, m, hh, a, f * P:(f + 1) * P],
                                            ka[0:ROWS, m, a, :], start=True, stop=True)
                        ins.then_inc(s_done, 1)

                def turn_max(j, m):
                    pe.wait_ge(max_done, count(j, m, HEADS, HEADS + 2))
                    pe.transpose(psM[0:2 * HEADS, 0, 0:P], mx[:, m % 2, :], core.ident[:, :]).then_inc(max_turned, 1)

                def scores_t(j, m, a):
                    if a == 0:
                        pe.wait_ge(q_loaded[m], j * 48 + 48)
                        if with_max:
                            pe.wait_ge(shift_loaded[m], j * 64 + 64)
                    pe.wait_ge(exp_done, count(j, m, PAIRS, a + 1))
                    for k in range(KC):
                        ins = pe.matmul(psS[:, a % 2, k, :], ka[0:KR, m, a, k * P:(k + 1) * P], qa[0:KR, m, :, a, :], start=True, stop=True)
                    ins.then_inc(st_done, 1)

                def values(j, m, g):
                    if g == 0:
                        wait_count(pe, out_done, count(j, m, 1, 0))
                        pe.wait_ge(v_loaded[m // 2], j * 16 + 16)
                    pe.wait_ge(exp_done, count(j, m, PAIRS, 2 * g + 4))
                    for k in range(KC):
                        for q in range(4):
                            a, hh = 2 * g + q // 2, q % 2
                            ins = pe.matmul(psV[32 * q:32 * q + HD + 1, g, :], vt[:, m // 2, k, HEADS * (m % 2) + 4 * hh + a, :],
                                            pt[:, a, k, hh * DIM:(hh + 1) * DIM], start=(k == 0), stop=(k == KC - 1),
                                            tile_position=(0, 32 * q))
                    ins.then_inc(pv_done, 1)

                def gather_heads(j, m):
                    pe.wait_ge(out_done, count(j, m, 1, 1))
                    b = m % 2
                    if b == 0:
                        wait_count(pe, added, j * 2 + m // 2)
                    for d in range(2):
                        for g in range(2):
                            ins = pe.matmul(psN[64 * b:64 * b + 64, d, :], pick[:, d, g, :], ov[:, b, g, :],
                                            start=(g == 0), stop=(g == 1), tile_position=(0, 64 * b))
                    ins.then_inc(nd_done, 1)

                pe.sem_inc(pv_done, 2)
                pe.sem_inc(nd_done, 2)
                pe.wait_ge(made, 7)
                pe.wait_ge(cleared, 1)
                if with_max:
                    for m in range(2):
                        scores(0, m, range(HEADS))
                        turn_max(0, m)

                def step(j, first, last):
                    for m in range(NB):
                        ahead = with_max and not (last and m >= 2)
                        nj, nm = j + (m + 2) // NB, (m + 2) % NB
                        scores_t(j, m, 0)
                        scores_t(j, m, 1)
                        if not (first and m == 0):
                            if m:
                                gather_heads(j, m - 1)
                            else:
                                gather_heads(j - 1, NB - 1)
                        if ahead:
                            scores(nj, nm, (0, 1))
                        scores_t(j, m, 2)
                        if ahead:
                            scores(nj, nm, (2, 3))
                        scores_t(j, m, 3)
                        if ahead:
                            scores(nj, nm, (4, 5))
                        values(j, m, 0)
                        if ahead:
                            scores(nj, nm, (6, 7))
                        values(j, m, 1)
                        if ahead:
                            turn_max(nj, nm)

                step(0, True, False)
                with pe.Fori(1, STEPS - 1) as j:
                    step(j, False, False)
                step(STEPS - 1, False, True)
                gather_heads(STEPS - 1, NB - 1)

            @block.scalar
            def _(act):
                act.sem_inc(exp_done, 2)
                act.wait_ge(made, 7)

                def step(j):
                    for m in range(NB):
                        for a in range(PAIRS):
                            act.wait_ge(st_done, count(j, m, PAIRS, a + 1))
                            act.wait_ge(pv_done, count(j, m, 2, a // 2 + 1))
                            act.activation(pt[:, a, :, :], psS[:, a % 2, :, :], ACT.Exp, scale=scale).then_inc(exp_done, 1)
                        act.wait_ge(pv_done, count(j, m, 2, 4))
                        act.wait_ge(nd_done, count(j, m, 1, 1))
                        act.activation(ov[:, m % 2, :, :], psV[:, :, :], ACT.Copy).then_inc(out_done, 1)

                @looped(act, STEPS)
                def _(j):
                    step(j)

            @block.vector
            def _(dve):
                def maxima(j, m, heads):
                    for h in heads:
                        dve.wait_ge(s_done, count(j, m, HEADS, h + 1))
                        if h == 0:
                            wait_count(dve, max_turned, count(j, m, 1, 0))
                        dve.tensor_reduce(mx[:, m % 2, h % 2 * 8 + h // 2 * 2:h % 2 * 8 + h // 2 * 2 + 2], psM[:, h % 2, :].rearrange("p (f c) -> p f c", f=2),
                                          AX_X, ALU.max).then_inc(max_done, 1)

                def shifts(j, m):
                    dve.wait_ge(max_turned, count(j, m, 1, 1))
                    if m >= 2:
                        dve.wait_ge(shift_loaded[m - 2], j * 64 + 64)
                    else:
                        wait_count(dve, shift_loaded[m + 2], j * 64)
                    dve.tensor_scalar(sh[:, m % 2, 0, :], psM[0:2 * HEADS, 0, 0:P], -1.0, None, ALU.mult).then_inc(chain, 1)
                    dve.wait_ge(chain, count(j, m, 1, 1))
                    dve.scalar_tensor_tensor(out=sh[:, m % 2, 1, :], in0=psM[0:2 * HEADS, 0, 0:P], scalar=-1.0,
                                             in1=sh[:, m % 2, 0, :], op0=ALU.mult, op1=ALU.subtract).then_inc(shift_ready, 1)
                    dve.wait_ge(shift_ready, count(j, m, 1, 1))
                    dve.sem_inc(shift_read, 1)

                def add_tile(j, u):
                    t = j * 2 + u
                    dve.wait_ge(nd_done, j * NB + (2 * u + 4))
                    dve.reciprocal(rec[:, :], psN[:, 1, :]).then_inc(rec_done, 1)
                    dve.wait_ge(rec_done, j * 4 + (2 * u + 1))
                    dve.tensor_tensor(rec[:, :], psN[:, 0, :], rec[:, :], ALU.mult).then_inc(rec_done, 1)
                    dve.wait_ge(rec_done, j * 4 + (2 * u + 2))
                    dve.scalar_tensor_tensor(out=core.xs[:, t, :], in0=rec[:, :], scalar=gate, in1=core.xs[:, t, :],
                                             op0=ALU.mult, op1=ALU.add).then_inc(added, 1)
                    dve.wait_ge(added, t + 1)

                dve.memset(psV[:, :, :], 0.0).then_inc(cleared, 1)
                dve.sem_inc(max_done, 2)
                if with_max:
                    for m in range(2):
                        maxima(0, m, range(HEADS))
                        shifts(0, m)

                def step(j, first, last):
                    for m in range(NB):
                        ahead = with_max and not (last and m >= 2)
                        nj, nm = j + (m + 2) // NB, (m + 2) % NB
                        if ahead:
                            maxima(nj, nm, range(0, 2))
                        if m == 2:
                            add_tile(j, 0)
                        if m == 0 and not first:
                            add_tile(j - 1, 1)
                        if ahead:
                            maxima(nj, nm, range(2, HEADS))
                            shifts(nj, nm)

                step(0, True, False)
                with dve.Fori(1, STEPS - 1) as j:
                    step(j, False, False)
                step(STEPS - 1, False, True)
                add_tile(STEPS - 1, 1)


def pipelined(eng, step, first, last, head, tail):
    lo, hi = first + head, last - tail
    assert lo % 2 == 0 and (hi - lo) % 2 == 0
    for s in range(first, lo):
        step(s, s % 2)
    with eng.Fori(lo // 2, hi // 2) as j:
        for v in range(2):
            step(j * 2 + v, v)
    for s in range(hi, last):
        step(s, s % 2)


def valid(t):
    return not isinstance(t, int) or 0 <= t < TILES


def phase_turn_weights(core, name, pairs):
    nc = core.nc
    n = len(pairs)
    loaded, turned, copied, stored = (core.sem(name + k) for k in ("_l", "_t", "_c", "_s"))
    with ExitStack() as ctx:
        w = core.sb(ctx, name + "_w", [P, n, KC, DIM], F32)
        wt = core.sb(ctx, name + "_wt", [P, n, KC, DIM], F32)
        ps = core.ps(ctx, name + "_ps", [P, n, 512])
        with nc.Block() as block:
            @block.sync
            def _(sp):
                for m, (src, _) in enumerate(pairs):
                    sp.dma_start(w[:, m, :, :], src.rearrange("(o p) i -> p o i", p=P)).then_inc(loaded, 16)
                for m, (_, dst) in enumerate(pairs):
                    sp.wait_ge(copied, m + 1)
                    sp.dma_start(dst.rearrange("(k p) o -> p k o", p=P), wt[:, m, :, :]).then_inc(stored, 16)
                sp.wait_ge(stored, 16 * n)

            @block.tensor
            def _(pe):
                pe.wait_ge(loaded, 16 * n)
                for m in range(n):
                    for k in range(KC):
                        for o in range(KC):
                            ins = pe.transpose(ps[:, m, k * DIM + o * P:k * DIM + (o + 1) * P], w[:, m, o, k * P:(k + 1) * P], core.ident[:, :])
                    ins.then_inc(turned, 1)

            @block.scalar
            def _(act):
                for m in range(n):
                    act.wait_ge(turned, m + 1)
                    act.activation(wt[:, m, :, :], ps[:, m, :].rearrange("p (k o) -> p k o", k=KC), ACT.Copy).then_inc(copied, 1)


def phase_keys_values(core, name, ctxT_dram, kv_all, wk, wv, bk, bv):
    nc = core.nc
    w_loaded, done, added = (core.sem(name + k) for k in ("_w", "_d", "_a"))
    loaded = [core.sem(f"{name}_l{u}") for u in range(2)]
    with ExitStack() as ctx:
        w = core.sb(ctx, name + "_ws", [P, KC, 2, DIM], F32)
        b = core.sb(ctx, name + "_bs", [P, 2, DIM], F32)
        ct = core.sb(ctx, name + "_ct", [P, 2, KC, P], F32)
        ps = core.ps(ctx, name + "_ps", [P, 2, 512])
        with nc.Block() as block:
            @block.sync
            def _(sp):
                for m, (ww, bb) in enumerate(((wk, bk), (wv, bv))):
                    sp.dma_start(w[:, :, m, :], ww.rearrange("(k p) o -> p k o", p=P)).then_inc(w_loaded, 16)
                    sp.dma_start(b[:, m, :], bb.rearrange("(a n) -> a n", a=1).broadcast_to([P, DIM])).then_inc(w_loaded, 16)
                @looped(sp, TILES // 2)
                def _(i):
                    for u in range(2):
                        sp.wait_ge(done, i * 2 + (u + 1))
                        sp.dma_start(ct[:, u, :, :].rearrange("p k c -> p (k c)"), ctxT_dram[i * 2 + u]).then_inc(loaded[u], 16)

            @block.tensor
            def _(pe):
                pe.sem_inc(done, 2)
                pe.wait_ge(w_loaded, 64)
                @looped(pe, TILES // 2)
                def _(i):
                    for u in range(2):
                        pe.wait_ge(loaded[u], i * 16 + 16)
                        pe.wait_ge(added, i * 2 + (u + 1))
                        for k in range(KC):
                            ins = pe.matmul(ps[:, u, :], ct[:, u, k, :], w[:, k, :, :], start=(k == 0), stop=(k == KC - 1))
                        ins.then_inc(done, 1)

            @block.vector
            def _(dve):
                dve.sem_inc(added, 2)
                dve.wait_ge(w_loaded, 64)
                @looped(dve, TILES // 2)
                def _(i):
                    for u in range(2):
                        dve.wait_ge(done, i * 2 + (u + 3))
                        dve.tensor_tensor(kv_all[:, i * 2 + u, :], ps[:, u, :], b[:, :, :].rearrange("p m o -> p (m o)"), ALU.add).then_inc(added, 1)
                dve.wait_ge(added, TILES + 2)


def phase_rms(core, name, q_all, kv_all, rq, rk, eps):
    nc = core.nc
    summed, based, powed = (core.sem(name + k) for k in ("_s", "_b", "_p"))
    with ExitStack() as ctx:
        junk = core.sb(ctx, name + "_junk", [P, 2, DIM], F32)
        ss = core.sb(ctx, name + "_ss", [P, 2, TILES], F32)
        base = core.sb(ctx, name + "_base", [P, 2, TILES], F32)
        with nc.Block() as block:
            @block.vector
            def _(dve):
                for t in range(TILES):
                    for m, src in ((0, q_all[:, t, :]), (1, kv_all[:, t, 0:DIM])):
                        if t:
                            dve.wait_ge(summed, 2 * t + m - 1)
                        dve.tensor_tensor_reduce(out=junk[:, m, :], in0=src, in1=src, scale=1.0, scalar=0.0, op0=ALU.mult,
                                                 op1=ALU.add, accum_out=ss[:, m, t:t + 1]).then_inc(summed, 1)
                dve.wait_ge(summed, 2 * TILES)
                dve.tensor_scalar(base[:, :, :], ss[:, :, :], 1.0 / DIM, eps, ALU.mult, ALU.add).then_inc(based, 1)

            @block.gpsimd
            def _(pool):
                pool.wait_ge(based, 1)
                pool.tensor_tensor(rq, base[:, 0, :], core.half[:, 0:TILES], ALU.pow).then_inc(powed, 1)
                pool.tensor_tensor(rk, base[:, 1, :], core.half[:, 0:TILES], ALU.pow).then_inc(powed, 1)
                pool.wait_ge(powed, 2)


def phase_cross(core, name, q_all, kv_all, rq, rk, gq, gk, wo, bo, gate):
    nc = core.nc
    H, W = 16, DIM // 16
    HP, HK = H // 2, H // KC
    n = name + "_"
    w_loaded, made, scaled_bias = (core.sem(n + k) for k in ("wl", "mk", "gb"))
    laid = core.sem(n + "la")
    normed, qk_turned, qk_copied, keys_ready, values_ready = (core.sem(n + k) for k in ("nm", "qt", "qc", "kr", "vr"))
    s_done, maxed, shifted, exped, summed, p_turned, p_copied, pv_done = (
        core.sem(n + k) for k in ("sd", "mx", "sf", "ex", "sm", "pt", "pc", "pv"))
    o_ready, o_turned, o_copied, out_done, added, part_added, den_ready = (
        core.sem(n + k) for k in ("or", "ot", "oc", "od", "ad", "pa", "dn"))
    with ExitStack() as ctx:
        sb, ps = core.sb, core.ps
        wos = sb(ctx, n + "wo", [P, KC, DIM], F32)
        gains = sb(ctx, n + "gains", [P, 3, DIM], F32)
        mask = sb(ctx, n + "mask", [P, HK], F32)
        qkn = sb(ctx, n + "qkn", [P, 2, 2, DIM], F32)
        qkT = sb(ctx, n + "qkT", [P, 2, 2, KC, P], F32)
        kbd = sb(ctx, n + "kbd", [P, 2, KC, 2, HK, SEQ], F32)
        vbd = sb(ctx, n + "vbd", [P, 2, 2, HP, 2, W], F32)
        prob = sb(ctx, n + "prob", [P, 2, H, SEQ], F32)
        pT = sb(ctx, n + "pT", [P, 2, HP, P], F32)
        mx = sb(ctx, n + "mx_sb", [P, H], F32)
        den = sb(ctx, n + "den", [P, H], F32)
        rden = sb(ctx, n + "rden", [P, 2, H], F32)
        o = sb(ctx, n + "o", [P, 2, DIM], F32)
        oT = sb(ctx, n + "oT", [P, 2, KC, P], F32)
        psT = ps(ctx, n + "psT", [P, 512])
        psS = ps(ctx, n + "psS", [P, 2, 512])
        psP = ps(ctx, n + "psP", [P, 2, 512])
        psO = ps(ctx, n + "psO", [P, 512])
        psQ = ps(ctx, n + "psQ", [P, 512])
        psX = ps(ctx, n + "psX", [P, 512])

        with nc.Block() as block:
            @block.sync
            def _(sp):
                sp.dma_start(wos[:, :, :], wo.rearrange("(k p) o -> p k o", p=P)).then_inc(w_loaded, 16)
                for m, v in enumerate((gq, gk, bo)):
                    sp.dma_start(gains[:, m, :], v.rearrange("(a n) -> a n", a=1).broadcast_to([P, DIM])).then_inc(w_loaded, 16)

            @block.gpsimd
            def _(pool):
                pool.memset(mask[:, :], 1.0).then_inc(made, 1)
                pool.memset(vbd[:, :, :, :, :, :], 0.0).then_inc(made, 1)
                pool.wait_ge(made, 2)
                pool.affine_select(out=mask[:, :], in_=mask[:, :], compare_op=ALU.is_ge, fill=0.0, base=0,
                                   pattern=[[-W, HK]], channel_multiplier=1).then_inc(made, 1)
                pool.wait_ge(made, 3)
                pool.affine_select(out=mask[:, :], in_=mask[:, :], compare_op=ALU.is_ge, fill=0.0, base=W - 1,
                                   pattern=[[W, HK]], channel_multiplier=-1).then_inc(made, 1)
                pool.wait_ge(made, 4)

                def step(s, v):
                    t, u = s + 2, v
                    if valid(t):
                        pool.wait_ge(qk_copied, t + 1)
                        wait_count(pool, s_done, t - 1)
                        for k in range(KC):
                            for b in range(2):
                                src = qkT[:, u, 1, k, SEQ * b:SEQ * b + SEQ].rearrange("p (a c) -> p a c", a=1).broadcast_to([P, HK, SEQ])
                                ins = pool.tensor_tensor(kbd[:, u, k, b, :, :], src,
                                                         mask[:, :].rearrange("p (h a) -> p h a", a=1).broadcast_to([P, HK, SEQ]), ALU.mult)
                        ins.then_inc(keys_ready, 1)
                    t, u = s + 1, (v + 1) % 2
                    if valid(t):
                        wait_count(pool, pv_done, t - 1)
                        for c, (b, hh) in enumerate(((0, 0), (1, 1), (0, 1), (1, 0))):
                            if c == 0 and valid(s + 2):
                                pool.wait_ge(keys_ready, s + 3)
                            if c:
                                pool.wait_ge(laid, t * 3 + c)
                            src = kv_all[SEQ * b:SEQ * b + SEQ, t, DIM:2 * DIM].rearrange("p (a h w) -> p a h w", h=2, w=W)[:, :, hh, :]
                            pool.tensor_copy(vbd[SEQ * hh:SEQ * hh + SEQ, u, b, :, hh, :], src).then_inc(laid if c < 3 else values_ready, 1)
                        pool.wait_ge(values_ready, t + 1)

                pipelined(pool, step, -2, TILES, 4, 2)

            @block.tensor
            def _(pe):
                pe.wait_ge(w_loaded, 64)

                def step(s, v):
                    t, u = s, v
                    if valid(t):
                        pe.wait_ge(exped, t + 1)
                        wait_count(pe, p_copied, t)
                        for a in range(HP):
                            ins = pe.transpose(psP[:, a // 4, a % 4 * P:(a % 4 + 1) * P],
                                               prob[:, u, 2 * a:2 * a + 2, :].rearrange("p h c -> p (h c)"), core.ident[:, :])
                        ins.then_inc(p_turned, 1)
                    t, u = s + 1, (v + 1) % 2
                    if valid(t):
                        pe.wait_ge(keys_ready, t + 1)
                        wait_count(pe, shifted, t)
                        for k in range(KC):
                            for b in range(2):
                                ins = pe.matmul(psS[SEQ * b:SEQ * b + SEQ, k, :], qkT[:, u, 0, k, SEQ * b:SEQ * b + SEQ],
                                                kbd[:, u, k, b, :, :], start=True, stop=True, tile_position=(0, SEQ * b))
                        ins.then_inc(s_done, 1)
                    t, u = s - 1, (v + 1) % 2
                    if valid(t):
                        pe.wait_ge(o_ready, t + 1)
                        wait_count(pe, o_copied, t)
                        for k in range(KC):
                            ins = pe.transpose(psQ[:, k * P:(k + 1) * P], o[:, u, k * P:(k + 1) * P], core.ident[:, :])
                        ins.then_inc(o_turned, 1)
                    t, u = s + 2, v
                    if valid(t):
                        pe.wait_ge(normed, t + 1)
                        wait_count(pe, qk_copied, t)
                        for m in range(2):
                            for k in range(KC):
                                at = (m * KC + k) * P
                                ins = pe.transpose(psT[:, at:at + P], qkn[:, u, m, k * P:(k + 1) * P], core.ident[:, :])
                        ins.then_inc(qk_turned, 1)
                    t, u = s, v
                    if valid(t):
                        pe.wait_ge(p_copied, t + 1)
                        pe.wait_ge(values_ready, t + 1)
                        wait_count(pe, o_ready, t)
                        for a in range(HP):
                            for b in range(2):
                                ins = pe.matmul(psO[SEQ * b:SEQ * b + SEQ, 2 * W * a:2 * W * (a + 1)], pT[:, u, a, SEQ * b:SEQ * b + SEQ],
                                                vbd[:, u, b, a, :, :], start=True, stop=True, tile_position=(0, SEQ * b))
                        ins.then_inc(pv_done, 1)
                    t, u = s - 1, (v + 1) % 2
                    if valid(t):
                        pe.wait_ge(o_copied, t + 1)
                        wait_count(pe, part_added, t)
                        for k in range(KC):
                            ins = pe.matmul(psX[:, 0:DIM], oT[:, u, k, :], wos[:, k, :], start=(k == 0), stop=(k == KC - 1))
                        ins.then_inc(out_done, 1)

                pipelined(pe, step, -2, TILES + 1, 4, 3)

            @block.scalar
            def _(act):
                def step(s, v):
                    t, u = s, v
                    if valid(t):
                        act.wait_ge(p_turned, t + 1)
                        wait_count(act, pv_done, t - 1)
                        act.activation(pT[:, u, :, :], psP[:, :, :].rearrange("p b (a c) -> p (b a) c", c=P), ACT.Copy).then_inc(p_copied, 1)
                    t, u = s + 1, (v + 1) % 2
                    if valid(t):
                        act.wait_ge(shifted, t + 1)
                        act.activation(prob[:, u, :, :], prob[:, u, :, :], ACT.Exp, scale=W ** -0.5).then_inc(exped, 1)
                    t, u = s - 1, (v + 1) % 2
                    if valid(t):
                        act.wait_ge(o_turned, t + 1)
                        wait_count(act, out_done, t - 1)
                        act.activation(oT[:, u, :, :], psQ[:, 0:KC * P].rearrange("p (k c) -> p k c", k=KC), ACT.Copy).then_inc(o_copied, 1)
                    t, u = s + 2, v
                    if valid(t):
                        act.wait_ge(qk_turned, t + 1)
                        wait_count(act, s_done, t - 1)
                        wait_count(act, keys_ready, t - 1)
                        act.activation(qkT[:, u, :, :, :], psT[:, :].rearrange("p (m k c) -> p m k c", m=2, k=KC), ACT.Copy).then_inc(qk_copied, 1)

                pipelined(act, step, -2, TILES + 1, 4, 3)

            @block.vector
            def _(dve):
                dve.wait_ge(w_loaded, 64)
                dve.tensor_scalar(gains[:, 2, :], gains[:, 2, :], gate, None, ALU.mult).then_inc(scaled_bias, 1)
                dve.wait_ge(scaled_bias, 1)

                def normalise(t, u):
                    if valid(t):
                        wait_count(dve, qk_turned, t - 1)
                        dve.scalar_tensor_tensor(out=qkn[:, u, 0, :], in0=q_all[:, t, :], scalar=rq[:, bass.ds(t, 1)], in1=gains[:, 0, :],
                                                 op0=ALU.mult, op1=ALU.mult)
                        dve.scalar_tensor_tensor(out=qkn[:, u, 1, :], in0=kv_all[:, t, 0:DIM], scalar=rk[:, bass.ds(t, 1)], in1=gains[:, 1, :],
                                                 op0=ALU.mult, op1=ALU.mult).then_inc(normed, 1)

                def step(s, v):
                    t, u = s + 1, (v + 1) % 2
                    if valid(t):
                        dve.wait_ge(s_done, t + 1)
                        wait_count(dve, shifted, t)
                        scores = psS[:, :, :].rearrange("p k (h c) -> p (k h) c", c=SEQ)
                        dve.tensor_reduce(mx[:, :], scores, AX_X, ALU.max).then_inc(maxed, 1)
                        dve.wait_ge(maxed, t + 1)
                        wait_count(dve, p_turned, t - 1)
                        dve.tensor_tensor(prob[:, u, :, :], scores, mx[:, :].rearrange("p (h a) -> p h a", a=1).broadcast_to([P, H, SEQ]),
                                          ALU.subtract).then_inc(shifted, 1)
                    normalise(s + 3, (v + 1) % 2)
                    t, u = s + 1, (v + 1) % 2
                    if valid(t):
                        dve.wait_ge(exped, t + 1)
                        dve.tensor_reduce(den[:, :], prob[:, u, :, :], AX_X, ALU.add).then_inc(summed, 1)
                        dve.wait_ge(summed, t + 1)
                        dve.reciprocal(rden[:, u, :], den[:, :]).then_inc(den_ready, 1)
                        dve.wait_ge(den_ready, t + 1)
                    t, u = s, v
                    if valid(t):
                        dve.wait_ge(pv_done, t + 1)
                        wait_count(dve, o_turned, t - 1)
                        dve.tensor_tensor(o[:, u, :].rearrange("p (h w) -> p h w", w=W), psO[:, 0:DIM].rearrange("p (h w) -> p h w", w=W),
                                          rden[:, u, :].rearrange("p (h a) -> p h a", a=1).broadcast_to([P, H, W]), ALU.mult).then_inc(o_ready, 1)
                        dve.tensor_tensor(core.xs[:, t, :], core.xs[:, t, :], gains[:, 2, :], ALU.add).then_inc(added, 1)
                    t, u = s - 1, (v + 1) % 2
                    if valid(t):
                        dve.wait_ge(out_done, t + 1)
                        dve.wait_ge(added, t + 1)
                        dve.scalar_tensor_tensor(out=core.xs[:, t, :], in0=psX[:, 0:DIM], scalar=gate, in1=core.xs[:, t, :],
                                                 op0=ALU.mult, op1=ALU.add).then_inc(part_added, 1)

                normalise(0, 0)
                normalise(1, 1)
                pipelined(dve, step, -1, TILES + 1, 3, 5)
                dve.wait_ge(part_added, TILES)


F1 = 704
F1C = (F1 + P - 1) // P


def phase_bit_weights(core, gu_dram, down_dram, guT, downT, mu):
    nc = core.nc
    loaded, summed, total, chain, cut, turned, copied, made = (core.sem("bw_" + k) for k in ("l", "s", "t", "c", "q", "tr", "cp", "mk"))
    RG = 2 * F1 // P
    with ExitStack() as ctx:
        wg = core.sb(ctx, "bw_wg", [P, RG, DIM], F32)
        wd = core.sb(ctx, "bw_wd", [P, KC, F1], F32)
        junk = core.sb(ctx, "bw_junk", [P, RG, DIM], F32)
        tg = core.sb(ctx, "bw_tg", [P, RG, DIM], BF16)
        td = core.sb(ctx, "bw_td", [P, KC, F1], BF16)
        part = core.sb(ctx, "bw_part", [P, 2], F32)
        inv = core.sb(ctx, "bw_inv", [P, 2], F32)
        ones = core.sb(ctx, "bw_ones", [P, P], F32)
        ident16 = core.sb(ctx, "bw_id", [P, P], BF16)
        psA = core.ps(ctx, "bw_psA", [P, 512])
        psB = [core.ps(ctx, f"bw_psB{i}", [P, KC * P], BF16) for i in range(2)]
        with nc.Block() as block:
            @block.sync
            def _(sp):
                sp.dma_start(wg[:, :, :], gu_dram.rearrange("(o p) i -> p o i", p=P)).then_inc(loaded, 16)
                sp.dma_start(wd[:, :, :], down_dram.rearrange("(o p) i -> p o i", p=P)).then_inc(loaded, 16)

            @block.gpsimd
            def _(pool):
                pool.memset(ones[:, :], 1.0).then_inc(made, 1)
                pool.tensor_copy(ident16[:, :], core.ident[:, :]).then_inc(made, 1)

            @block.scalar
            def _(act):
                act.wait_ge(loaded, 32)
                act.activation(junk[:, :, :], wg[:, :, :], ACT.Abs, accum_out=part[:, 0:1]).then_inc(summed, 1)
                act.wait_ge(summed, 1)
                act.activation(junk[:, 0:KC * F1 // DIM + 1, :].rearrange("p o i -> p (o i)")[:, 0:KC * F1],
                               wd[:, :, :].rearrange("p o i -> p (o i)"), ACT.Abs, accum_out=part[:, 1:2]).then_inc(summed, 1)

            def turns():
                for o in range(RG):
                    yield [(guT[:, k, o * P:(o + 1) * P], tg[:, o, k * P:(k + 1) * P], P) for k in range(KC)]
                for c in range(F1C):
                    rows = min(P, F1 - c * P)
                    yield [(downT[0:rows, c, k * P:(k + 1) * P], td[:, k, c * P:c * P + rows], rows) for k in range(KC)]

            @block.tensor
            def _(pe):
                pe.wait_ge(summed, 2)
                pe.wait_ge(made, 2)
                pe.matmul(psA[:, 0:2], ones[:, :], part[:, :], start=True, stop=True).then_inc(total, 1)
                pe.wait_ge(cut, 2)
                for n, group in enumerate(turns()):
                    if n >= 2:
                        pe.wait_ge(copied, n - 1)
                    for k, (_, src, rows) in enumerate(group):
                        ins = pe.transpose(psB[n % 2][0:rows, k * P:(k + 1) * P], src, ident16[:, :])
                    ins.then_inc(turned, 1)

            @block.vector
            def _(dve):
                dve.wait_ge(total, 1)
                c = Chain(dve, chain)
                c.link(dve.tensor_scalar(mu[:, 0:1], psA[:, 0:1], 1.0 / (2 * F1 * DIM), 1e-5, ALU.mult, ALU.max))
                c.link(dve.tensor_scalar(mu[:, 1:2], psA[:, 1:2], 1.0 / (F1 * DIM), 1e-5, ALU.mult, ALU.max))
                c.link(dve.reciprocal(inv[:, :], mu[:, 0:2]))
                for m, (w, t) in enumerate(((wg, tg), (wd, td))):
                    c.link(dve.tensor_scalar(w[:, :, :], w[:, :, :], inv[:, m:m + 1], ROUND_MAGIC, ALU.mult, ALU.add))
                    c.link(dve.tensor_scalar(w[:, :, :], w[:, :, :], ROUND_MAGIC, 1.0, ALU.subtract, ALU.min))
                    dve.tensor_scalar(t[:, :, :], w[:, :, :], -1.0, None, ALU.max).then_inc(cut, 1)
                for n, group in enumerate(turns()):
                    dve.wait_ge(turned, n + 1)
                    for k, (dst, _, rows) in enumerate(group):
                        ins = dve.tensor_copy(dst, psB[n % 2][0:rows, k * P:(k + 1) * P])
                    ins.then_inc(copied, 1)
                dve.wait_ge(copied, RG + F1C)


def phase_bit_inputs(core, norm_w, qT_all, sg_all, mu):
    nc = core.nc
    G = 4
    loaded, based, powed, chain, quantised, turned, copied, made, maxed = (
        core.sem("bi_" + k) for k in ("l", "b", "p", "c", "q", "t", "cp", "mk", "mx"))
    with ExitStack() as ctx:
        wb = core.sb(ctx, "bi_w", [P, DIM], F32)
        rr = core.sb(ctx, "bi_rr", [P, TILES], F32)
        tmp = core.sb(ctx, "bi_tmp", [P, 2, TILES], F32)
        z = core.sb(ctx, "bi_z", [P, G, DIM], F32)
        za = core.sb(ctx, "bi_za", [P, G, DIM], F32)
        am = core.sb(ctx, "bi_am", [P, G], F32)
        s1 = core.sb(ctx, "bi_s1", [P, G], F32)
        q = core.sb(ctx, "bi_q", [P, G, DIM], BF16)
        ident16 = core.sb(ctx, "bi_id", [P, P], BF16)
        psT = core.ps(ctx, "bi_psT", [P, G * KC * P], BF16)
        with nc.Block() as block:
            @block.sync
            def _(sp):
                sp.dma_start(wb[:, :], norm_w.rearrange("(a n) -> a n", a=1).broadcast_to([P, DIM])).then_inc(loaded, 16)

            @block.gpsimd
            def _(pool):
                pool.tensor_copy(ident16[:, :], core.ident[:, :]).then_inc(made, 1)
                pool.wait_ge(based, 1)
                pool.tensor_tensor(tmp[:, 1, :], tmp[:, 0, :], core.half[:, 0:TILES], ALU.pow).then_inc(powed, 1)

            @block.tensor
            def _(pe):
                pe.wait_ge(made, 1)
                @looped(pe, TILES // G)
                def _(i):
                    pe.wait_ge(quantised, i + 1)
                    wait_count(pe, copied, i)
                    for g in range(G):
                        for k in range(KC):
                            at = (g * KC + k) * P
                            ins = pe.transpose(psT[:, at:at + P], q[:, g, k * P:(k + 1) * P], ident16[:, :])
                    ins.then_inc(turned, 1)

            @block.scalar
            def _(act):
                @looped(act, TILES // G)
                def _(i):
                    act.wait_ge(turned, i + 1)
                    act.activation(qT_all[:, bass.ds(i * G, G), :, :], psT[:, :].rearrange("p (g k c) -> p g k c", g=G, k=KC), ACT.Copy).then_inc(copied, 1)
                act.wait_ge(copied, TILES // G)

            @block.vector
            def _(dve):
                c = Chain(dve, chain)
                c.link(dve.tensor_tensor(tmp[:, 0, :], core.rstd[:, :], core.rstd[:, :], ALU.mult))
                c.link(dve.tensor_tensor(tmp[:, 0, :], tmp[:, 0, :], core.mv[:, :, 1], ALU.mult))
                dve.tensor_scalar(tmp[:, 0, :], tmp[:, 0, :], 1e-5, None, ALU.add).then_inc(based, 1)
                dve.wait_ge(powed, 1)
                c.link(dve.tensor_tensor(rr[:, :], tmp[:, 1, :], core.rstd[:, :], ALU.mult))
                dve.wait_ge(loaded, 16)
                @looped(dve, TILES // G)
                def _(i):
                    c2 = Chain(dve, chain, i, 7, base=3)
                    for g in range(G):
                        ins = dve.tensor_scalar(z[:, g, :], core.xs[:, i * G + g, :], core.mv[:, i * G + g, 0:1],
                                                rr[:, bass.ds(i * G + g, 1)], ALU.subtract, ALU.mult)
                    c2.link(ins)
                    c2.link(dve.tensor_tensor(z[:, :, :], z[:, :, :], wb[:, :].rearrange("p (a c) -> p a c", a=1).broadcast_to([P, G, DIM]), ALU.mult))
                    c2.link(dve.tensor_reduce(am[:, :], z[:, :, :], AX_X, ALU.max, apply_absolute_value=True))
                    c2.link(dve.tensor_scalar(am[:, :], am[:, :], 1e-5, 1.0 / 127.0, ALU.max, ALU.mult))
                    c2.link(dve.reciprocal(s1[:, :], am[:, :]))
                    for g in range(G):
                        ins = dve.tensor_scalar(z[:, g, :], z[:, g, :], s1[:, g:g + 1], ROUND_MAGIC, ALU.mult, ALU.add)
                    c2.link(ins)
                    wait_count(dve, turned, i)
                    dve.tensor_scalar(q[:, :, :], z[:, :, :], ROUND_MAGIC, None, ALU.subtract).then_inc(quantised, 1)
                    dve.wait_ge(quantised, i + 1)
                    c2.link(dve.tensor_scalar(sg_all[:, bass.ds(i * G, G)], am[:, :], mu[:, 0:1], None, ALU.mult))
                    c2.close()


def phase_bit_ffn(core, qT_all, sg_all, guT, downT, mu, gate):
    nc = core.nc
    n = "bf_"
    HALF = F1 // 2
    gu_done, relued, squared, u_read, maxed, quantised, turned, copied, down_done, added, chain, cubed, made = (
        core.sem(n + k) for k in ("gu", "re", "sq", "ur", "mx", "q", "t", "c", "d", "a", "ch", "cu", "mk"))
    with ExitStack() as ctx:
        rg = core.sb(ctx, n + "rg", [P, 2, HALF], F32)
        h = core.sb(ctx, n + "h", [P, 2, 2, HALF], F32)
        q = core.sb(ctx, n + "q", [P, 2, F1], BF16)
        hT = core.sb(ctx, n + "hT", [P, 2, F1C, P], BF16)
        sg3 = core.sb(ctx, n + "sg3", [P, TILES], F32)
        isg3 = core.sb(ctx, n + "isg3", [P, TILES], F32)
        sm = core.sb(ctx, n + "sm", [P, 2, 4], F32)
        ident16 = core.sb(ctx, n + "id", [P, P], BF16)
        psG = core.ps(ctx, n + "psG", [P, 4, 512])
        psT = core.ps(ctx, n + "psT", [P, 1024], BF16)
        psD = core.ps(ctx, n + "psD", [P, 512])
        with nc.Block() as block:
            @block.gpsimd
            def _(pool):
                pool.tensor_copy(ident16[:, :], core.ident[:, :]).then_inc(made, 1)

            @block.tensor
            def _(pe):
                pe.wait_ge(made, 1)

                def step(s, v):
                    t, u = s + 1, (v + 1) % 2
                    if valid(t):
                        wait_count(pe, relued, t)
                        for b in range(4):
                            if b == 2:
                                wait_count(pe, u_read, t)
                            for k in range(KC):
                                ins = pe.matmul(psG[:, b, 0:HALF], qT_all[:, t, k, :], guT[:, k, b * HALF:(b + 1) * HALF],
                                                start=(k == 0), stop=(k == KC - 1))
                            if b % 2:
                                ins.then_inc(gu_done, 1)
                    t, u = s, v
                    if valid(t):
                        pe.wait_ge(quantised, t + 1)
                        wait_count(pe, copied, t * 2)
                        for c in range(F1C):
                            rows = min(P, F1 - c * P)
                            ins = pe.transpose(psT[0:rows, c * P:(c + 1) * P], q[:, u, c * P:c * P + rows], ident16[:, :])
                        ins.then_inc(turned, 1)
                        pe.wait_ge(copied, t * 2 + 2)
                        wait_count(pe, added, t)
                        for c in range(F1C):
                            rows = min(P, F1 - c * P)
                            ins = pe.matmul(psD[:, 0:DIM], hT[0:rows, u, c, :], downT[0:rows, c, :], start=(c == 0), stop=(c == F1C - 1))
                        ins.then_inc(down_done, 1)

                pipelined(pe, step, -1, TILES, 3, 2)

            @block.scalar
            def _(act):
                def step(s, v):
                    t, u = s + 1, (v + 1) % 2
                    if valid(t):
                        act.wait_ge(gu_done, t * 2 + 1)
                        wait_count(act, squared, t)
                        act.activation(rg[:, :, :], psG[:, 0:2, 0:HALF], ACT.Relu).then_inc(relued, 1)
                        act.wait_ge(relued, t + 1)
                        wait_count(act, quantised, t - 1)
                        act.activation(h[:, u, :, :], rg[:, :, :], ACT.Square).then_inc(squared, 1)
                    t, u = s, v
                    if valid(t):
                        act.wait_ge(turned, t + 1)
                        wait_count(act, down_done, t - 1)
                        act.activation(hT[:, u, 0:F1C - 1, :], psT[:, 0:(F1C - 1) * P].rearrange("p (c d) -> p c d", d=P), ACT.Copy).then_inc(copied, 1)
                        act.activation(hT[0:64, u, F1C - 1, :], psT[0:64, (F1C - 1) * P:F1C * P], ACT.Copy).then_inc(copied, 1)

                pipelined(act, step, -1, TILES, 3, 2)

            @block.vector
            def _(dve):
                c = Chain(dve, cubed)
                c.link(dve.tensor_tensor(sg3[:, :], sg_all[:, :], sg_all[:, :], ALU.mult))
                c.link(dve.tensor_tensor(sg3[:, :], sg3[:, :], sg_all[:, :], ALU.mult))

                def step(s, v):
                    t, u = s, v
                    if valid(t):
                        PER = 6
                        k0 = t * PER

                        def link(ins, k):
                            ins.then_inc(chain, 1)
                            dve.wait_ge(chain, k0 + k)

                        dve.wait_ge(gu_done, t * 2 + 2)
                        dve.wait_ge(squared, t + 1)
                        dve.tensor_tensor(h[:, u, :, :], psG[:, 2:4, 0:HALF], h[:, u, :, :], ALU.mult).then_inc(u_read, 1)
                        dve.wait_ge(u_read, t + 1)
                        link(dve.tensor_reduce(sm[:, u, 0:1], h[:, u, :, :].rearrange("p a c -> p (a c)"), AX_X, ALU.max, apply_absolute_value=True), 1)
                        link(dve.tensor_scalar(sm[:, u, 1:2], sm[:, u, 0:1], sg3[:, bass.ds(t, 1)], 1e-5, ALU.mult, ALU.max), 2)
                        link(dve.tensor_scalar(sm[:, u, 1:2], sm[:, u, 1:2], 1.0 / 127.0, None, ALU.mult), 3)
                        link(dve.reciprocal(sm[:, u, 2:3], sm[:, u, 1:2]), 4)
                        link(dve.tensor_scalar(sm[:, u, 2:3], sm[:, u, 2:3], sg3[:, bass.ds(t, 1)], None, ALU.mult), 5)
                        link(dve.tensor_scalar(h[:, u, :, :], h[:, u, :, :], sm[:, u, 2:3], ROUND_MAGIC, ALU.mult, ALU.add), 6)
                        wait_count(dve, turned, t - 1)
                        dve.tensor_scalar(q[:, u, :], h[:, u, :, :].rearrange("p a c -> p (a c)"), ROUND_MAGIC, None, ALU.subtract).then_inc(quantised, 1)
                        dve.tensor_scalar(sm[:, u, 3:4], sm[:, u, 1:2], mu[:, 1:2], gate, ALU.mult, ALU.mult).then_inc(maxed, 1)
                    t, u = s - 1, (v + 1) % 2
                    if valid(t):
                        dve.wait_ge(down_done, t + 1)
                        dve.wait_ge(maxed, t + 1)
                        dve.scalar_tensor_tensor(out=core.xs[:, t, :], in0=psD[:, 0:DIM], scalar=sm[:, u, 3:4], in1=core.xs[:, t, :],
                                                 op0=ALU.mult, op1=ALU.add).then_inc(added, 1)

                pipelined(dve, step, 0, TILES + 1, 2, 1)
                dve.wait_ge(added, TILES)


def phase_mix(core, name, amplitudes, expert_scale, mix):
    nc = core.nc
    E, K = 128, 8
    loaded, chain = core.sem(name + "_l"), core.sem(name + "_c")
    with ExitStack() as ctx:
        a = core.sb(ctx, name + "_a", [E, K, 2], F32)
        es = core.sb(ctx, name + "_es", [E, 1], F32)
        p = core.sb(ctx, name + "_p", [E, K], F32)
        s = core.sb(ctx, name + "_s", [E, 1], F32)
        with nc.Block() as block:
            @block.sync
            def _(sp):
                sp.dma_start(a[:, :, :], amplitudes).then_inc(loaded, 16)
                sp.dma_start(es[:, :], expert_scale.rearrange("(e a) -> e a", a=1)).then_inc(loaded, 16)

            @block.vector
            def _(dve):
                dve.wait_ge(loaded, 32)
                c = Chain(dve, chain)
                c.link(dve.tensor_tensor(a[:, :, :], a[:, :, :], a[:, :, :], ALU.mult))
                c.link(dve.tensor_tensor(p[:, :], a[:, :, 0], a[:, :, 1], ALU.add))
                c.link(dve.tensor_reduce(s[:, :], p[:, :], AX_X, ALU.add))
                c.link(dve.tensor_scalar(s[:, :], s[:, :], 1e-8, None, ALU.add))
                c.link(dve.reciprocal(s[:, :], s[:, :]))
                c.link(dve.tensor_scalar(mix[:, :], p[:, :], s[:, 0:1], es[:, 0:1], ALU.mult, ALU.mult))


def phase_basis_ffn(core, yT_all, score_all, mix, w_gate, w_up, w_down, s_gate, s_up, s_down, gate):
    nc = core.nc
    K, I, E = 8, 128, 128
    n = "bs_"
    loaded = core.sem(n + "l")
    fetched = [core.sem(f"{n}f{u}") for u in range(2)]
    sc_ready, small_done, small_copied, c_done, c_ready = (core.sem(n + k) for k in ("scr", "sm", "smc", "cd", "cr"))
    g_done, u_done, s_done, tanhed, glued, mixed, m_turned, m_copied, down_done, added, chain, basised = (
        core.sem(n + k) for k in ("g", "u", "s", "th", "gl", "mx", "mt", "mc", "d", "a", "ch", "bb"))
    with ExitStack() as ctx:
        sb, ps = core.sb, core.ps
        wg = sb(ctx, n + "wg", [P, KC, K * I], F32)
        wu = sb(ctx, n + "wu", [P, KC, K * I], F32)
        ws = sb(ctx, n + "ws", [P, KC, 2, DIM], F32)
        wd = sb(ctx, n + "wd", [P, 1 + KC, DIM], F32)
        yT = sb(ctx, n + "yT", [P, 2, KC, P], F32)
        sc = sb(ctx, n + "sc", [P, 2, E], F32)
        scT = sb(ctx, n + "scT", [P, 2, E], F32)
        cf = sb(ctx, n + "cf", [P, 2, K], F32)
        th = sb(ctx, n + "th", [P, K * I], F32)
        ths = sb(ctx, n + "ths", [P, DIM], F32)
        b = sb(ctx, n + "b", [P, K, I], F32)
        m = sb(ctx, n + "m", [P, 2, 3, P], F32)
        mT = sb(ctx, n + "mT", [P, 2, 3, P], F32)
        psG = ps(ctx, n + "psG", [P, 2, 512])
        psU = ps(ctx, n + "psU", [P, 2, 512])
        psS = ps(ctx, n + "psS", [P, 512])
        psT = ps(ctx, n + "psT", [P, 512])
        psO = ps(ctx, n + "psO", [P, 512])
        psC = ps(ctx, n + "psC", [P, 512])
        with nc.Block() as block:
            @block.sync
            def _(sp):
                for dst, src in ((wg[:, :, :], w_gate), (wu[:, :, :], w_up), (ws[:, :, 0, :], s_gate), (ws[:, :, 1, :], s_up),
                                 (wd[:, 1:3, :], s_down)):
                    sp.dma_start(dst, src.rearrange("(k p) o -> p k o", p=P)).then_inc(loaded, 16)
                sp.dma_start(wd[:, 0, :], w_down).then_inc(loaded, 16)

                def step(s, v):
                    wait_count(sp, u_done, s - 1)
                    sp.dma_start(yT[:, v, :, :].rearrange("p k c -> p (k c)"), yT_all[s]).then_inc(fetched[v], 16)

                pipelined(sp, step, 0, TILES, 2, 0)

            @block.gpsimd
            def _(pool):
                def step(s, v):
                    wait_count(pool, small_done, s - 1)
                    pool.tensor_copy(sc[:, v, :], score_all[:, s, :]).then_inc(sc_ready, 1)

                pipelined(pool, step, 0, TILES, 2, 0)

            @block.tensor
            def _(pe):
                pe.wait_ge(loaded, 96)

                def step(s, v, half):
                    t, u = s, v
                    if valid(t):
                        pe.wait_ge(fetched[u], half * 16 + 16)
                        wait_count(pe, glued, t)
                        for c in range(2):
                            for k in range(KC):
                                ins = pe.matmul(psG[:, c, :], yT[:, u, k, :], wg[:, k, c * 512:(c + 1) * 512], start=(k == 0), stop=(k == KC - 1))
                        ins.then_inc(g_done, 1)
                        pe.wait_ge(sc_ready, t + 1)
                        wait_count(pe, c_ready, t)
                        pe.transpose(psC[:, 0:E], sc[:, u, :], core.ident[:, :]).then_inc(small_done, 1)
                    t, u = s - 1, (v + 1) % 2
                    if valid(t):
                        pe.wait_ge(mixed, t * 2 + 2)
                        wait_count(pe, m_copied, t)
                        for k in range(3):
                            ins = pe.transpose(psT[:, k * P:(k + 1) * P], m[:, u, k, :], core.ident[:, :])
                        ins.then_inc(m_turned, 1)
                    t, u = s, v
                    if valid(t):
                        wait_count(pe, mixed, t * 2)
                        for k in range(KC):
                            ins = pe.matmul(psS[:, :], yT[:, u, k, :], ws[:, k, :, :], start=(k == 0), stop=(k == KC - 1))
                        ins.then_inc(s_done, 1)
                        wait_count(pe, basised, t)
                        for c in range(2):
                            for k in range(KC):
                                ins = pe.matmul(psU[:, c, :], yT[:, u, k, :], wu[:, k, c * 512:(c + 1) * 512], start=(k == 0), stop=(k == KC - 1))
                        ins.then_inc(u_done, 1)
                        pe.wait_ge(small_copied, t + 1)
                        pe.matmul(psC[:, 256:256 + K], scT[:, u, :], mix[:, :], start=True, stop=True).then_inc(c_done, 1)
                    t, u = s - 1, (v + 1) % 2
                    if valid(t):
                        pe.wait_ge(m_copied, t + 1)
                        wait_count(pe, added, t)
                        for k in range(3):
                            ins = pe.matmul(psO[:, 0:DIM], mT[:, u, k, :], wd[:, k, :], start=(k == 0), stop=(k == 2))
                        ins.then_inc(down_done, 1)

                for s in range(2):
                    step(s, s, 0)
                with pe.Fori(1, TILES // 2) as j:
                    for v in range(2):
                        step(j * 2 + v, v, j)
                step(TILES, 0, 0)

            @block.scalar
            def _(act):
                def step(s, v):
                    t, u = s, v
                    if valid(t):
                        act.wait_ge(g_done, t + 1)
                        wait_count(act, glued, t)
                        act.activation(th[:, :], psG[:, :, :].rearrange("p b c -> p (b c)"), ACT.Tanh, scale=0.5).then_inc(tanhed, 1)
                        act.wait_ge(small_done, t + 1)
                        wait_count(act, c_done, t - 1)
                        act.activation(scT[:, u, :], psC[:, 0:E], ACT.Copy).then_inc(small_copied, 1)
                    t, u = s - 1, (v + 1) % 2
                    if valid(t):
                        act.wait_ge(m_turned, t + 1)
                        wait_count(act, down_done, t - 1)
                        act.activation(mT[:, u, :, :], psT[:, 0:3 * P].rearrange("p (k c) -> p k c", c=P), ACT.Copy).then_inc(m_copied, 1)
                    t, u = s, v
                    if valid(t):
                        act.wait_ge(s_done, t + 1)
                        act.activation(ths[:, :], psS[:, 0:DIM], ACT.Tanh, scale=0.5).then_inc(tanhed, 1)

                pipelined(act, step, 0, TILES + 1, 2, 1)

            @block.vector
            def _(dve):
                dve.wait_ge(loaded, 96)

                def step(s, v):
                    t, u = s, v
                    if valid(t):
                        def link(ins, k):
                            ins.then_inc(chain, 1)
                            dve.wait_ge(chain, t * 2 + k)

                        dve.wait_ge(tanhed, t * 2 + 1)
                        dve.wait_ge(g_done, t + 1)
                        wait_count(dve, mixed, t * 2)
                        dve.scalar_tensor_tensor(out=b[:, :, :].rearrange("p k i -> p (k i)"), in0=th[:, :], scalar=1.0,
                                                 in1=psG[:, :, :].rearrange("p b c -> p (b c)"), op0=ALU.add, op1=ALU.mult).then_inc(glued, 1)
                        dve.wait_ge(tanhed, t * 2 + 2)
                        link(dve.scalar_tensor_tensor(out=ths[:, :], in0=ths[:, :], scalar=1.0, in1=psS[:, 0:DIM], op0=ALU.add, op1=ALU.mult), 1)
                        wait_count(dve, m_turned, t - 1)
                        dve.scalar_tensor_tensor(out=m[:, u, 1:3, :].rearrange("p k c -> p (k c)"), in0=psS[:, DIM:2 * DIM], scalar=0.5, in1=ths[:, :],
                                                 op0=ALU.mult, op1=ALU.mult).then_inc(mixed, 1)
                    t, u = s - 1, (v + 1) % 2
                    if valid(t):
                        dve.wait_ge(down_done, t + 1)
                        dve.scalar_tensor_tensor(out=core.xs[:, t, :], in0=psO[:, 0:DIM], scalar=gate, in1=core.xs[:, t, :],
                                                 op0=ALU.mult, op1=ALU.add).then_inc(added, 1)
                    t, u = s, v
                    if valid(t):
                        dve.wait_ge(u_done, t + 1)
                        dve.wait_ge(glued, t + 1)
                        dve.scalar_tensor_tensor(out=b[:, :, :].rearrange("p k i -> p (k i)"), in0=psU[:, :, :].rearrange("p b c -> p (b c)"), scalar=0.5,
                                                 in1=b[:, :, :].rearrange("p k i -> p (k i)"), op0=ALU.mult, op1=ALU.mult).then_inc(basised, 1)
                        dve.wait_ge(c_done, t + 1)
                        dve.tensor_copy(cf[:, u, :], psC[:, 256:256 + K]).then_inc(c_ready, 1)
                        dve.wait_ge(c_ready, t + 1)
                        dve.wait_ge(basised, t + 1)
                        link(dve.tensor_tensor(b[:, :, :], b[:, :, :], cf[:, u, :].rearrange("p (k a) -> p k a", a=1).broadcast_to([P, K, I]), ALU.mult), 2)
                        dve.tensor_reduce(m[:, u, 0, :], b[:, :, :].rearrange("p k i -> p i k"), AX_X, ALU.add).then_inc(mixed, 1)

                pipelined(dve, step, 0, TILES + 1, 2, 1)
                dve.wait_ge(added, TILES)




def phase_slots(core, name, E, K, lg_all, weight, slot, gate, capacity=None, expert_of=None):
    nc = core.nc
    T = TILES
    all_experts = capacity is not None
    chain, found, exped, posed, ioted, tops, indices = (
        core.sem(name + k) for k in ("_ch", "_fd", "_ex", "_ps", "_io", "_tp", "_ix"))
    with ExitStack() as ctx:
        sb = core.sb
        top = sb(ctx, name + "_top", [P, T, 8], F32)
        idx = sb(ctx, name + "_idx", [P, T, 8], U32)
        idxf = sb(ctx, name + "_idxf", [P, T, 8], F32)
        ex = sb(ctx, name + "_exs", [P, T, K], F32)
        exall = sb(ctx, name + "_exall", [P, T, E], F32)
        den = sb(ctx, name + "_den", [P, 2, T], F32)
        hot = sb(ctx, name + "_hot", [P, K, T, E], F32)
        mask = sb(ctx, name + "_mask", [P, T, E], F32)
        tmp = sb(ctx, name + "_tmp", [P, T, E], F32)
        cum = sb(ctx, name + "_cum", [P, T, E], F32)
        pos = sb(ctx, name + "_pos", [P, T, K], F32)
        kept = sb(ctx, name + "_kept", [P, T, K], F32)
        iota = sb(ctx, name + "_iota", [P, E], F32)
        before = sb(ctx, name + "_before", [P, P], F32)
        ones = sb(ctx, name + "_ones", [P, P], F32)
        tiles = sb(ctx, name + "_tiles", [P, 3, E], F32)
        tile_no = sb(ctx, name + "_tn", [P, T0], F32)
        passed = sb(ctx, name + "_pd", [P, T0, E], F32)
        psR = core.ps(ctx, name + "_psR", [P, 512])
        psC = core.ps(ctx, name + "_psC", [P, 512])
        io_b = iota[:, :].rearrange("p (a e) -> p a e", a=1).broadcast_to([P, T, E])

        def per_tile(ap, n):
            return ap.rearrange("p (t a) -> p t a", a=1).broadcast_to([P, T, n])

        with nc.Block() as block:
            @block.gpsimd
            def _(pool):
                pool.iota(iota[:, :], pattern=[[1, E]], base=0, channel_multiplier=0,
                          allow_small_or_imprecise_dtypes=True).then_inc(ioted, 1)
                pool.iota(tile_no[:, :], pattern=[[1, T0]], base=0, channel_multiplier=0,
                          allow_small_or_imprecise_dtypes=True).then_inc(ioted, 1)
                pool.memset(before[:, :], 1.0).then_inc(ioted, 1)
                pool.memset(ones[:, :], 1.0).then_inc(ioted, 1)
                pool.wait_ge(ioted, 4)
                pool.affine_select(out=before[:, :], in_=before[:, :], compare_op=ALU.is_gt, fill=0.0,
                                   base=0, pattern=[[1, P]], channel_multiplier=-1).then_inc(ioted, 1)

            @block.scalar
            def _(act):
                act.wait_ge(chain, 1)
                act.activation(ex[:, :, :], ex[:, :, :], ACT.Exp).then_inc(exped, 1)
                if all_experts:
                    act.wait_ge(chain, 2)
                    act.activation(exall[:, :, :], exall[:, :, :], ACT.Exp).then_inc(exped, 1)

            @block.tensor
            def _(pe):
                pe.wait_ge(posed, 1)
                pe.wait_ge(ioted, 5)
                pe.matmul(psR[:, 0:T * E], before[:, :], mask[:, :, :], start=True, stop=True).then_inc(found, 1)
                pe.matmul(psC[:, 0:T * E], ones[:, :], mask[:, :, :], start=True, stop=True).then_inc(found, 1)

            @block.vector
            def _(dve):
                for t in range(T):
                    dve.max(top[:, t, :], lg_all[:, t, :]).then_inc(tops, 1)
                for t in range(T):
                    dve.wait_ge(tops, t + 1)
                    dve.max_index(idx[:, t, :], top[:, t, :], lg_all[:, t, :]).then_inc(indices, 1)
                c = Chain(dve, chain)
                c.link(dve.tensor_tensor(ex[:, :, :], top[:, :, 0:K], per_tile(top[:, :, 0], K), ALU.subtract))
                if all_experts:
                    c.link(dve.tensor_tensor(exall[:, :, :], lg_all[:, :, :], per_tile(top[:, :, 0], E), ALU.subtract))
                dve.wait_ge(indices, T)
                c.link(dve.tensor_copy(idxf[:, :, :], idx[:, :, :]))
                dve.wait_ge(ioted, 2)
                for k in range(K):
                    ins = dve.tensor_tensor(hot[:, k, :, :], io_b, per_tile(idxf[:, :, k], E), ALU.is_equal)
                c.link(ins)
                c.link(dve.tensor_tensor(mask[:, :, :], hot[:, 0, :, :], hot[:, 1, :, :], ALU.add))
                for k in range(2, K):
                    c.link(dve.tensor_tensor(mask[:, :, :], mask[:, :, :], hot[:, k, :, :], ALU.add))
                dve.sem_inc(posed, 1)
                dve.wait_ge(exped, 2 if all_experts else 1)
                c.link(dve.tensor_reduce(den[:, 0, :], exall[:, :, :] if all_experts else ex[:, :, :], AX_X, ALU.add))
                c.link(dve.reciprocal(den[:, 1, :], den[:, 0, :]))
                c.link(dve.tensor_tensor(ex[:, :, :], ex[:, :, :], per_tile(den[:, 1, :], K), ALU.mult))
                c.link(dve.tensor_scalar(weight[:, :, :], ex[:, :, :], gate, None, ALU.mult))
                dve.wait_ge(found, 2)
                c.link(dve.tensor_copy(tmp[:, :, :], psC[:, 0:T * E].rearrange("p (t e) -> p t e", t=T)))
                c.link(dve.memset(exall[:, :, :], 1.0))
                for e in range(E):
                    ins = dve.tensor_tensor_scan(cum[:, :, e], exall[:, :, e], tmp[:, :, e], 0.0, ALU.mult, ALU.add)
                c.link(ins)
                if capacity is None:
                    c.link(dve.tensor_scalar(tiles[:, 0, :], cum[:, T - 1, :], 1.0 / P, (P - 1.0) / P - 0.5 + 0.5 / P, ALU.mult, ALU.add))
                    c.link(dve.tensor_scalar(tiles[:, 0, :], tiles[:, 0, :], ROUND_MAGIC, ROUND_MAGIC, ALU.add, ALU.subtract))
                    c.link(dve.tensor_tensor_scan(tiles[:, 1, :], exall[:, 0, :], tiles[:, 0, :], 0.0, ALU.mult, ALU.add))
                    c.link(dve.tensor_tensor(tiles[:, 2, :], tiles[:, 1, :], tiles[:, 0, :], ALU.subtract))
                    c.link(dve.tensor_scalar(tiles[:, 2, :], tiles[:, 2, :], float(P), None, ALU.mult))
                    c.link(dve.tensor_tensor(passed[:, :, :], tile_no[:, :].rearrange("p (t a) -> p t a", a=1).broadcast_to([P, T0, E]),
                                             tiles[:, 1, :].rearrange("p (a e) -> p a e", a=1).broadcast_to([P, T0, E]), ALU.is_ge))
                    c.link(dve.tensor_reduce(tile_no[:, :], passed[:, :, :], AX_X, ALU.add))
                    c.link(dve.tensor_scalar(expert_of[:, :], tile_no[:, :], E - 1.0, None, ALU.min))
                else:
                    c.link(dve.tensor_scalar(tiles[:, 2, :], iota[:, :], float(capacity), None, ALU.mult))
                c.link(dve.tensor_tensor(cum[:, :, :], cum[:, :, :], tmp[:, :, :], ALU.subtract))
                c.link(dve.tensor_tensor(cum[:, :, :], psR[:, 0:T * E].rearrange("p (t e) -> p t e", t=T), cum[:, :, :], ALU.add))
                if capacity is not None:
                    for k in range(K):
                        c.link(dve.tensor_tensor(tmp[:, :, :], hot[:, k, :, :], cum[:, :, :], ALU.mult))
                        c.link(dve.tensor_reduce(pos[:, :, k], tmp[:, :, :], AX_X, ALU.add))
                    c.link(dve.tensor_scalar(kept[:, :, :], pos[:, :, :], float(capacity), None, ALU.is_lt))
                    c.link(dve.tensor_tensor(weight[:, :, :], weight[:, :, :], kept[:, :, :], ALU.mult))
                c.link(dve.tensor_tensor(cum[:, :, :], cum[:, :, :], tiles[:, 2, :].rearrange("p (a e) -> p a e", a=1).broadcast_to([P, T, E]), ALU.add))
                for k in range(K):
                    c.link(dve.tensor_tensor(tmp[:, :, :], hot[:, k, :, :], cum[:, :, :], ALU.mult))
                    c.link(dve.tensor_reduce(pos[:, :, k], tmp[:, :, :], AX_X, ALU.add))
                if capacity is not None:
                    c.link(dve.tensor_scalar(kept[:, :, :], kept[:, :, :], -float(D0), float(D0), ALU.mult, ALU.add))
                    c.link(dve.tensor_tensor(pos[:, :, :], pos[:, :, :], kept[:, :, :], ALU.add))
                c.link(dve.tensor_copy(slot[:, :, :], pos[:, :, :]))


def phase_scatter(core, name, K, slot, rows_in, limit):
    nc = core.nc
    ready, passed = core.sem(name + "_r"), core.sem(name + "_p")
    sent = [core.lasting_sem(f"{name}_s{u}") for u in range(2)]
    with ExitStack() as ctx:
        y = core.sb(ctx, name + "_y", [P, 2, DIM], F32)
        index = [core.sb(ctx, f"{name}_i{u}", [P, K], U32) for u in range(2)]
        with nc.Block() as block:
            @block.vector
            def _(dve):
                @looped(dve, TILES // 2)
                def _(i):
                    for u in range(2):
                        t = i * 2 + u
                        wait_count(dve, sent[u], i * (16 * K))
                        dve.tensor_copy(index[u][:, :], slot[:, t, :])
                        dve.tensor_scalar(y[:, u, :], core.xs[:, t, :], core.mv[:, t, 0:1],
                                          core.rstd[:, bass.ds(t, 1)], ALU.subtract, ALU.mult).then_inc(ready, 1)

            @block.gpsimd
            def _(pool):
                pool.wait_ge(core.rows_zeroed, 16 * ZERO_DMAS)
                @looped(pool, TILES // 2)
                def _(i):
                    for u in range(2):
                        pool.wait_ge(ready, i * 2 + (u + 1))
                        pool.sem_inc(passed, 1)
                        for k in range(K):
                            pool.indirect_dma_start(out=rows_in[:, :], out_offset=bass.IndirectOffsetOnAxis(ap=index[u][:, k:k + 1], axis=0),
                                                    in_=y[:, u, :], in_offset=None, bounds_check=limit - 1, oob_is_err=False).then_inc(sent[u], 16)
                for u in range(2):
                    pool.wait_ge(sent[u], 16 * K * (TILES // 2))


def phase_combine(core, name, K, slot, weight, rows_out, limit):
    nc = core.nc
    ready, passed, added = (core.sem(name + k) for k in ("_r", "_p", "_a"))
    got = [core.lasting_sem(f"{name}_g{u}") for u in range(2)]
    with ExitStack() as ctx:
        rows = [[core.sb(ctx, f"{name}_rows{u}_{k}", [P, DIM], F32) for k in range(K)] for u in range(2)]
        index = [core.sb(ctx, f"{name}_i{u}", [P, K], U32) for u in range(2)]
        with nc.Block() as block:
            @block.vector
            def _(dve):
                for u in range(2):
                    for k in range(K):
                        dve.memset(rows[u][k][:, :], 0.0)
                for u in range(2):
                    dve.tensor_copy(index[u][:, :], slot[:, u, :]).then_inc(ready, 1)

                def step(i, last):
                    for u in range(2):
                        t = i * 2 + u
                        dve.wait_ge(got[u], i * (16 * K) + 16 * K)
                        for k in range(K):
                            dve.scalar_tensor_tensor(out=core.xs[:, t, :], in0=rows[u][k][:, :], scalar=weight[:, t, k:k + 1],
                                                     in1=core.xs[:, t, :], op0=ALU.mult, op1=ALU.add).then_inc(added, 1)
                            dve.wait_ge(added, i * (2 * K) + (K * u + k + 1))
                        if not last:
                            dve.tensor_copy(index[u][:, :], slot[:, t + 2, :]).then_inc(ready, 1)

                with dve.Fori(0, TILES // 2 - 1) as i:
                    step(i, False)
                step(TILES // 2 - 1, True)

            @block.gpsimd
            def _(pool):
                @looped(pool, TILES // 2)
                def _(i):
                    for u in range(2):
                        pool.wait_ge(ready, i * 2 + (u + 1))
                        pool.sem_inc(passed, 1)
                        for k in range(K):
                            pool.indirect_dma_start(out=rows[u][k][:, :], out_offset=None, in_=rows_out[0:limit, :],
                                                    in_offset=bass.IndirectOffsetOnAxis(ap=index[u][:, k:k + 1], axis=0),
                                                    bounds_check=limit - 1, oob_is_err=False).then_inc(got[u], 16)


def phase_experts0(core, rows_in, rows_out, expert_of, gate_up, gate_up_b, down, down_b):
    nc = core.nc
    E, D2, D = 16, 2 * DIM, DIM
    n = "e0_"
    loaded = core.sem(n + "loaded")
    fetched = [core.sem(f"{n}f{u}") for u in range(2)]
    stored = [core.sem(f"{n}s{u}") for u in range(2)]
    x_turned, x_copied, up_done, biased, clipped, tanhed, glu, acted = (
        core.sem(n + k) for k in ("xt", "xc", "up", "bias", "clip", "tanh", "glu", "act"))
    h_turned, h_copied, down_done, out_ready = (core.sem(n + k) for k in ("ht", "hc", "down", "out"))
    with ExitStack() as ctx:
        sb, ps = core.sb, core.ps
        wgu = sb(ctx, n + "wgu", [P, E, KC, D2], F32)
        wd = sb(ctx, n + "wd", [P, E, KC, D], F32)
        bgu = sb(ctx, n + "bgu", [P, E, D2], F32)
        bd = sb(ctx, n + "bd", [P, E, D], F32)
        xin = sb(ctx, n + "xin", [P, 2, DIM], F32)
        yT = sb(ctx, n + "yT", [P, 2, KC, P], F32)
        gub = sb(ctx, n + "gub", [P, D, 2], F32)
        gcap = sb(ctx, n + "gcap", [P, 2, D], F32)
        ucl = sb(ctx, n + "ucl", [P, 2, D], F32)
        th = sb(ctx, n + "th", [P, 2, D], F32)
        h = sb(ctx, n + "h", [P, 2, D], F32)
        hT = sb(ctx, n + "hT", [P, 2, KC, P], F32)
        out = sb(ctx, n + "out", [P, 2, D], F32)
        psX = ps(ctx, n + "psX", [P, 2, 512])
        psG = ps(ctx, n + "psG", [P, 2, 512])
        psA = ps(ctx, n + "psA", [P, 2, 512])
        psO = ps(ctx, n + "psO", [P, 2, 512])

        def ok(t):
            return not isinstance(t, int) or 0 <= t < T0

        def run(eng, step, first, last, lo, hi):
            for s in range(first, lo):
                step(s, s % 2, 0)
            with eng.Fori(lo // 2, hi // 2) as j:
                for v in range(2):
                    step(j * 2 + v, v, j)
            for s in range(hi, last):
                step(s, s % 2, 0)

        def expert(eng, t):
            at = expert_of[0:1, t:t + 1] if isinstance(t, int) else expert_of[0:1, bass.ds(t, 1)]
            return eng.value_load(at, min_val=0, max_val=E - 1)

        with nc.Block() as block:
            @block.sync
            def _(sp):
                for e in range(E):
                    sp.dma_start(wgu[:, e, :, :], gate_up[e].rearrange("(k p) f -> p k f", p=P)).then_inc(loaded, 16)
                    sp.dma_start(wd[:, e, :, :], down[e].rearrange("(k p) f -> p k f", p=P)).then_inc(loaded, 16)
                sp.dma_start(bgu[:, :, :], gate_up_b.rearrange("(a e) f -> a e f", a=1).broadcast_to([P, E, D2])).then_inc(loaded, 16)
                sp.dma_start(bd[:, :, :], down_b.rearrange("(a e) f -> a e f", a=1).broadcast_to([P, E, D])).then_inc(loaded, 16)

                def step(s, v, j):
                    t, u = s + 2, v
                    if ok(t):
                        wait_count(sp, x_turned, t - 1)
                        sp.dma_start(xin[:, u, :], rows_in[t]).then_inc(fetched[u], 16)
                    t, u = s - 2, v
                    if ok(t):
                        sp.wait_ge(out_ready, t + 1)
                        sp.dma_start(rows_out[t], out[:, u, :]).then_inc(stored[u], 16)

                run(sp, step, -2, T0 + 2, 2, T0 - 2)
                for u in range(2):
                    sp.wait_ge(stored[u], 16 * (T0 // 2))

            @block.tensor
            def _(pe):
                pe.wait_ge(loaded, 16 * (2 * E + 2))

                def step(s, v, j):
                    t, u = s + 2, v
                    if ok(t):
                        half = t // 2 if isinstance(t, int) else j + 1
                        pe.wait_ge(fetched[u], half * 16 + 16)
                        wait_count(pe, x_copied, t - 1)
                        for k in range(KC):
                            ins = pe.transpose(psX[:, u, k * P:(k + 1) * P], xin[:, u, k * P:(k + 1) * P], core.ident[:, :])
                        ins.then_inc(x_turned, 1)
                    t, u = s + 1, (v + 1) % 2
                    if ok(t):
                        e = expert(pe, t)
                        pe.wait_ge(x_copied, t + 1)
                        wait_count(pe, biased, t - 1)
                        for k in range(KC):
                            ins = pe.matmul(psG[:, u, :], yT[:, u, k, :], wgu[:, e, k, :], start=(k == 0), stop=(k == KC - 1))
                        ins.then_inc(up_done, 1)
                    t, u = s, v
                    if ok(t):
                        pe.wait_ge(acted, t + 1)
                        wait_count(pe, h_copied, t - 1)
                        for k in range(KC):
                            ins = pe.transpose(psA[:, u, k * P:(k + 1) * P], h[:, u, k * P:(k + 1) * P], core.ident[:, :])
                        ins.then_inc(h_turned, 1)
                    t, u = s - 1, (v + 1) % 2
                    if ok(t):
                        e = expert(pe, t)
                        pe.wait_ge(h_copied, t + 1)
                        wait_count(pe, out_ready, t - 1)
                        for k in range(KC):
                            ins = pe.matmul(psO[:, u, 0:D], hT[:, u, k, :], wd[:, e, k, :], start=(k == 0), stop=(k == KC - 1))
                        ins.then_inc(down_done, 1)

                run(pe, step, -2, T0 + 1, 2, T0 - 2)

            @block.scalar
            def _(act):
                def step(s, v, j):
                    t, u = s + 2, v
                    if ok(t):
                        act.wait_ge(x_turned, t + 1)
                        wait_count(act, up_done, t - 1)
                        act.activation(yT[:, u, :, :], psX[:, u, 0:KC * P].rearrange("p (k c) -> p k c", k=KC), ACT.Copy).then_inc(x_copied, 1)
                    t, u = s, v
                    if ok(t):
                        act.wait_ge(h_turned, t + 1)
                        wait_count(act, down_done, t - 1)
                        act.activation(hT[:, u, :, :], psA[:, u, 0:KC * P].rearrange("p (k c) -> p k c", k=KC), ACT.Copy).then_inc(h_copied, 1)
                    t, u = s + 1, (v + 1) % 2
                    if ok(t):
                        act.wait_ge(clipped, t + 1)
                        wait_count(act, glu, t - 1)
                        act.activation(th[:, u, :], gcap[:, u, :], ACT.Tanh, scale=0.5 * 1.702).then_inc(tanhed, 1)

                run(act, step, -2, T0, 2, T0 - 2)

            @block.vector
            def _(dve):
                dve.wait_ge(loaded, 16 * (2 * E + 2))

                def step(s, v, j):
                    t, u = s, v
                    if ok(t):
                        dve.wait_ge(tanhed, t + 1)
                        dve.scalar_tensor_tensor(out=gcap[:, u, :], in0=th[:, u, :], scalar=1.0, in1=gcap[:, u, :],
                                                 op0=ALU.add, op1=ALU.mult).then_inc(glu, 1)
                        dve.wait_ge(glu, t + 1)
                        wait_count(dve, h_turned, t - 1)
                        dve.scalar_tensor_tensor(out=h[:, u, :], in0=ucl[:, u, :], scalar=1.0, in1=gcap[:, u, :],
                                                 op0=ALU.add, op1=ALU.mult).then_inc(acted, 1)
                    t, u = s + 1, (v + 1) % 2
                    if ok(t):
                        e = expert(dve, t)
                        dve.wait_ge(up_done, t + 1)
                        wait_count(dve, clipped, t)
                        wait_count(dve, acted, t - 1)
                        dve.tensor_tensor(gub[:, :, :].rearrange("p d a -> p (d a)"), psG[:, u, :], bgu[:, e, :], ALU.add).then_inc(biased, 1)
                        dve.wait_ge(biased, t + 1)
                        dve.tensor_scalar(gcap[:, u, :], gub[:, :, 0], 7.0, None, ALU.min)
                        dve.tensor_scalar(ucl[:, u, :], gub[:, :, 1], 7.0, -7.0, ALU.min, ALU.max).then_inc(clipped, 1)
                    t, u = s - 1, (v + 1) % 2
                    if ok(t):
                        e = expert(dve, t)
                        dve.wait_ge(down_done, t + 1)
                        half = t // 2 if isinstance(t, int) else (j - 1 if v == 0 else j)
                        wait_count(dve, stored[u], half * 16)
                        dve.scalar_tensor_tensor(out=out[:, u, :], in0=psO[:, u, 0:D], scalar=0.5, in1=bd[:, e, :],
                                                 op0=ALU.mult, op1=ALU.add).then_inc(out_ready, 1)

                run(dve, step, -1, T0 + 1, 4, T0 - 2)


def phase_experts3(core, rows_in, rows_out, w1, w2):
    nc = core.nc
    E, F, D = 8, 1024, DIM
    R = 2 * P
    GR = CAPACITY // R
    FC = F // P
    NG = 2 * GR
    n = "e3_"
    w_loaded = [core.sem(f"{n}w{m}") for m in range(2)]
    fetched = [core.sem(f"{n}f{u}") for u in range(2)]
    stored = [core.sem(f"{n}s{u}") for u in range(2)]
    x_turned, x_copied, up_done, relued, down_done, out_ready = (core.sem(n + k) for k in ("xt", "xc", "up", "re", "down", "out"))
    with ExitStack() as ctx:
        sb, ps = core.sb, core.ps
        w1s = sb(ctx, n + "w1", [P, 2, KC, F], F32)
        w2s = sb(ctx, n + "w2", [P, 2, FC, D], F32)
        xin = sb(ctx, n + "xin", [P, 2, 2, DIM], F32)
        yT = sb(ctx, n + "yT", [P, 2, 2, KC, P], F32)
        hT = sb(ctx, n + "hT", [P, 2, FC, R], F32)
        out = sb(ctx, n + "out", [P, 2, 2, D], F32)
        psX = ps(ctx, n + "psX", [P, 2 * KC * P])
        psH = ps(ctx, n + "psH", [P, FC // 2, 512])
        psD = ps(ctx, n + "psD", [P, 2, 512])

        def run(eng, step):
            @looped(eng, E // 2)
            def _(j):
                for g in range(NG):
                    step(j, g)

        with nc.Block() as block:
            @block.scalar
            def _(act):
                for m in range(2):
                    act.dma_start(w1s[:, m, :, :], w1[m].rearrange("(k p) f -> p k f", p=P)).then_inc(w_loaded[m], 16)
                    act.dma_start(w2s[:, m, :, :], w2[m].rearrange("(k p) d -> p k d", p=P)).then_inc(w_loaded[m], 16)

                def step(j, g):
                    i, u = j * NG + g, g % 2
                    act.wait_ge(x_turned, i + 1)
                    wait_count(act, up_done, j * (NG * 4) + (g - 1) * 4)
                    act.activation(yT[:, u, :, :, :], psX[:, :].rearrange("p (t k c) -> p t k c", t=2, k=KC), ACT.Copy).then_inc(x_copied, 1)
                    for b in range(FC // 2):
                        act.wait_ge(up_done, j * (NG * 4) + (g * 4 + b + 1))
                        wait_count(act, down_done, j * NG + (g - 1))
                        act.activation(hT[:, u, 2 * b:2 * b + 2, :], psH[:, b, :].rearrange("p (f c) -> p f c", f=2), ACT.Relu).then_inc(relued, 1)

                run(act, step)

            @block.sync
            def _(sp):
                def load(j, g):
                    i, u = j * NG + g, g % 2
                    wait_count(sp, x_turned, j * NG + (g - 1))
                    sp.dma_start(xin[:, u, :, :], rows_in[bass.ds(i * 2, 2)].rearrange("t p c -> p t c")
                                 if not isinstance(i, int) else rows_in[2 * i:2 * i + 2].rearrange("t p c -> p t c")).then_inc(fetched[u], 16)

                def store(j, g):
                    i, u = j * NG + g, g % 2
                    sp.wait_ge(out_ready, i + 1)
                    rows = rows_out[bass.ds(i * 2, 2)] if not isinstance(i, int) else rows_out[2 * i:2 * i + 2]
                    sp.dma_start(rows.rearrange("t p c -> p t c"), out[:, u, :, :]).then_inc(stored[u], 16)

                def weights(j, m):
                    sp.dma_start(w1s[:, m, :, :], w1[j * 2 + m].rearrange("(k p) f -> p k f", p=P)).then_inc(w_loaded[m], 16)
                    sp.dma_start(w2s[:, m, :, :], w2[j * 2 + m].rearrange("(k p) d -> p k d", p=P)).then_inc(w_loaded[m], 16)

                def pair(j, last):
                    for g in range(NG):
                        if g + 2 < NG:
                            load(j, g + 2)
                        elif not last:
                            load(j + 1, g + 2 - NG)
                        store(j, g)
                        if not last and g % GR == GR - 1:
                            weights(j + 1, g // GR)

                load(0, 0)
                load(0, 1)
                pair(0, False)
                with sp.Fori(1, E // 2 - 1) as j:
                    pair(j, False)
                pair(E // 2 - 1, True)
                for u in range(2):
                    sp.wait_ge(stored[u], 16 * (E // 2) * GR)

            @block.tensor
            def _(pe):
                def turn(j, g):
                    i, u = j * NG + g, g % 2
                    pe.wait_ge(fetched[u], j * (16 * GR) + (g // 2 * 16 + 16))
                    wait_count(pe, x_copied, i)
                    for tt in range(2):
                        for k in range(KC):
                            at = (tt * KC + k) * P
                            ins = pe.transpose(psX[:, at:at + P], xin[:, u, tt, k * P:(k + 1) * P], core.ident[:, :])
                    ins.then_inc(x_turned, 1)

                def up(j, g):
                    i, u, m = j * NG + g, g % 2, g // GR
                    pe.wait_ge(w_loaded[m], j * 32 + 32)
                    pe.wait_ge(x_copied, i + 1)
                    for b in range(FC // 2):
                        wait_count(pe, relued, j * (NG * 4) + ((g - 1) * 4 + b + 1))
                        for f in (2 * b, 2 * b + 1):
                            for k in range(KC):
                                ins = pe.matmul(psH[:, b, (f % 2) * R:(f % 2 + 1) * R], w1s[:, m, k, f * P:(f + 1) * P],
                                                yT[:, u, :, k, :], start=(k == 0), stop=(k == KC - 1))
                        ins.then_inc(up_done, 1)

                def project(j, g):
                    i, u, m = j * NG + g, g % 2, g // GR
                    pe.wait_ge(relued, j * (NG * 4) + (g * 4 + 4))
                    wait_count(pe, out_ready, j * NG + (g - 1))
                    for tt in range(2):
                        for f in range(FC):
                            ins = pe.matmul(psD[:, u, tt * D:(tt + 1) * D], hT[:, u, f, tt * P:(tt + 1) * P],
                                            w2s[:, m, f, :], start=(f == 0), stop=(f == FC - 1))
                    ins.then_inc(down_done, 1)

                def pair(j, last):
                    for g in range(NG):
                        if g + 1 < NG:
                            up(j, g + 1)
                        elif not last:
                            up(j + 1, 0)
                        if g + 2 < NG:
                            turn(j, g + 2)
                        elif not last:
                            turn(j + 1, g + 2 - NG)
                        project(j, g)

                turn(0, 0)
                up(0, 0)
                turn(0, 1)
                pair(0, False)
                with pe.Fori(1, E // 2 - 1) as j:
                    pair(j, False)
                pair(E // 2 - 1, True)

            @block.vector
            def _(dve):
                def step(j, g):
                    i, u = j * NG + g, g % 2
                    dve.wait_ge(down_done, i + 1)
                    wait_count(dve, stored[u], j * (16 * GR) + g // 2 * 16)
                    dve.tensor_copy(out[:, u, :, :], psD[:, u, :].rearrange("p (t d) -> p t d", t=2)).then_inc(out_ready, 1)

                run(dve, step)


def flamingo_decoder(nc, a, out):
    def dram(name, shape, dt=F32):
        return nc.dram_tensor(name, shape, dt, kind="Internal").ap()

    ctx_tiles = a["ctx_2048"].rearrange("b s d -> (b s) d").rearrange("(t p) d -> t p d", p=P)
    ctxT = dram("ctxT", [TILES, P, DIM])
    vt = dram("vt", [TILES, P, KC * 2 * HEADS * (HD + 1)])
    yT = dram("yT", [TILES, P, DIM])
    q_aug = dram("q_aug", [TILES // GROUP, 2, ROWS, PAIRS, GROUP * DIM], BF16)
    k_aug = dram("k_aug", [TILES // GROUP, 2, ROWS, PAIRS, GROUP * DIM], BF16)
    rows_in, rows_out = dram("rows_in", [D0, DIM]), dram("rows_out", [D0, DIM])
    tiles_in, tiles_out = (r.rearrange("(t p) d -> t p d", p=P) for r in (rows_in, rows_out))
    with ExitStack() as ctx:
        core = Core(nc, ctx)

        def x_gate(layer):
            return core.gates[:, layer:layer + 1]

        def f_gate(layer):
            return core.gates[:, 4 + layer:5 + layer]

        phase_setup(core, a["x"], a["g_xattn"], a["g_ffn"], rows_in)
        phase_context(core, ctx_tiles, ctxT, vt)

        phase_norms(core, "n0")
        phase_split(core, "k0", ctx_tiles, k_aug, K_SLOTS, False)
        phase_split(core, "q0", None, q_aug, Q_SLOTS, False)
        phase_attend(core, "a0", q_aug, k_aug, vt, x_gate(0), float(HD) ** -0.5, True)
        core.clear_semaphores()
        phase_norms(core, "n1")
        with ExitStack() as c:
            weight = core.sb(c, "weight0", [P, TILES, 4], F32)
            slot = core.sb(c, "slot0", [P, TILES, 4], U32)
            expert_of = core.sb(c, "expert_of", [P, T0], I32)
            with ExitStack() as c2:
                logits = core.sb(c2, "logits0", [P, TILES, 16], F32)
                phase_logits(core, "l0", 16, yT, logits, router_rows=a["L0_ffn_router_weight"], router_b=a["L0_ffn_router_bias"])
                phase_slots(core, "s0", 16, 4, logits, weight, slot, f_gate(0), expert_of=expert_of)
            phase_scatter(core, "sc0", 4, slot, rows_in, D0)
            phase_experts0(core, tiles_in, tiles_out, expert_of, a["L0_ffn_gate_up_proj"], a["L0_ffn_gate_up_proj_bias"],
                           a["L0_ffn_down_proj"], a["L0_ffn_down_proj_bias"])
            phase_combine(core, "cb0", 4, slot, weight, rows_out, D0)

        core.clear_semaphores()
        phase_norms(core, "n2")
        phase_split(core, "k1", ctx_tiles, k_aug, K_SLOTS, True)
        phase_split(core, "q1", None, q_aug, Q_SLOTS, True)
        phase_attend(core, "a1", q_aug, k_aug, vt, x_gate(1), 5.0, False)
        core.clear_semaphores()
        phase_norms(core, "n3")
        with ExitStack() as c:
            guT = core.sb(c, "guT", [P, KC, 2 * F1], BF16)
            downT = core.sb(c, "downT", [P, F1C, DIM], BF16)
            mu = core.sb(c, "mu", [P, 2], F32)
            qT = core.sb(c, "qT", [P, TILES, KC, P], BF16)
            sg = core.sb(c, "sg", [P, TILES], F32)
            phase_bit_weights(core, a["L1_ffn_w_gate_up"], a["L1_ffn_w_down"], guT, downT, mu)
            phase_bit_inputs(core, a["L1_ffn_norm_weight"], qT, sg, mu)
            phase_bit_ffn(core, qT, sg, guT, downT, mu, f_gate(1))

        def cross(layer, wq, wk, wv, wo, bq, bk, bv, bo, gq, gk):
            n = str(layer)
            with ExitStack() as c:
                q_all = core.sb(c, "q_all" + n, [P, TILES, DIM], F32)
                kv_all = core.sb(c, "kv_all" + n, [P, TILES, 2 * DIM], F32)
                rq = core.sb(c, "rq" + n, [P, TILES], F32)
                rk = core.sb(c, "rk" + n, [P, TILES], F32)
                phase_logits(core, "cq" + n, DIM, yT, q_all, router_cols=wq, router_b=bq)
                phase_keys_values(core, "kv" + n, ctxT, kv_all, wk, wv, bk, bv)
                phase_rms(core, "rm" + n, q_all, kv_all, rq[:, :], rk[:, :], 1e-6)
                phase_cross(core, "cr" + n, q_all, kv_all, rq, rk, gq, gk, wo, bo, x_gate(layer))

        core.clear_semaphores()
        phase_norms(core, "n4")
        cross(2, *(a["L2_xattn_" + k] for k in ("Wq", "Wk_img", "Wv_img", "Wo", "bq", "bk_img", "bv_img", "bo", "gq", "gk_img")))
        core.clear_semaphores()
        phase_norms(core, "n5")
        with ExitStack() as c:
            score = core.sb(c, "score2", [P, TILES, 128], F32)
            mix = core.sb(c, "mix", [P, 8], F32)
            with ExitStack() as c2:
                logits = core.sb(c2, "logits2", [P, TILES, 128], F32)
                phase_logits(core, "l2", 128, yT, logits, router_cols=a["L2_ffn_w_router"])
                phase_topk(core, "t2", 128, 4, logits, score, 1.0, "eps")
            phase_mix(core, "mx", a["L2_ffn_amplitudes"], a["L2_ffn_expert_scale"], mix)
            phase_basis_ffn(core, yT, score, mix, *(a["L2_ffn_" + k] for k in (
                "w_gate", "w_up", "w_down", "shared_w_gate", "shared_w_up", "shared_w_down")), f_gate(2))

        turned = [dram(f"turned{k}", [DIM, DIM]) for k in range(4)]
        core.clear_semaphores()
        phase_norms(core, "n6")
        phase_turn_weights(core, "tw", list(zip((a["L3_xattn_" + k] for k in ("w_q", "w_k_img", "w_v_img", "w_o")), turned)))
        cross(3, *turned, *(a["L3_xattn_" + k] for k in ("b_q", "b_k_img", "b_v_img", "b_o", "g_q", "g_k_img")))
        core.clear_semaphores()
        phase_norms(core, "n7")
        with ExitStack() as c:
            weight = core.sb(c, "weight3", [P, TILES, 2], F32)
            slot = core.sb(c, "slot3", [P, TILES, 2], U32)
            with ExitStack() as c2:
                logits = core.sb(c2, "logits3", [P, TILES, 8], F32)
                phase_logits(core, "l3", 8, yT, logits, router_cols=a["L3_ffn_Wg"])
                phase_slots(core, "s3", 8, 2, logits, weight, slot, f_gate(3), capacity=CAPACITY)
            phase_scatter(core, "sc3", 2, slot, rows_in, 8 * CAPACITY)
            phase_experts3(core, tiles_in, tiles_out, a["L3_ffn_w1"], a["L3_ffn_w2"])
            phase_combine(core, "cb3", 2, slot, weight, rows_out, 8 * CAPACITY)

        core.clear_semaphores()
        phase_store(core, out)


_INS = ['x', 'ctx_2048', 'g_xattn', 'g_ffn', 'L0_ffn_router_weight', 'L0_ffn_router_bias',
        'L0_ffn_gate_up_proj', 'L0_ffn_gate_up_proj_bias', 'L0_ffn_down_proj', 'L0_ffn_down_proj_bias',
        'L1_ffn_w_gate_up', 'L1_ffn_w_down', 'L1_ffn_norm_weight',
        'L2_xattn_Wq', 'L2_xattn_bq', 'L2_xattn_gq', 'L2_xattn_Wk_img', 'L2_xattn_bk_img', 'L2_xattn_gk_img',
        'L2_xattn_Wv_img', 'L2_xattn_bv_img', 'L2_xattn_Wo', 'L2_xattn_bo',
        'L2_ffn_w_router', 'L2_ffn_w_gate', 'L2_ffn_w_up', 'L2_ffn_w_down', 'L2_ffn_amplitudes',
        'L2_ffn_expert_scale', 'L2_ffn_shared_w_gate', 'L2_ffn_shared_w_up', 'L2_ffn_shared_w_down',
        'L3_xattn_w_q', 'L3_xattn_b_q', 'L3_xattn_w_k_img', 'L3_xattn_b_k_img', 'L3_xattn_w_v_img',
        'L3_xattn_b_v_img', 'L3_xattn_w_o', 'L3_xattn_b_o', 'L3_xattn_g_q', 'L3_xattn_g_k_img',
        'L3_ffn_Wg', 'L3_ffn_w1', 'L3_ffn_w2']


def kernel(**inputs):
    import numpy as _np
    import concourse.bacc as _bacc
    from concourse import mybir as _mybir
    from concourse.bass_utils import run_bass_kernel_spmd as _run

    nc = _bacc.Bacc("TRN2", target_bir_lowering=False, num_devices=1)
    arrays, aps = {}, {}
    for name in _INS:
        v = _np.ascontiguousarray(inputs[name])
        arrays[f"in_{name}_dram"] = v
        aps[name] = nc.dram_tensor(f"in_{name}_dram", v.shape, _mybir.dt.from_np(v.dtype), kind="ExternalInput").ap()
    out = nc.dram_tensor("out_0_dram", (BATCH, SEQ, DIM), _mybir.dt.float32, kind="ExternalOutput").ap()
    flamingo_decoder(nc, aps, out)
    r = _run(nc, [arrays], core_ids=[0])
    return r.results[0]["out_0_dram"]
```
